# Optimizing a Trainium2 kernel written in Bass

```python
import numpy as np
import jax
import jax.numpy as jnp

def _softmax(x, axis=-1):
    return jax.nn.softmax(x, axis=axis)

def _gelu(x):
    return jax.nn.gelu(x, approximate=True)

def _silu(x):
    return jax.nn.silu(x)

def _sigmoid(x):
    return jax.nn.sigmoid(x)

def _layernorm(x, axis=-1, eps=1e-05):
    m = jnp.mean(x, axis=axis, keepdims=True)
    v = jnp.var(x, axis=axis, keepdims=True)
    return (x - m) / jnp.sqrt(v + eps)

def _scatter_add(tgt, idx, src, axis=0):
    return tgt.at[idx].add(src)

def _segment_sum(src, seg, n):
    return jax.ops.segment_sum(src, seg, n)
kernel_name = 'mk_xattn_ffn_d2_seqx_r8_28faa9'

def setup_inputs(seed: int=0):
    np.random.seed(seed)
    _w = jnp.asarray

    def _rec_inputs():
        import jax
        import jax.numpy as jnp
        _rk = jax.random.key(seed)
        x = 0.0002417 + 0.9998 * jax.random.normal(jax.random.fold_in(_rk, 1), (4, 512, 128), jnp.float32)
        _lenS = 512 - jax.random.randint(jax.random.fold_in(_rk, 7), (4,), 0, max(1, 512 // 4) + 1, jnp.int32)
        _lenS2 = 77 - jax.random.randint(jax.random.fold_in(_rk, 8), (4,), 0, max(1, 77 // 4) + 1, jnp.int32)
        _ctx_1024P = jax.random.normal(jax.random.fold_in(_rk, 11), (4, 16, 128), jnp.float32)
        _ctx_1024c = jax.random.dirichlet(jax.random.fold_in(_rk, 511), 0.3 * jnp.ones((16,), jnp.float32), (4, 77))
        _ctx_1024t = jnp.einsum('bsk,bkd->bsd', _ctx_1024c, _ctx_1024P)
        _ctx_1024t = _ctx_1024t * jax.lax.rsqrt(jnp.mean(jnp.square(_ctx_1024t)) + 1e-12) * 0.953939
        ctx_1024 = 7.22013e-05 + 1.00017 * (_ctx_1024t + 0.3 * jax.random.normal(jax.random.fold_in(_rk, 611), (4, 77, 128), jnp.float32))
        _validS = jnp.arange(512)[None, :] < _lenS[:, None]
        _validS2 = jnp.arange(77)[None, :] < _lenS2[:, None]
        _causal = jnp.tril(jnp.ones((512, 512), dtype=bool))
        mask_BxSxS2_ik0 = jnp.where(jnp.broadcast_to(_validS2[:, None, :], (4, 512, 77)), 0, 1).astype(jnp.int32)
        return (x, ctx_1024, mask_BxSxS2_ik0)
    x, ctx_1024, mask_BxSxS2_ik0 = _rec_inputs()

    def _L0_xattn_setup():
        import jax, jax.numpy as jnp
        import numpy as np
        EMBED = 128
        HEADS = 16
        HEAD_DIM = EMBED // HEADS
        EXP_DIM = 2 * HEAD_DIM

        def _feature_map(x, fm_w, fm_b):
            z = jnp.einsum('nshd,ed->nshe', x, fm_w) + fm_b
            return jnp.concatenate([jnp.exp(z), jnp.exp(-z)], axis=-1)
        key = jax.random.key(seed)
        ks = jax.random.split(key, 7)
        N, S = (4, 256)
        values = jax.random.normal(ks[0], (N, S, EMBED), dtype=jnp.float32)
        keys_ = jax.random.normal(ks[1], (N, S, EMBED), dtype=jnp.float32)
        query = jax.random.normal(ks[2], (N, S, EMBED), dtype=jnp.float32)
        fm_w = jnp.eye(HEAD_DIM, dtype=jnp.float32) + 0.02 * jax.random.normal(ks[3], (HEAD_DIM, HEAD_DIM), dtype=jnp.float32)
        fm_b = 0.02 * jax.random.normal(ks[4], (HEAD_DIM,), dtype=jnp.float32)
        fc_w = jax.random.normal(ks[5], (EMBED, HEADS * EXP_DIM), dtype=jnp.float32) * (1.0 / np.sqrt(HEADS * EXP_DIM))
        fc_b = jnp.zeros((EMBED,), dtype=jnp.float32)
        return {'values': values, 'keys': keys_, 'query': query, 'fm_w': fm_w, 'fm_b': fm_b, 'fc_w': fc_w, 'fc_b': fc_b}
    _L0_xattn_all = _L0_xattn_setup()
    _L0_xattn_in = {k: v for k, v in _L0_xattn_all.items() if k in ('fm_w', 'fm_b', 'fc_w', 'fc_b')}
    del _L0_xattn_all

    def _L0_ffn_setup():
        import jax, jax.numpy as jnp
        import numpy as np
        B, S, D, E, H, K = (4, 256, 128, 8, 64, 2)
        key = jax.random.key(seed)
        ks = jax.random.split(key, 11)
        sc = 0.02
        return {'x': jax.random.normal(ks[0], (B, S, D), dtype=jnp.float32), 'gate_W': jax.random.normal(ks[1], (D, E), dtype=jnp.float32) * sc, 'W1': jax.random.normal(ks[2], (E, D, H), dtype=jnp.float32) * sc, 'b1': jnp.zeros((E, H), dtype=jnp.float32), 'W2': jax.random.normal(ks[3], (E, H, D), dtype=jnp.float32) * sc, 'b2': jnp.zeros((E, D), dtype=jnp.float32), 'Ws1': jax.random.normal(ks[4], (D, H), dtype=jnp.float32) * sc, 'bs1': jnp.zeros((H,), dtype=jnp.float32), 'Ws2': jax.random.normal(ks[5], (H, D), dtype=jnp.float32) * sc, 'bs2': jnp.zeros((D,), dtype=jnp.float32), 'route_scale': jnp.ones((), dtype=jnp.float32)}
    _L0_ffn_all = _L0_ffn_setup()
    _L0_ffn_in = {k: v for k, v in _L0_ffn_all.items() if k in ('gate_W', 'W1', 'b1', 'W2', 'b2', 'Ws1', 'bs1', 'Ws2', 'bs2', 'route_scale')}
    del _L0_ffn_all

    def _L1_xattn_setup():
        import jax, jax.numpy as jnp
        import numpy as np
        import math
        B, S, E = (4, 256, 128)
        key = jax.random.key(seed)
        ks = jax.random.split(key, 12)
        scale = 1.0 / math.sqrt(E)
        inp = {'query': jax.random.normal(ks[0], (B, S, E), jnp.float32), 'key_': jax.random.normal(ks[1], (B, S, E), jnp.float32), 'value': jax.random.normal(ks[2], (B, S, E), jnp.float32), 'mask': jnp.broadcast_to(jnp.tril(jnp.ones((S, S), jnp.int32)), (B, S, S)), 'Wq': jax.random.uniform(ks[3], (E, E), jnp.float32, -scale, scale), 'bq': jax.random.uniform(ks[4], (E,), jnp.float32, -scale, scale), 'Wk': jax.random.uniform(ks[5], (E, E), jnp.float32, -scale, scale), 'bk': jax.random.uniform(ks[6], (E,), jnp.float32, -scale, scale), 'Wv': jax.random.uniform(ks[7], (E, E), jnp.float32, -scale, scale), 'bv': jax.random.uniform(ks[8], (E,), jnp.float32, -scale, scale), 'Wo': jax.random.uniform(ks[9], (E, E), jnp.float32, -scale, scale), 'bo': jax.random.uniform(ks[10], (E,), jnp.float32, -scale, scale)}
        return inp
    _L1_xattn_all = _L1_xattn_setup()
    _L1_xattn_in = {k: v for k, v in _L1_xattn_all.items() if k in ('Wq', 'bq', 'Wk', 'bk', 'Wv', 'bv', 'Wo', 'bo')}
    del _L1_xattn_all

    def _L1_ffn_setup():
        import jax, jax.numpy as jnp
        import numpy as np
        H = 128
        F = 512
        E = 8
        TOP_K = 2
        B, S = (1, 256)
        key = jax.random.key(seed)
        k0, k1, k2, k3 = jax.random.split(key, 4)
        hidden_states = jax.random.normal(k0, (B, S, H), dtype=jnp.float32)
        gate_w = jax.random.normal(k1, (E, H), dtype=jnp.float32) * 0.02
        gate_up_w = jax.random.normal(k2, (E, 2 * F, H), dtype=jnp.float32) * 0.02
        down_w = jax.random.normal(k3, (E, H, F), dtype=jnp.float32) * 0.02
        return {'hidden_states': hidden_states, 'gate_w': gate_w, 'gate_up_w': gate_up_w, 'down_w': down_w}
    _L1_ffn_all = _L1_ffn_setup()
    _L1_ffn_in = {k: v for k, v in _L1_ffn_all.items() if k in ('gate_w', 'gate_up_w', 'down_w')}
    del _L1_ffn_all
    return {'x': x, 'ctx_1024': ctx_1024, 'mask_BxSxS2_ik0': mask_BxSxS2_ik0, 'L0_xattn_fm_w': _L0_xattn_in['fm_w'], 'L0_xattn_fm_b': _L0_xattn_in['fm_b'], 'L0_xattn_fc_w': _L0_xattn_in['fc_w'], 'L0_xattn_fc_b': _L0_xattn_in['fc_b'], 'L0_ffn_gate_W': _L0_ffn_in['gate_W'], 'L0_ffn_W1': _L0_ffn_in['W1'], 'L0_ffn_b1': _L0_ffn_in['b1'], 'L0_ffn_W2': _L0_ffn_in['W2'], 'L0_ffn_b2': _L0_ffn_in['b2'], 'L0_ffn_Ws1': _L0_ffn_in['Ws1'], 'L0_ffn_bs1': _L0_ffn_in['bs1'], 'L0_ffn_Ws2': _L0_ffn_in['Ws2'], 'L0_ffn_bs2': _L0_ffn_in['bs2'], 'L0_ffn_route_scale': _L0_ffn_in['route_scale'], 'L1_xattn_Wq': _L1_xattn_in['Wq'], 'L1_xattn_bq': _L1_xattn_in['bq'], 'L1_xattn_Wk': _L1_xattn_in['Wk'], 'L1_xattn_bk': _L1_xattn_in['bk'], 'L1_xattn_Wv': _L1_xattn_in['Wv'], 'L1_xattn_bv': _L1_xattn_in['bv'], 'L1_xattn_Wo': _L1_xattn_in['Wo'], 'L1_xattn_bo': _L1_xattn_in['bo'], 'L1_ffn_gate_w': _L1_ffn_in['gate_w'], 'L1_ffn_gate_up_w': _L1_ffn_in['gate_up_w'], 'L1_ffn_down_w': _L1_ffn_in['down_w']}

def reference(x, ctx_1024, mask_BxSxS2_ik0, L0_xattn_fm_w, L0_xattn_fm_b, L0_xattn_fc_w, L0_xattn_fc_b, L0_ffn_gate_W, L0_ffn_W1, L0_ffn_b1, L0_ffn_W2, L0_ffn_b2, L0_ffn_Ws1, L0_ffn_bs1, L0_ffn_Ws2, L0_ffn_bs2, L0_ffn_route_scale, L1_xattn_Wq, L1_xattn_bq, L1_xattn_Wk, L1_xattn_bk, L1_xattn_Wv, L1_xattn_bv, L1_xattn_Wo, L1_xattn_bo, L1_ffn_gate_w, L1_ffn_gate_up_w, L1_ffn_down_w):
    import jax
    import jax.numpy as jnp

    def _L0_xattn_ref(values, keys, query, fm_w, fm_b, fc_w, fc_b):
        import jax, jax.numpy as jnp
        import numpy as np
        EMBED = 128
        HEADS = 16
        HEAD_DIM = EMBED // HEADS
        EXP_DIM = 2 * HEAD_DIM

        def _feature_map(x, fm_w, fm_b):
            z = jnp.einsum('nshd,ed->nshe', x, fm_w) + fm_b
            return jnp.concatenate([jnp.exp(z), jnp.exp(-z)], axis=-1)
        N, S, _ = query.shape
        v = values.reshape(N, -1, HEADS, HEAD_DIM)
        k = keys.reshape(N, -1, HEADS, HEAD_DIM)
        q = query.reshape(N, -1, HEADS, HEAD_DIM)
        v, k, q = (_feature_map(x, fm_w, fm_b) for x in (v, k, q))
        scores = jnp.einsum('nqhd,nkhd->nhqk', q, k) / jnp.sqrt(jnp.float32(EMBED))
        attn = jax.nn.softmax(scores, axis=-1)
        out = jnp.einsum('nhql,nlhd->nqhd', attn, v)
        out = out.reshape(N, S, HEADS * EXP_DIM)
        return out @ fc_w.T + fc_b

    def _L0_ffn_ref(x, gate_W, W1, b1, W2, b2, Ws1, bs1, Ws2, bs2, route_scale):
        import jax, jax.numpy as jnp
        import numpy as np
        B, S, D, E, H, K = (4, 256, 128, 8, 64, 2)
        scores = jax.nn.sigmoid(x @ gate_W) * route_scale
        topk_scores, topk_idx = jax.lax.top_k(scores, K)
        topk_w = topk_scores / topk_scores.sum(-1, keepdims=True)
        onehot = jax.nn.one_hot(topk_idx, E, dtype=x.dtype)
        gate_full = jnp.einsum('bsk,bske->bse', topk_w, onehot)
        h = jax.nn.gelu(jnp.einsum('bsd,edh->bseh', x, W1) + b1, approximate=False)
        y = jnp.einsum('bseh,ehd->bsed', h, W2) + b2
        expert_out = jnp.einsum('bse,bsed->bsd', gate_full, y)
        shared = jax.nn.gelu(x @ Ws1 + bs1, approximate=False) @ Ws2 + bs2
        return expert_out + shared

    def _L1_xattn_ref(query, key_, value, mask, Wq, bq, Wk, bk, Wv, bv, Wo, bo):
        import jax, jax.numpy as jnp
        import numpy as np
        import math
        B, S, E = (4, 256, 128)
        Q = jnp.einsum('bse,fe->bsf', query, Wq) + bq
        K = jnp.einsum('bse,fe->bsf', key_, Wk) + bk
        V = jnp.einsum('bse,fe->bsf', value, Wv) + bv
        scores = jnp.einsum('bqe,bke->bqk', Q, K) / jnp.sqrt(jnp.asarray(E, Q.dtype))
        scores = jnp.where(mask == 0, -jnp.inf, scores)
        attn = jax.nn.softmax(scores, axis=-1)
        attn_out = jnp.einsum('bqk,bke->bqe', attn, V)
        return jnp.einsum('bse,fe->bsf', attn_out, Wo) + bo

    def _L1_ffn_ref(hidden_states, gate_w, gate_up_w, down_w):
        import jax, jax.numpy as jnp
        import numpy as np
        H = 128
        F = 512
        E = 8
        TOP_K = 2
        B, S = (1, 256)
        b, s, h = hidden_states.shape
        x = hidden_states.reshape(-1, h)
        router_logits = x @ gate_w.T
        probs = jax.nn.softmax(router_logits.astype(jnp.float32), axis=-1)
        topw, sel = jax.lax.top_k(probs, TOP_K)
        topw = topw / jnp.sum(topw, axis=-1, keepdims=True)
        topw = topw.astype(x.dtype)
        combine = jnp.sum(jax.nn.one_hot(sel, E, dtype=x.dtype) * topw[..., None], axis=1)
        gu = jnp.einsum('th,efh->etf', x, gate_up_w)
        gate, up = (gu[..., :F], gu[..., F:])
        hact = up * jax.nn.gelu(gate, approximate=False)
        expert_out = jnp.einsum('etf,ehf->eth', hact, down_w)
        out = jnp.einsum('eth,te->th', expert_out, combine)
        return out.reshape(b, s, h)
    x = x + _L0_xattn_ref(ctx_1024, ctx_1024, _layernorm(x, axis=-1), L0_xattn_fm_w, L0_xattn_fm_b, L0_xattn_fc_w, L0_xattn_fc_b)
    x = x + _L0_ffn_ref(_layernorm(x, axis=-1), L0_ffn_gate_W, L0_ffn_W1, L0_ffn_b1, L0_ffn_W2, L0_ffn_b2, L0_ffn_Ws1, L0_ffn_bs1, L0_ffn_Ws2, L0_ffn_bs2, L0_ffn_route_scale)
    x = x + _L1_xattn_ref(_layernorm(x, axis=-1), ctx_1024, ctx_1024, mask_BxSxS2_ik0, L1_xattn_Wq, L1_xattn_bq, L1_xattn_Wk, L1_xattn_bk, L1_xattn_Wv, L1_xattn_bv, L1_xattn_Wo, L1_xattn_bo)
    x = x + _L1_ffn_ref(_layernorm(x, axis=-1), L1_ffn_gate_w, L1_ffn_gate_up_w, L1_ffn_down_w)
    return x

_drawn_inputs = setup_inputs


def setup_inputs(seed=0):
    import zlib

    import numpy as np

    out = dict(_drawn_inputs(seed))
    spreads = {'L0_xattn_fc_b': (0.0, 0.8),
     'L0_ffn_b1': (0.0, 0.8),
     'L0_ffn_b2': (0.0, 0.8),
     'L0_ffn_bs1': (0.0, 0.8),
     'L0_ffn_bs2': (0.0, 0.8)}
    factors = {'L0_ffn_gate_W': 8.0,
     'L0_ffn_W1': 8.0,
     'L0_ffn_W2': 8.0,
     'L0_ffn_Ws1': 8.0,
     'L0_ffn_Ws2': 8.0,
     'L1_xattn_Wq': 8.0,
     'L1_xattn_bq': 8.0,
     'L1_xattn_Wk': 8.0,
     'L1_xattn_bk': 8.0,
     'L1_xattn_Wv': 3.614,
     'L1_xattn_bv': 8.0,
     'L1_xattn_Wo': 3.783,
     'L1_xattn_bo': 8.0,
     'L1_ffn_gate_w': 8.0,
     'L1_ffn_gate_up_w': 8.0,
     'L1_ffn_down_w': 8.0}
    for name, (base, spread) in spreads.items():
        noise = np.random.default_rng([zlib.crc32(name.encode()), seed]).standard_normal(out[name].shape)
        drawn = base * np.exp(spread * noise) if base else spread * noise
        out[name] = jnp.asarray(drawn.astype(out[name].dtype))
    for name, factor in factors.items():
        out[name] = (out[name] * factor).astype(out[name].dtype)
    return out
```

```python
from contextlib import ExitStack

import concourse.bass as bass
from concourse import mybir

F32 = mybir.dt.float32
F32R = mybir.dt.float32r
BF16 = mybir.dt.bfloat16
I32 = mybir.dt.int32
ALU = mybir.AluOpType
ACT = mybir.ActivationFunctionType
AX = mybir.AxisListType

P = 128
NB, SEQ, D = 4, 512, 128
NI = SEQ // P
KEYS = 77
HEADS, HD, FD = 16, 8, 16
HH = HEADS // 2
HK = HH * KEYS
NC = -(-HK // P)
E0, H0 = 8, 64
E1, F1 = 8, 512
EPS = 1e-5
BIG = 3.0e38
SCALE = float(D) ** -0.5


def chunk_rows(c):
    return min(P, HK - c * P)


def chunk_heads(c):
    first = c * P // KEYS
    last = (c * P + chunk_rows(c) - 1) // KEYS
    return first, last + 1


def two_layer_kernel(nc, A, out):
    with ExitStack() as ctx:
        def sem(name):
            return ctx.enter_context(nc.semaphore(name))

        def sb(name, shape, dt=F32, at=ctx):
            return at.enter_context(nc.sbuf_tensor(name, shape, dt))

        ps = ctx.enter_context(nc.psum_tensor("ps", [P, 8, 512], F32))
        bank = [ps[:, i, :] for i in range(8)]

        x = sb("x", [P, NB, NI, D])
        xb = sb("xb", [P, NB, NI, D])
        xn = sb("xn", [P, NB, NI, D])
        xnT = sb("xnT", [P, NB, SEQ])
        stats = sb("stats", [P, NB, NI, 6])
        mv = sb("mv", [P, NB, NI, 2])
        rstd = sb("rstd", [P, NB, NI])
        ident = sb("ident", [P, P])
        identb = sb("identb", [P, P], BF16)
        identr = sb("identr", [P, P], F32R)
        neghalf = sb("neghalf", [P, NI])
        ones_row = sb("ones_row", [1, P])
        biases = sb("biases", [P, 3, D])
        fcT = sb("fcT", [P, 2, D])
        W1 = sb("W1", [P, E0 * H0])
        Ws1 = sb("Ws1", [P, H0])
        gate0 = sb("gate0", [P, E0])
        W2 = sb("W2", [P, 4, D])
        Ws2 = sb("Ws2", [H0, D])
        b1 = sb("b1", [P, 4])
        bs1 = sb("bs1", [H0, 1])
        b2 = sb("b2", [3 * E0, D])
        b2s = sb("b2s", [3 * E0, 3, D], BF16)
        b2r = sb("b2r", [3 * E0, D])
        route_scale = sb("route_scale", [P, 1])
        gate1 = sb("gate1", [P, E1])
        mask_i = sb("mask_i", [P, NB, NI * KEYS], I32)
        maskb = mask_i[:, :, :].bitcast(F32)
        keyA = sb("keyA", [P, NB * KEYS])
        keyc = sb("keyc", [1, NB * KEYS])
        Vo = sb("Vo", [KEYS, NB, D + 1])
        iota8 = sb("iota8", [P, NI, E0])
        sel = sb("sel", [3 * HEADS, 2, NC * P], BF16)
        selG = sb("selG", [3 * E0, 4, P], BF16)
        selGt = sb("selGt", [3 * E0, 3, 4 * P], BF16)
        r_s = sb("r_s", [P, 2, NI, E0])
        r_a = sb("r_a", [P, 2, NI, E0])
        r_b = sb("r_b", [P, 2, NI, E0])
        r_o1 = sb("r_o1", [P, 2, NI, E0])
        r_o2 = sb("r_o2", [P, 2, NI, E0])
        r_m = sb("r_m", [P, 2, 6, NI])
        gate = sb("gate", [P, NB, NI, E0])

        l0 = ExitStack()
        ctx_tok = sb("ctx_tok", [KEYS, NB, D], at=l0)
        ctxT = sb("ctxT", [P, NB * KEYS], at=l0)
        wnat = sb("wnat", [P, 4, D], at=l0)
        wT = sb("wT", [P, 3, D], at=l0)
        bqkv = sb("bqkv", [P, 3], at=l0)
        KT = sb("KT", [P, NB * KEYS], at=l0)
        VT = sb("VT", [P, NB * KEYS], at=l0)
        fcn = sb("fcn", [P, 2, D], at=l0)
        gate1n = sb("gate1n", [E1, D], at=l0)
        fm = sb("fm", [HD, HD + 1], at=l0)
        fmT = sb("fmT", [P, HD + 1], at=l0)
        mask16 = sb("mask16", [P, 2, HEADS], at=l0)
        maskK = sb("maskK", [P, HH], at=l0)
        ind = sb("ind", [P, NC, HH], at=l0)
        indw = sb("indw", [P, 2, NC, 3, HEADS], BF16, at=l0)
        Wz = sb("Wz", [P, 2, HH, 2, HD], at=l0)
        kbhi = sb("kbhi", [P, NB, 2, HK], F32R, at=l0)
        kblo = sb("kblo", [P, NB, 2, HK], F32R, at=l0)
        Vx = sb("Vx", [P, NB * 2, NC, HH, FD + 1], at=l0)
        qf = sb("qf", [P, 2, SEQ], at=l0)
        qhi = sb("qhi", [P, NB, 2, SEQ], F32R, at=l0)
        qlo = sb("qlo", [P, NB, 2, SEQ], F32R, at=l0)
        mx = sb("mx", [P, 2, NI, HEADS], at=l0)
        nm = sb("nm", [P, 2, NI, 3, HEADS], BF16, at=l0)
        nmr = sb("nmr", [P, 2, NI, HEADS], at=l0)
        nmT = sb("nmT", [3 * HEADS, 2, SEQ], BF16, at=l0)
        early = ExitStack()
        kf = sb("kf", [P, 2, NB * KEYS], at=early)
        kfhi = sb("kfhi", [P, 2, NB * KEYS], F32R, at=early)
        kflo = sb("kflo", [P, 2, NB * KEYS], F32R, at=early)
        isgn = sb("isgn", [HD, HH, 2, HD], at=early)
        fmrep = sb("fmrep", [HD, HEADS, HD], at=early)
        early.close()
        ex = sb("ex", [P, 2 * NC, SEQ], at=l0)
        rec = sb("rec", [P, 2, HEADS], at=l0)
        on = sb("on", [P, NI, HEADS * FD], at=l0)
        onT = sb("onT", [P, NI, 2, P], at=l0)
        l0.close()

        hraw = sb("hraw", [P, 2, SEQ])
        hg = sb("hg", [P, 2, 4, SEQ])
        hs = sb("hs", [H0, 2, SEQ])
        g3 = sb("g3", [P, NB, NI, 3, E0], BF16)
        g3r = sb("g3r", [P, NB, NI, E0])
        gT3 = sb("gT3", [3 * E0, NB, SEQ], BF16)
        sc = sb("sc", [P, 2, NI, KEYS])
        scm = sb("scm", [P, 2, NI])
        pr = sb("pr", [P, 2, NI, KEYS])
        prT = sb("prT", [KEYS, 2, SEQ])
        srec = sb("srec", [P, 2, NI])
        upn = sb("upn", [P, E1, 8, D])
        dnn = sb("dnn", [P, E1, F1])
        upT = sb("upT", [P, E1, 2 * F1])
        dnT = sb("dnT", [P, E1, 4, D])
        gl = hraw
        hT = hg

        n_ld = [0]

        def load_sem(name):
            return sem("ld_" + name)

        ld_x = [load_sem(f"x{b}") for b in range(NB)]
        ld_ctx, ld_fm, ld_w, ld_small, ld_mask = (load_sem(n) for n in ("ctx", "fm", "w", "small", "mask"))
        ld_up = [load_sem(f"up{e}") for e in range(E1)]
        ld_dn = [load_sem(f"dn{e}") for e in range(E1)]
        stored = sem("stored")
        pool_ident, pool_const, pool_mask, pool_ind, pool_kb = (sem("pool_" + n) for n in ("ident", "const", "mask", "ind", "kb"))
        pool_xb, pool_var, pool_rstd, pool_q = (sem("pool_" + n) for n in ("xb", "var", "rstd", "q"))
        dve_c, dve_link = sem("dve_c"), sem("dve_link")
        pe_ctxT, pe_fm, pe_kz, pe_wT, pe_kv, pe_ak, pe_vt = (sem("pe_" + n) for n in ("ctxT", "fm", "kz", "wT", "kv", "ak", "vt"))
        dve_ctxT, dve_fmT, dve_Wz, dve_kf, dve_kb, dve_wT, dve_kv, dve_ak = (
            sem("dve_" + n) for n in ("ctxT", "fmT", "Wz", "kf", "kb", "wT", "kv", "ak"))
        act_kf, act_vx = sem("act_kf"), sem("act_vx")
        dve_mv, dve_xn, pe_xT, xT_ready = sem("dve_mv"), sem("dve_xn"), sem("pe_xT"), sem("act_xT")
        pe_z, act_q, dve_q = sem("pe_z"), sem("act_q"), sem("dve_q")
        pe_max, dve_max, dve_nm, pe_nmT, act_nmT = (sem(n) for n in ("pe_max", "dve_max", "dve_nm", "pe_nmT", "act_nmT"))
        pe_sc, act_ex, pe_av, dve_on, pe_onT, act_onT, pe_fc = (
            sem(n) for n in ("pe_sc", "act_ex", "pe_av", "dve_on", "pe_onT", "act_onT", "pe_fc"))
        dve_x = sem("dve_x")
        pe_lg, act_lg, dve_g, pe_gT, dve_gT, pe_G, pe_h, act_h, dve_hg, pe_y = (
            sem(n) for n in ("pe_lg", "act_lg", "dve_g", "pe_gT", "dve_gT", "pe_G", "pe_h", "act_h", "dve_hg", "pe_y"))
        pe_s1, dve_s1, act_s1, pe_pT, act_pT, pe_o1 = (sem(n) for n in ("pe_s1", "dve_s1", "act_s1", "pe_pT", "act_pT", "pe_o1"))
        pe_upT, act_upT, dve_upT = sem("pe_upT"), sem("act_upT"), sem("dve_upT")
        pe_gu, act_gl, dve_hT, pe_dn, dve_acc = (sem(n) for n in ("pe_gu", "act_gl", "dve_hT", "pe_dn", "dve_acc"))

        x_dram = A["x"].rearrange("b (p i) d -> b p (i d)", i=NI)
        out_dram = out.rearrange("b (p i) d -> b p (i d)", i=NI)
        mask_dram = A["mask_BxSxS2_ik0"].rearrange("b (p i) k -> b p (i k)", i=NI)

        def row(name):
            return A[name].rearrange("(a n) -> a n", a=1)

        def col(name):
            return A[name].rearrange("(n a) -> n a", a=1)

        def everywhere(name, n=P):
            return A[name].partition_broadcast(n)

        block = ctx.enter_context(nc.Block())

        N_SMALL = 14
        N_FM = 2
        N_W = 9

        @block.sync
        def _(sp):
            sp.dma_start(ctx_tok[:, :, :], A["ctx_1024"].rearrange("b k d -> k b d")).then_inc(ld_ctx, 16)
            sp.dma_start(fm[:, 0:HD], A["L0_xattn_fm_w"]).then_inc(ld_fm, 16)
            sp.dma_start(fm[:, HD:HD + 1], col("L0_xattn_fm_b")).then_inc(ld_fm, 16)
            for b in range(NB):
                sp.dma_start(x[:, b, :, :].rearrange("p i d -> p (i d)"), x_dram[b]).then_inc(ld_x[b], 16)
            for n, name in enumerate(("Wq", "Wk", "Wv", "Wo")):
                sp.dma_start(wnat[:, n, :], A["L1_xattn_" + name]).then_inc(ld_w, 16)
            for n, name in enumerate(("bq", "bk", "bv")):
                sp.dma_start(bqkv[:, n:n + 1], col("L1_xattn_" + name)).then_inc(ld_w, 16)
            sp.dma_start(fcn[:, :, :], A["L0_xattn_fc_w"].rearrange("n (a f) -> n a f", a=2)).then_inc(ld_w, 16)
            sp.dma_start(gate1n[:, :], A["L1_ffn_gate_w"]).then_inc(ld_w, 16)
            for n, name in enumerate(("L0_xattn_fc_b", "L0_ffn_bs2", "L1_xattn_bo")):
                sp.dma_start(biases[:, n, :], everywhere(name)).then_inc(ld_small, 16)
            sp.dma_start(W1[:, :].rearrange("d (e h) -> d e h", e=E0), A["L0_ffn_W1"].rearrange("e d h -> d e h")).then_inc(ld_small, 16)
            sp.dma_start(Ws1[:, :], A["L0_ffn_Ws1"]).then_inc(ld_small, 16)
            sp.dma_start(gate0[:, :], A["L0_ffn_gate_W"]).then_inc(ld_small, 16)
            sp.dma_start(W2[:, :, :], A["L0_ffn_W2"].rearrange("(c a) h d -> (a h) c d", a=2)).then_inc(ld_small, 16)
            sp.dma_start(Ws2[:, :], A["L0_ffn_Ws2"]).then_inc(ld_small, 16)
            sp.dma_start(b1[:, :], A["L0_ffn_b1"].rearrange("(c a) h -> (a h) c", a=2),
                         allow_slow_non_contiguous=True).then_inc(ld_small, 16)
            sp.dma_start(bs1[:, :], col("L0_ffn_bs1")).then_inc(ld_small, 16)
            for t in range(3):
                sp.dma_start(b2[E0 * t:E0 * t + E0, :], A["L0_ffn_b2"]).then_inc(ld_small, 16)
            sp.dma_start(route_scale[:, :], A["L0_ffn_route_scale"].partition_broadcast(P)).then_inc(ld_small, 16)
            for b in range(NB):
                sp.dma_start(mask_i[:, b, :], mask_dram[b]).then_inc(ld_mask, 16)
            sp.wait_ge(pe_fc, NB)
            sp.wait_ge(dve_on, NB * NI)
            sp.wait_ge(act_onT, NB * NI)
            for e in range(E1):
                sp.dma_start(upn[:, e, :, :], A["L1_ffn_gate_up_w"][e].rearrange("(c f) h -> f c h", f=P)).then_inc(ld_up[e], 16)
                sp.dma_start(dnn[:, e, :], A["L1_ffn_down_w"][e]).then_inc(ld_dn[e], 16)
            for b in range(NB):
                sp.wait_ge(dve_acc, NI * ((E1 - 1) * NB + b + 1))
                sp.dma_start(out_dram[b], x[:, b, :, :].rearrange("p i d -> p (i d)")).then_inc(stored, 16)
            sp.wait_ge(stored, 16 * NB)


        def wide(ap, *shape):
            return ap.to_broadcast(list(shape))

        @block.gpsimd
        def _(g):
            link = [0]

            def ordered(ins):
                link[0] += 1
                ins.then_inc(pool_const, 1)
                g.wait_ge(pool_const, link[0])

            def band(t, pattern, mult, width, base=0):
                ordered(g.affine_select(out=t, in_=t, compare_op=ALU.is_ge, fill=0.0, base=base,
                                        pattern=pattern, channel_multiplier=mult))
                ordered(g.affine_select(out=t, in_=t, compare_op=ALU.is_ge, fill=0.0, base=width - 1 - base,
                                        pattern=[[-s, n] for s, n in pattern], channel_multiplier=-mult))

            def layernorm_rstd(k):
                for b in range(NB):
                    g.wait_ge(dve_mv, k * NB + b + 1)
                    ordered(g.tensor_scalar(rstd[:, b, :], mv[:, b, :, 1], EPS, None, ALU.add))
                    g.tensor_tensor(rstd[:, b, :], rstd[:, b, :], neghalf[:, :], ALU.pow).then_inc(pool_rstd, 1)

            def add_bias(k):
                for b in range(NB):
                    if k == 0:
                        g.wait_ge(ld_x[b], 16)
                        g.wait_ge(ld_small, 16 * N_SMALL)
                    else:
                        g.wait_ge(dve_x, (k - 1) * NB + b + 1)
                    g.tensor_tensor(xb[:, b, :, :], x[:, b, :, :], wide(biases[:, k:k + 1, :], P, NI, D), ALU.add)\
                        .then_inc(pool_xb, 1)

            ordered(g.memset(ident[:, :], 1.0))
            band(ident[:, :], [[-1, P]], 1, 1)
            g.tensor_copy(identb[:, :], ident[:, :]).then_inc(pool_ident, 1)
            g.tensor_copy(identr[:, :], ident[:, :]).then_inc(pool_ident, 1)
            ordered(g.memset(mask16[:, 0, :], 1.0))
            band(mask16[:, 0, :], [[-HD, HEADS]], 1, HD)
            ordered(g.memset(maskK[:, :], 1.0))
            band(maskK[:, :], [[-FD, HH]], 1, FD)
            ordered(g.memset(isgn[:, :, 0, :], 1.0))
            band(isgn[:, :, 0, :], [[0, HH], [-1, HD]], 1, 1)
            g.tensor_scalar(isgn[:, :, 1, :], isgn[:, :, 0, :], -1.0, None, ALU.mult).then_inc(pool_mask, 1)
            g.tensor_scalar(mask16[:, 1, :], mask16[:, 0, :], -1.0, None, ALU.mult).then_inc(pool_mask, 1)
            ordered(g.memset(neghalf[:, :], -0.5))
            layernorm_rstd(0)
            ordered(g.memset(ind[:, :, :], 1.0))
            band(ind[:, :, :], [[P, NC], [-KEYS, HH]], 1, KEYS)
            ordered(g.memset(indw[:, :, :, :, :], 0.0))
            for half in range(2):
                for part in range(3):
                    g.tensor_copy(indw[:, half, :, part, half * HH:half * HH + HH], ind[:, :, :]).then_inc(pool_ind, 1)
            g.tensor_copy(Vx[:, :, :, :, FD],
                          wide(ind[:, :, :].unsqueeze(1), P, NB * 2, NC, HH)).then_inc(pool_ind, 1)
            for b in range(NB):
                for half in range(2):
                    if b == half == 0:
                        g.wait_ge(dve_kf, 4)
                    g.tensor_tensor(kblo[:, b, half, :].bitcast(F32R).rearrange("p (h k) -> p h k", h=HH),
                                    wide(kflo[:, half, b * KEYS:(b + 1) * KEYS].bitcast(F32).unsqueeze(1), P, HH, KEYS),
                                    wide(maskK[:, :].unsqueeze(2), P, HH, KEYS), ALU.mult).then_inc(pool_kb, 1)
            add_bias(0)
            ordered(g.memset(ones_row[:, :], 1.0))
            ordered(g.iota(iota8[:, :, :], pattern=[[0, NI], [-1, E0]], base=E0, channel_multiplier=0,
                           allow_small_or_imprecise_dtypes=True))
            for part in range(3):
                ordered(g.memset(selGt[:, part, :], 1.0))
                band(selGt[:, part, :], [[1, 4 * P]], -H0, H0, base=H0 * E0 * part)
            ordered(g.tensor_tensor(selGt[:, 0, :], selGt[:, 0, :], selGt[:, 1, :], ALU.add))
            ordered(g.tensor_tensor(selGt[:, 0, :], selGt[:, 0, :], selGt[:, 2, :], ALU.add))
            ordered(g.tensor_copy(selG[:, :, :].rearrange("q c r -> q (c r)"), selGt[:, 0, :]))
            g.wait_ge(ld_small, 16 * N_SMALL)
            ordered(g.tensor_copy(b2s[:, 0, :], b2[:, :]))
            ordered(g.tensor_tensor(b2r[:, :], b2[:, :], b2s[:, 0, :], ALU.subtract))
            ordered(g.tensor_copy(b2s[:, 1, :], b2r[:, :]))
            ordered(g.tensor_tensor(b2r[:, :], b2r[:, :], b2s[:, 1, :], ALU.subtract))
            ordered(g.tensor_copy(b2s[:, 2, :], b2r[:, :]))
            g.wait_ge(ld_mask, 16 * NB)
            ordered(g.tensor_scalar(maskb[:, :, :], mask_i[:, :, :], 0.0, -BIG, ALU.is_equal, ALU.mult))
            g.memset(Vo[:, :, D:D + 1], 1.0).then_inc(pool_mask, 1)
            layernorm_rstd(1)
            add_bias(1)
            layernorm_rstd(2)
            add_bias(2)
            layernorm_rstd(3)

        @block.vector
        def _(v):
            link = [0]

            def step(ins):
                link[0] += 1
                ins.then_inc(dve_link, 1)

            def settle():
                v.wait_ge(dve_link, link[0])

            def layernorm_stats(b):
                for i in range(NI):
                    step(v.bn_stats(stats[:, b, i, :], x[:, b, i, :]))
                settle()
                for i in range(NI):
                    ins = v.bn_aggr(mv[:, b, i, :], stats[:, b, i, :])
                    if i < NI - 1:
                        step(ins)
                settle()
                ins.then_inc(dve_mv, 1)

            def layernorm_apply(k, b):
                v.wait_ge(pool_rstd, k * NB + b + 1)
                for i in range(NI):
                    v.tensor_scalar(xn[:, b, i, :], x[:, b, i, :], mv[:, b, i, 0:1], rstd[:, b, i:i + 1],
                                    ALU.subtract, ALU.mult).then_inc(dve_xn, 1)

            def route(b, scores, sem_done):
                s, a, t = r_s[:, b % 2], r_a[:, b % 2], r_b[:, b % 2]
                o1, o2, m = r_o1[:, b % 2], r_o2[:, b % 2], r_m[:, b % 2]

                def w(i):
                    return wide(m[:, i, :].unsqueeze(2), P, NI, E0)

                def first_best(src, best, onehot, i):
                    step(v.tensor_reduce(m[:, i, :], src, AX.X, ALU.max))
                    settle()
                    step(v.tensor_tensor(t, src, w(i), ALU.is_equal))
                    settle()
                    step(v.tensor_tensor(t, t, iota8[:, :, :], ALU.mult))
                    settle()
                    step(v.tensor_reduce(m[:, i + 1, :], t, AX.X, ALU.max))
                    settle()
                    step(v.tensor_tensor(onehot, t, w(i + 1), ALU.is_equal))
                    settle()

                first_best(s, None, o1, 0)
                step(v.scalar_tensor_tensor(out=a, in0=o1, scalar=-BIG, in1=s, op0=ALU.mult, op1=ALU.add))
                settle()
                first_best(a, None, o2, 2)
                step(v.tensor_tensor(m[:, 4, :], m[:, 0, :], m[:, 2, :], ALU.add))
                settle()
                step(v.reciprocal(m[:, 5, :], m[:, 4, :]))
                settle()
                step(v.tensor_tensor(m[:, 0, :], m[:, 0, :], m[:, 5, :], ALU.mult))
                step(v.tensor_tensor(m[:, 2, :], m[:, 2, :], m[:, 5, :], ALU.mult))
                settle()
                step(v.tensor_tensor(o1, o1, w(0), ALU.mult))
                step(v.tensor_tensor(o2, o2, w(2), ALU.mult))
                settle()

            v.wait_ge(ld_fm, 16 * N_FM)
            v.tensor_copy(fmrep[:, :, :], wide(fm[:, 0:HD].unsqueeze(1), HD, HEADS, HD)).then_inc(dve_c, 1)
            v.wait_ge(pe_ctxT, 1)
            v.tensor_copy(ctxT[:, :], bank[0][:, 0:NB * KEYS]).then_inc(dve_ctxT, 1)
            v.wait_ge(pe_fm, 1)
            v.tensor_copy(fmT[:, :], bank[1][:, 0:HD + 1]).then_inc(dve_fmT, 1)
            v.wait_ge(dve_fmT, 1)
            v.wait_ge(pool_mask, 2)
            for half in range(2):
                for s in range(2):
                    v.tensor_tensor(Wz[:, half, :, s, :], wide(fmT[:, 0:HD].unsqueeze(1), P, HH, HD),
                                    wide(mask16[:, s, half * HH:half * HH + HH].unsqueeze(2), P, HH, HD),
                                    ALU.mult).then_inc(dve_Wz, 1)
            for b in range(NB):
                v.wait_ge(ld_x[b], 16)
                layernorm_stats(b)
            for b in range(NB):
                layernorm_apply(0, b)
            v.wait_ge(act_kf, 2)
            for half in range(2):
                v.tensor_copy(kfhi[:, half, :], kf[:, half, :]).then_inc(dve_kf, 1)
            v.wait_ge(dve_kf, 2)
            for half in range(2):
                v.tensor_tensor(kflo[:, half, :], kf[:, half, :], kfhi[:, half, :].bitcast(F32), ALU.subtract)\
                    .then_inc(dve_kf, 1)
            for b in range(NB):
                for half in range(2):
                    v.tensor_tensor(kbhi[:, b, half, :].rearrange("p (h k) -> p h k", h=HH),
                                    wide(kfhi[:, half, b * KEYS:(b + 1) * KEYS].bitcast(F32).unsqueeze(1), P, HH, KEYS),
                                    wide(maskK[:, :].unsqueeze(2), P, HH, KEYS), ALU.mult).then_inc(dve_kb, 1)
                for half in range(2):
                    n = 2 * b + half
                    v.wait_ge(act_q, n + 1)
                    v.tensor_copy(qhi[:, b, half, :], qf[:, half, :]).then_inc(dve_q, 1)
                    v.wait_ge(dve_q, 2 * n + 1)
                    v.tensor_tensor(qlo[:, b, half, :], qf[:, half, :], qhi[:, b, half, :].bitcast(F32), ALU.subtract)\
                        .then_inc(dve_q, 1)
            for half in range(2):
                v.wait_ge(pe_kz, 3 + half)
                v.tensor_copy(sel[:, half, :], bank[6 + half].bitcast(BF16)[0:3 * HEADS, 0:NC * P]).then_inc(dve_Wz, 1)
            v.wait_ge(pe_wT, 2)
            v.tensor_copy(wT[:, :, :], bank[0][:, 0:3 * D].rearrange("p (n d) -> p n d", n=3)).then_inc(dve_wT, 1)
            v.tensor_copy(fcT[:, :, :], bank[1][:, 0:2 * D].rearrange("p (n d) -> p n d", n=2)).then_inc(dve_wT, 1)
            v.tensor_copy(gate1[:, :], bank[1][:, 2 * D:2 * D + E1]).then_inc(dve_wT, 1)
            v.wait_ge(pe_kv, 2)
            v.wait_ge(ld_w, 16 * N_W)
            v.tensor_scalar(KT[:, :], bank[2][:, 0:NB * KEYS], bqkv[:, 1:2], None, ALU.add).then_inc(dve_kv, 1)
            v.tensor_scalar(VT[:, :], bank[3][:, 0:NB * KEYS], bqkv[:, 2:3], None, ALU.add).then_inc(dve_kv, 1)
            v.wait_ge(pe_ak, 3)
            v.tensor_copy(keyA[:, :], bank[0][:, 0:NB * KEYS]).then_inc(dve_ak, 1)
            v.tensor_copy(keyc[:, :], bank[1][0:1, 0:NB * KEYS]).then_inc(dve_ak, 1)
            v.tensor_copy(Vo[:, :, 0:D], bank[2][0:KEYS, :].rearrange("k (b d) -> k b d", b=NB)).then_inc(dve_ak, 1)

            def maxima(b):
                for j in range(2 * NI):
                    i, half = divmod(j, 2)
                    n = b * 2 * NI + j
                    v.wait_ge(pe_max, n + 1)
                    pair = 4 + 2 * (n % 2)
                    v.tensor_reduce(mx[:, b % 2, i, half * HH:half * HH + HH].rearrange("p (a h) -> p a h", a=2),
                                    ps[:, pair:pair + 2, 0:HK // 2].rearrange("p a (h k) -> p a h k", h=HH // 2),
                                    AX.X, ALU.max).then_inc(dve_max, 1)
                v.wait_ge(dve_max, (b + 1) * 2 * NI)
                if b >= 2:
                    v.wait_ge(pe_nmT, b - 1)
                m, r = mx[:, b % 2], nmr[:, b % 2]
                step(v.tensor_scalar(nm[:, b % 2, :, 0, :], m, -1.0, None, ALU.mult))
                settle()
                step(v.scalar_tensor_tensor(out=r, in0=m, scalar=-1.0, in1=nm[:, b % 2, :, 0, :], op0=ALU.mult, op1=ALU.subtract))
                settle()
                step(v.tensor_copy(nm[:, b % 2, :, 1, :], r))
                settle()
                v.tensor_tensor(nm[:, b % 2, :, 2, :], r, nm[:, b % 2, :, 1, :], ALU.subtract).then_inc(dve_nm, 1)

            maxima(0)
            for b in range(NB + 1):
                if b >= 1:
                    for i in range(NI):
                        n = (b - 1) * NI + i
                        v.wait_ge(pe_av, n + 1)
                        if n >= NI:
                            v.wait_ge(pe_onT, n - NI + 1)
                        av = bank[4 + i][:, 0:HEADS * (FD + 1)].rearrange("p (h f) -> p h f", h=HEADS)
                        step(v.reciprocal(rec[:, n % 2, :], av[:, :, FD]))
                        settle()
                        v.tensor_tensor(on[:, i, :].rearrange("p (h f) -> p h f", h=HEADS), av[:, :, 0:FD],
                                        wide(rec[:, n % 2, :].unsqueeze(2), P, HEADS, FD), ALU.mult).then_inc(dve_on, 1)
                if b + 1 < NB:
                    maxima(b + 1)
                if b >= 1:
                    v.wait_ge(pe_fc, b)
                    v.wait_ge(pool_xb, b)
                    v.tensor_tensor(x[:, b - 1, :, :].rearrange("p i d -> p (i d)"), bank[3],
                                    xb[:, b - 1, :, :].rearrange("p i d -> p (i d)"), ALU.add).then_inc(dve_x, 1)
                    v.wait_ge(dve_x, b)
                    layernorm_stats(b - 1)
                if b >= 2:
                    layernorm_apply(1, b - 2)
            layernorm_apply(1, NB - 1)

            for b in range(NB):
                v.wait_ge(act_lg, b + 1)
                s = r_s[:, b % 2]
                step(v.tensor_scalar(s, s, 1.0, None, ALU.add))
                settle()
                step(v.reciprocal(s, s))
                settle()
                step(v.tensor_scalar(s, s, route_scale[:, 0:1], None, ALU.mult))
                settle()
                route(b, s, None)
                o1, o2, r = r_o1[:, b % 2], r_o2[:, b % 2], g3r[:, b]
                step(v.tensor_tensor(r, o1, o2, ALU.add))
                settle()
                step(v.tensor_copy(g3[:, b, :, 0, :], r))
                settle()
                step(v.tensor_tensor(r, r, g3[:, b, :, 0, :], ALU.subtract))
                settle()
                step(v.tensor_copy(g3[:, b, :, 1, :], r))
                settle()
                v.tensor_tensor(g3[:, b, :, 2, :], r, g3[:, b, :, 1, :], ALU.subtract).then_inc(dve_g, 1)
            for b in range(NB + 1):
                if b < NB:
                    v.wait_ge(pe_gT, b + 1)
                    v.tensor_copy(gT3[:, b, :], bank[0].bitcast(BF16)[0:3 * E0, 0:SEQ]).then_inc(dve_gT, 1)
                    if b >= 2:
                        v.wait_ge(pe_y, b - 1)
                    for c in range(4):
                        n = 4 * b + c
                        v.wait_ge(act_h, 5 * b + c + 1)
                        v.wait_ge(pe_G, n + 1)
                        v.tensor_tensor(hg[:, b % 2, c, :], hraw[:, n % 2, :], bank[3 + n % 2], ALU.mult).then_inc(dve_hg, 1)
                if b >= 1:
                    v.wait_ge(pe_y, b)
                    v.wait_ge(pool_xb, NB + b)
                    v.tensor_tensor(x[:, b - 1, :, :].rearrange("p i d -> p (i d)"), bank[5 + (b - 1) % 2],
                                    xb[:, b - 1, :, :].rearrange("p i d -> p (i d)"), ALU.add).then_inc(dve_x, 1)
                    v.wait_ge(dve_x, NB + b)
                    layernorm_stats(b - 1)
                if b >= 2:
                    layernorm_apply(2, b - 2)
            layernorm_apply(2, NB - 1)

            for b in range(NB):
                v.wait_ge(pe_s1, b + 1)
                if b >= 2:
                    v.wait_ge(act_s1, b - 1)
                s = sc[:, b % 2]
                step(v.tensor_tensor(s, bank[4 + b % 2][:, 0:NI * KEYS].rearrange("p (i k) -> p i k", i=NI),
                                     maskb[:, b, :].rearrange("p (i k) -> p i k", i=NI), ALU.add))
                settle()
                step(v.tensor_reduce(scm[:, b % 2, :], s, AX.X, ALU.max))
                settle()
                v.scalar_tensor_tensor(out=s, in0=wide(scm[:, b % 2, :].unsqueeze(2), P, NI, KEYS), scalar=-BIG / 2,
                                       in1=s, op0=ALU.max, op1=ALU.subtract).then_inc(dve_s1, 1)
            for b in range(NB):
                for pair in range(2):
                    v.wait_ge(pe_o1, 2 * b + pair + 1)
                    o = bank[6 + pair][:, 0:2 * (D + 1)].rearrange("p (i d) -> p i d", i=2)
                    step(v.reciprocal(srec[:, b % 2, 2 * pair:2 * pair + 2], o[:, :, D]))
                    settle()
                    v.wait_ge(pool_xb, 2 * NB + b + 1)
                    for i in range(2):
                        t = 2 * pair + i
                        ins = v.scalar_tensor_tensor(out=x[:, b, t, :], in0=o[:, i, 0:D], scalar=srec[:, b % 2, t:t + 1],
                                                     in1=xb[:, b, t, :], op0=ALU.mult, op1=ALU.add)
                        if t < NI - 1:
                            step(ins)
                ins.then_inc(dve_x, 1)
                settle()
                v.wait_ge(dve_x, 2 * NB + b + 1)
                layernorm_stats(b)
            for b in range(NB):
                layernorm_apply(3, b)

            for b in range(NB):
                v.wait_ge(pe_lg, NB + b + 1)
                s, t, m = r_s[:, b % 2], r_a[:, b % 2], r_m[:, b % 2]
                lg = bank[4 + b][:, 0:NI * E1].rearrange("p (i e) -> p i e", i=NI)
                step(v.tensor_reduce(m[:, 0, :], lg, AX.X, ALU.max))
                settle()
                v.tensor_tensor(t, lg, wide(m[:, 0, :].unsqueeze(2), P, NI, E1), ALU.subtract).then_inc(dve_g, 1)
                v.wait_ge(act_lg, NB + b + 1)
                route(b, s, None)
                step(v.tensor_tensor(gate[:, b], r_o1[:, b % 2], r_o2[:, b % 2], ALU.add))
                settle()
            for n in range(E1 * NB + 1):
                if n < E1 * NB:
                    for c in range(4):
                        j = 4 * n + c
                        v.wait_ge(act_gl, j + 1)
                        if n >= 2 and c == 0:
                            v.wait_ge(pe_dn, n - 1)
                        v.tensor_tensor(hT[:, n % 2, c, :], gl[:, j % 2, :], bank[2 + j % 2], ALU.mult).then_inc(dve_hT, 1)
                if n >= 1:
                    e, b = divmod(n - 1, NB)
                    v.wait_ge(pe_dn, n)
                    if n > NB:
                        v.wait_ge(dve_acc, (n - NB) * NI)
                    for i in range(NI):
                        v.scalar_tensor_tensor(out=x[:, b, i, :], in0=bank[4 + (n - 1) % 2][:, i * D:(i + 1) * D],
                                               scalar=gate[:, b, i, e:e + 1], in1=x[:, b, i, :],
                                               op0=ALU.mult, op1=ALU.add).then_inc(dve_acc, 1)

        @block.scalar
        def _(s):
            def copy_xT(k, b, src):
                s.wait_ge(pe_xT, k * NB + b + 1)
                s.activation(xnT[:, b, :], src, ACT.Copy).then_inc(xT_ready, 1)

            for half in range(2):
                s.wait_ge(pe_kz, half + 1)
                s.wait_ge(dve_fmT, 1)
                s.activation(kf[:, half, :], bank[2 + half][:, 0:NB * KEYS], ACT.Exp, bias=fmT[:, HD:HD + 1]).then_inc(act_kf, 1)
            for b in range(NB):
                copy_xT(0, b, bank[4 + b % 2])
                for half in range(2):
                    n = 2 * b + half
                    s.wait_ge(pe_z, n + 1)
                    if b >= 1:
                        s.wait_ge(dve_q, 2 * n - 2)
                    s.activation(qf[:, half, :], bank[half], ACT.Exp, bias=fmT[:, HD:HD + 1]).then_inc(act_q, 1)
            for n in range(2 * NB):
                s.wait_ge(pe_vt, n + 1)
                if n == 0:
                    s.wait_ge(pool_ind, 7)
                for c0, c1, bk in ((0, 4, 2), (4, NC, 3)):
                    rows = chunk_rows(c1 - 1)
                    s.activation(Vx[0:rows, n, c0:c1, :, 0:FD],
                                 bank[bk][0:rows, 0:(c1 - c0) * P].rearrange("r (c h f) -> r c h f", h=HH, f=FD),
                                 ACT.Copy).then_inc(act_vx, 1)
            for b in range(NB + 1):
                if b < NB:
                    s.wait_ge(pe_nmT, b + 1)
                    s.activation(nmT[:, b % 2, :], bank[0].bitcast(BF16)[0:3 * HEADS, 0:SEQ], ACT.Copy).then_inc(act_nmT, 1)
                    for j in range(2 * NC):
                        n = 2 * NC * b + j
                        rows = chunk_rows(j % NC)
                        s.wait_ge(pe_sc, n + 1)
                        if b >= 1 and j == 0:
                            s.wait_ge(pe_av, NI * b)
                        s.activation(ex[0:rows, j, :], bank[1 + n % 3][0:rows, :], ACT.Exp, scale=SCALE).then_inc(act_ex, 1)
                if b >= 1:
                    for pair in range(2):
                        s.wait_ge(pe_onT, (b - 1) * NI + 2 * pair + 2)
                        s.activation(onT[:, 2 * pair:2 * pair + 2, :, :].rearrange("p i a t -> p (i a t)"),
                                     bank[1 + pair], ACT.Copy).then_inc(act_onT, 2)
            for b in range(NB):
                copy_xT(1, b, bank[b])
            for b in range(NB):
                s.wait_ge(pe_lg, b + 1)
                if b >= 2:
                    s.wait_ge(dve_g, b - 1)
                s.activation(r_s[:, b % 2], bank[4 + b][:, 0:NI * E0].rearrange("p (i e) -> p i e", i=NI),
                             ACT.Exp, scale=-1.0).then_inc(act_lg, 1)
            s.wait_ge(ld_small, 16 * N_SMALL)
            for b in range(NB):
                for c in range(5):
                    n = 5 * b + c
                    s.wait_ge(pe_h, n + 1)
                    if c < 4:
                        m = 4 * b + c
                        if m >= 2:
                            s.wait_ge(dve_hg, m - 1)
                        s.activation(hraw[:, m % 2, :], bank[1 + n % 2], ACT.Gelu, bias=b1[:, c:c + 1]).then_inc(act_h, 1)
                    else:
                        if b >= 2:
                            s.wait_ge(pe_y, b - 1)
                        s.activation(hs[:, b % 2, :], bank[1 + n % 2][0:H0, :], ACT.Gelu, bias=bs1[:, 0:1]).then_inc(act_h, 1)
            for b in range(NB):
                copy_xT(2, b, bank[b])
            for b in range(NB):
                s.wait_ge(dve_s1, b + 1)
                if b >= 2:
                    s.wait_ge(pe_pT, b - 1)
                s.activation(pr[:, b % 2], sc[:, b % 2], ACT.Exp, scale=-SCALE).then_inc(act_s1, 1)
            for b in range(NB):
                s.wait_ge(pe_pT, b + 1)
                if b >= 2:
                    s.wait_ge(pe_o1, 2 * (b - 1))
                s.activation(prT[:, b % 2, :], bank[b % 2][0:KEYS, :], ACT.Copy).then_inc(act_pT, 1)
            for b in range(NB):
                copy_xT(3, b, bank[b])
            for b in range(NB):
                s.wait_ge(dve_g, NB + b + 1)
                s.activation(r_s[:, b % 2], r_a[:, b % 2], ACT.Exp).then_inc(act_lg, 1)
            for e in range(E1):
                for c in range(3):
                    n = 3 * e + c
                    s.wait_ge(pe_upT, n + 1)
                    dst = upT[:, e, c * 512:(c + 1) * 512] if c < 2 else dnT[:, e, :, :].rearrange("p c d -> p (c d)")
                    s.activation(dst, bank[n % 2], ACT.Copy).then_inc(act_upT, 1)
            for n in range(E1 * NB * 4):
                s.wait_ge(pe_gu, n + 1)
                if n >= 2:
                    s.wait_ge(dve_hT, n - 1)
                s.activation(gl[:, n % 2, :], bank[n % 2], ACT.Gelu).then_inc(act_gl, 1)

        @block.tensor
        def _(pe):
            def mm(out_, lhsT, rhs, start=True, stop=True):
                return pe.matmul(out_, lhsT, rhs, start=start, stop=stop, skip_group_check=True)

            def transpose_xn(k, b, dst):
                for i in range(NI):
                    pe.wait_ge(dve_xn, (k * NB + b) * NI + i + 1)
                    ins = pe.transpose(dst[:, i * P:(i + 1) * P], xn[:, b, i, :], ident[:, :])
                ins.then_inc(pe_xT, 1)

            pe.wait_ge(pool_ident, 2)
            pe.wait_ge(ld_ctx, 16)
            for b in range(NB):
                ins = pe.transpose(bank[0][:, b * KEYS:(b + 1) * KEYS], ctx_tok[:, b, :], ident[0:KEYS, 0:KEYS])
            ins.then_inc(pe_ctxT, 1)
            pe.wait_ge(ld_fm, 16 * N_FM)
            pe.wait_ge(pool_mask, 2)
            pe.wait_ge(dve_c, 1)
            mm(bank[1][:, 0:HD], fmrep[:, :, :].rearrange("e h d -> e (h d)"), ident[0:HD, 0:HD])
            mm(bank[1][:, HD:HD + 1], isgn[:, :, :, :].rearrange("e h s d -> e (h s d)"), fm[:, HD:HD + 1]).then_inc(pe_fm, 1)
            pe.wait_ge(dve_ctxT, 1)
            pe.wait_ge(dve_Wz, 4)
            for half in range(2):
                mm(bank[2 + half][:, 0:NB * KEYS], Wz[:, half].rearrange("p h s d -> p (h s d)"), ctxT[:, :]).then_inc(pe_kz, 1)
            for b in range(NB):
                if b >= 2:
                    pe.wait_ge(xT_ready, b - 1)
                transpose_xn(0, b, bank[4 + b % 2])
                pe.wait_ge(xT_ready, b + 1)
                for half in range(2):
                    n = 2 * b + half
                    if b >= 1:
                        pe.wait_ge(act_q, n - 1)
                    mm(bank[half], Wz[:, half].rearrange("p h s d -> p (h s d)"), xnT[:, b, :]).then_inc(pe_z, 1)
            pe.wait_ge(pool_ind, 6)
            for half in range(2):
                for c in range(NC):
                    ins = pe.transpose(bank[6 + half].bitcast(BF16)[0:3 * HEADS, c * P:(c + 1) * P],
                                       indw[:, half, c, :, :].rearrange("p a h -> p (a h)"), identb[:, :])
                ins.then_inc(pe_kz, 1)
            pe.wait_ge(act_kf, 2)
            for n in range(2 * NB):
                b, half = divmod(n, 2)
                pe.wait_ge(dve_kb, n + 1)
                pe.wait_ge(pool_kb, n + 1)
                if n >= 1:
                    pe.wait_ge(act_vx, 2 * n)
                for c in range(NC):
                    rows = chunk_rows(c)
                    bk, at = (2, c * P) if c < 4 else (3, 0)
                    mm(bank[bk][0:rows, at:at + P], kbhi[:, b, half, c * P:c * P + rows], identr[:, :], True, False)
                    ins = mm(bank[bk][0:rows, at:at + P], kblo[:, b, half, c * P:c * P + rows], identr[:, :], False, True)
                ins.then_inc(pe_vt, 1)
            pe.wait_ge(ld_w, 16 * N_W)
            pe.wait_ge(act_q, 2 * NB)
            for n in range(3):
                ins = pe.transpose(bank[0][:, n * D:(n + 1) * D], wnat[:, n + 1, :], ident[:, :])
            ins.then_inc(pe_wT, 1)
            for n in range(2):
                pe.transpose(bank[1][:, n * D:(n + 1) * D], fcn[:, n, :], ident[:, :])
            pe.transpose(bank[1][:, 2 * D:2 * D + E1], gate1n[:, :], ident[0:E1, 0:E1]).then_inc(pe_wT, 1)
            pe.wait_ge(dve_wT, 3)
            pe.wait_ge(act_vx, 4 * NB)
            for n in range(2):
                mm(bank[2 + n][:, 0:NB * KEYS], wT[:, n, :], ctxT[:, :]).then_inc(pe_kv, 1)
            pe.wait_ge(dve_kv, 2)
            mm(bank[0][:, 0:NB * KEYS], wnat[:, 0, :], KT[:, :]).then_inc(pe_ak, 1)
            mm(bank[1][0:1, 0:NB * KEYS], bqkv[:, 0:1], KT[:, :]).then_inc(pe_ak, 1)
            for b in range(NB):
                ins = mm(bank[2][0:KEYS, b * D:(b + 1) * D], VT[:, b * KEYS:(b + 1) * KEYS], wT[:, 2, :])
            ins.then_inc(pe_ak, 1)
            pe.wait_ge(dve_ak, 3)

            def max_job(b, j):
                i, half = divmod(j, 2)
                n = b * 2 * NI + j
                if n >= 2:
                    pe.wait_ge(dve_max, n - 1)
                if b >= 2 and j < 2:
                    pe.wait_ge(dve_on, NI * (b - 1))
                pair = 4 + 2 * (n % 2)
                for a in range(2):
                    ins = mm(bank[pair + a][:, 0:HK // 2], qhi[:, b, half, i * P:(i + 1) * P],
                             kbhi[:, b, half, a * (HK // 2):(a + 1) * (HK // 2)])
                ins.then_inc(pe_max, 1)

            def score_job(b, j):
                half, c = divmod(j, NC)
                n = b * 2 * NC + j
                rows = chunk_rows(c)
                cols = slice(c * P, c * P + rows)
                o = bank[1 + n % 3][0:rows, :]
                if n >= 3:
                    pe.wait_ge(act_ex, n - 2)
                mm(o, sel[:, half, cols], nmT[:, b % 2, :], True, False)
                mm(o, kbhi[:, b, half, cols], qhi[:, b, half, :], False, False)
                mm(o, kblo[:, b, half, cols], qhi[:, b, half, :], False, False)
                mm(o, kbhi[:, b, half, cols], qlo[:, b, half, :], False, True).then_inc(pe_sc, 1)

            pe.wait_ge(dve_q, 4 * NB)
            pe.wait_ge(dve_Wz, 6)
            for j in range(2 * NI):
                max_job(0, j)
            for b in range(NB + 1):
                if b >= 1:
                    pe.wait_ge(act_ex, 2 * NC * b)
                    for i in range(NI):
                        o = bank[4 + i]
                        if b >= 2:
                            pe.wait_ge(dve_on, NI * (b - 2) + i + 1)
                        pe.wait_ge(dve_max, 2 * NI * min(b + 1, NB))
                        for half in range(2):
                            for c in range(NC):
                                rows = chunk_rows(c)
                                h0, h1 = chunk_heads(c)
                                at = (half * HH + h0) * (FD + 1)
                                ins = mm(o[:, at:at + (h1 - h0) * (FD + 1)],
                                         ex[0:rows, half * NC + c, i * P:(i + 1) * P],
                                         Vx[0:rows, 2 * (b - 1) + half, c, h0:h1, :].rearrange("r h f -> r (h f)"),
                                         start=(half == c == 0), stop=(half == 1 and c == NC - 1))
                        ins.then_inc(pe_av, 1)
                if b < NB:
                    pe.wait_ge(dve_nm, b + 1)
                    for i in range(NI):
                        ins = pe.transpose(bank[0].bitcast(BF16)[0:3 * HEADS, i * P:(i + 1) * P],
                                           nm[:, b % 2, i].rearrange("p a h -> p (a h)"), identb[:, :])
                    ins.then_inc(pe_nmT, 1)
                    pe.wait_ge(act_nmT, b + 1)
                    if b >= 2:
                        pe.wait_ge(dve_x, b - 1)
                        pe.wait_ge(act_onT, NI * (b - 1))
                    for j in range(2 * NC):
                        score_job(b, j)
                        if b + 1 < NB and j < 2 * NI:
                            max_job(b + 1, j)
                if b >= 1:
                    pe.wait_ge(act_ex, 2 * NC * min(b + 1, NB))
                    for i in range(NI):
                        n = (b - 1) * NI + i
                        pe.wait_ge(dve_on, n + 1)
                        if i == 0 and b >= 2:
                            pe.wait_ge(dve_x, b - 1)
                        for a in range(2):
                            at = 256 * (i % 2) + a * P
                            ins = pe.transpose(bank[1 + i // 2][:, at:at + P], on[:, i, a * P:(a + 1) * P], ident[:, :])
                        if i % 2:
                            ins.then_inc(pe_onT, 2)
                    for i in range(NI):
                        pe.wait_ge(act_onT, (b - 1) * NI + i + 1)
                        for a in range(2):
                            ins = mm(bank[3][:, i * D:(i + 1) * D], onT[:, i, a, :], fcT[:, a, :], a == 0, a == 1)
                    ins.then_inc(pe_fc, 1)

            for b in range(NB):
                if b == 3:
                    pe.wait_ge(dve_x, NB)
                transpose_xn(1, b, bank[b])
            pe.wait_ge(ld_small, 16 * N_SMALL)
            for b in range(NB):
                pe.wait_ge(xT_ready, NB + b + 1)
                pe.wait_ge(dve_on, NB * NI)
                for i in range(NI):
                    ins = mm(bank[4 + b][:, i * E0:(i + 1) * E0], xnT[:, b, i * P:(i + 1) * P], gate0[:, :])
                ins.then_inc(pe_lg, 1)
            pe.wait_ge(pool_mask, 3)
            for b in range(NB + 1):
                if b < NB:
                    pe.wait_ge(dve_g, b + 1)
                    if b >= 1:
                        pe.wait_ge(dve_gT, b)
                    for i in range(NI):
                        ins = pe.transpose(bank[0].bitcast(BF16)[0:3 * E0, i * P:(i + 1) * P],
                                           g3[:, b, i].rearrange("p a e -> p (a e)"), identb[:, :])
                    ins.then_inc(pe_gT, 1)
                    for c in range(5):
                        n = 5 * b + c
                        if n >= 2:
                            pe.wait_ge(act_h, n - 1)
                        if c < 4:
                            mm(bank[1 + n % 2], W1[:, c * P:(c + 1) * P], xnT[:, b, :]).then_inc(pe_h, 1)
                            m = 4 * b + c
                            if c == 0:
                                pe.wait_ge(dve_gT, b + 1)
                                pe.wait_ge(act_lg, NB)
                            if m >= 2:
                                pe.wait_ge(dve_hg, m - 1)
                            mm(bank[3 + m % 2], selG[:, c, :], gT3[:, b, :]).then_inc(pe_G, 1)
                        else:
                            mm(bank[1 + n % 2][0:H0, :], Ws1[:, :], xnT[:, b, :]).then_inc(pe_h, 1)
                if b >= 1:
                    p = b - 1
                    pe.wait_ge(dve_hg, 4 * b)
                    pe.wait_ge(act_h, 5 * b)
                    if p >= 2:
                        pe.wait_ge(dve_x, NB + p - 1)
                    for i in range(NI):
                        o = bank[5 + p % 2][:, i * D:(i + 1) * D]
                        tok = slice(i * P, (i + 1) * P)
                        for c in range(4):
                            mm(o, hg[:, p % 2, c, tok], W2[:, c, :], c == 0, False)
                        mm(o, hs[:, p % 2, tok], Ws2[:, :], False, False)
                        for t in range(3):
                            ins = mm(o, gT3[:, p, tok], b2s[:, t, :], False, t == 2)
                    ins.then_inc(pe_y, 1)

            pe.wait_ge(dve_x, 2 * NB)
            for b in range(NB):
                transpose_xn(2, b, bank[b])
            for b in range(NB):
                pe.wait_ge(xT_ready, 2 * NB + b + 1)
                if b >= 2:
                    pe.wait_ge(dve_s1, b - 1)
                for i in range(NI):
                    o = bank[4 + b % 2][:, i * KEYS:(i + 1) * KEYS]
                    mm(o, xnT[:, b, i * P:(i + 1) * P], keyA[:, b * KEYS:(b + 1) * KEYS], True, False)
                    ins = mm(o, ones_row[:, :], keyc[:, b * KEYS:(b + 1) * KEYS], False, True)
                ins.then_inc(pe_s1, 1)
            for b in range(NB + 1):
                if b < NB:
                    pe.wait_ge(act_s1, b + 1)
                    if b >= 2:
                        pe.wait_ge(act_pT, b - 1)
                    for i in range(NI):
                        ins = pe.transpose(bank[b % 2][0:KEYS, i * P:(i + 1) * P], pr[:, b % 2, i, :], ident[:, :])
                    ins.then_inc(pe_pT, 1)
                if b >= 1:
                    p = b - 1
                    pe.wait_ge(act_pT, b)
                    for pair in range(2):
                        if p >= 1:
                            pe.wait_ge(dve_x, 2 * NB + p)
                        for i in range(2):
                            t = 2 * pair + i
                            ins = mm(bank[6 + pair][:, i * (D + 1):(i + 1) * (D + 1)],
                                     prT[:, p % 2, t * P:(t + 1) * P], Vo[:, p, :])
                        ins.then_inc(pe_o1, 1)

            for b in range(NB):
                transpose_xn(3, b, bank[b])
            for b in range(NB):
                pe.wait_ge(xT_ready, 3 * NB + b + 1)
                if b == 0:
                    pe.wait_ge(dve_x, 3 * NB)
                for i in range(NI):
                    ins = mm(bank[4 + b][:, i * E1:(i + 1) * E1], xnT[:, b, i * P:(i + 1) * P], gate1[:, :])
                ins.then_inc(pe_lg, 1)
            for e in range(E1):
                pe.wait_ge(ld_up[e], 16)
                pe.wait_ge(ld_dn[e], 16)
                for c in range(3):
                    n = 3 * e + c
                    if n >= 2:
                        pe.wait_ge(act_upT, n - 1)
                    for j in range(4):
                        src = upn[:, e, 4 * c + j, :] if c < 2 else dnn[:, e, j * P:(j + 1) * P]
                        ins = pe.transpose(bank[n % 2][:, j * P:(j + 1) * P], src, ident[:, :])
                    ins.then_inc(pe_upT, 1)
            pe.wait_ge(act_upT, 3 * E1)
            for n in range(E1 * NB + 1):
                if n < E1 * NB:
                    e, b = divmod(n, NB)
                    for c in range(4):
                        j = 4 * n + c
                        if j >= 2:
                            pe.wait_ge(dve_hT, j - 1)
                        mm(bank[j % 2], upT[:, e, c * P:(c + 1) * P], xnT[:, b, :])
                        mm(bank[2 + j % 2], upT[:, e, F1 + c * P:F1 + (c + 1) * P], xnT[:, b, :]).then_inc(pe_gu, 1)
                if n >= 1:
                    e, b = divmod(n - 1, NB)
                    pe.wait_ge(dve_hT, 4 * n)
                    if n >= 3:
                        pe.wait_ge(dve_acc, (n - 2) * NI)
                    elif n == 1:
                        pe.wait_ge(act_lg, 2 * NB)
                    for i in range(NI):
                        for c in range(4):
                            ins = mm(bank[4 + (n - 1) % 2][:, i * D:(i + 1) * D],
                                     hT[:, (n - 1) % 2, c, i * P:(i + 1) * P], dnT[:, e, c, :], c == 0, c == 3)
                    ins.then_inc(pe_dn, 1)


_INS = ["x", "ctx_1024", "mask_BxSxS2_ik0", "L0_xattn_fm_w", "L0_xattn_fm_b", "L0_xattn_fc_w", "L0_xattn_fc_b",
        "L0_ffn_gate_W", "L0_ffn_W1", "L0_ffn_b1", "L0_ffn_W2", "L0_ffn_b2", "L0_ffn_Ws1", "L0_ffn_bs1", "L0_ffn_Ws2",
        "L0_ffn_bs2", "L0_ffn_route_scale", "L1_xattn_Wq", "L1_xattn_bq", "L1_xattn_Wk", "L1_xattn_bk", "L1_xattn_Wv",
        "L1_xattn_bv", "L1_xattn_Wo", "L1_xattn_bo", "L1_ffn_gate_w", "L1_ffn_gate_up_w", "L1_ffn_down_w"]


def kernel(**inputs):
    import numpy as _np
    import concourse.bacc as _bacc
    from concourse import mybir as _mybir
    from concourse.bass_utils import run_bass_kernel_spmd as _run

    nc = _bacc.Bacc("TRN2", target_bir_lowering=False, num_devices=1)
    arrays, aps = {}, {}
    for name in _INS:
        a = _np.ascontiguousarray(inputs[name])
        if a.ndim == 0:
            a = a.reshape(1)
        arrays[f"in_{name}_dram"] = a
        aps[name] = nc.dram_tensor(f"in_{name}_dram", a.shape, _mybir.dt.from_np(a.dtype), kind="ExternalInput").ap()
    out = nc.dram_tensor("out_0_dram", (NB, SEQ, D), F32, kind="ExternalOutput").ap()
    two_layer_kernel(nc, aps, out)
    r = _run(nc, [arrays], core_ids=[0])
    return r.results[0]["out_0_dram"]
```

```python
from contextlib import ExitStack

import concourse.bass as bass
from concourse import mybir

F32 = mybir.dt.float32
F32R = mybir.dt.float32r
BF16 = mybir.dt.bfloat16
I32 = mybir.dt.int32
ALU = mybir.AluOpType
ACT = mybir.ActivationFunctionType
AX = mybir.AxisListType

P = 128
NB, SEQ, D = 4, 512, 128
NI = SEQ // P
KEYS = 77
HEADS, HD, FD = 16, 8, 16
HH = HEADS // 2
HK = HH * KEYS
NC = -(-HK // P)
E0, H0 = 8, 64
E1, F1 = 8, 512
WR = 3
NT = NB * NI
CH = 2
ROWS = NT * P
NBLK = CH * NT + E1 - 1
EPS = 1e-5
BIG = 3.0e38
SCALE = float(D) ** -0.5
UNROLL = 4
LOOP0 = 4
LOOP1 = LOOP0 + (NBLK - 1 - LOOP0) // UNROLL * UNROLL


def chunk_rows(c):
    return min(P, HK - c * P)


def chunk_heads(c):
    first = c * P // KEYS
    last = (c * P + chunk_rows(c) - 1) // KEYS
    return first, last + 1


def two_layer_kernel(nc, A, out):
    with ExitStack() as ctx:
        def sem(name):
            return ctx.enter_context(nc.semaphore(name))

        def sb(name, shape, dt=F32, at=ctx):
            return at.enter_context(nc.sbuf_tensor(name, shape, dt))

        ps = ctx.enter_context(nc.psum_tensor("ps", [P, 8, 512], F32))
        bank = [ps[:, i, :] for i in range(8)]

        x = sb("x", [P, NB, NI, D])
        xb = sb("xb", [P, NB, NI, D])
        xn = sb("xn", [P, NB, NI, D])
        xnT = sb("xnT", [P, NB, SEQ])
        stats = sb("stats", [P, NB, NI, 6])
        mv = sb("mv", [P, NB, NI, 2])
        rstd = sb("rstd", [P, NB, NI])
        ident = sb("ident", [P, P])
        identb = sb("identb", [P, P], BF16)
        identr = sb("identr", [P, P], F32R)
        neghalf = sb("neghalf", [P, NI])
        ones_row = sb("ones_row", [1, P])
        biases = sb("biases", [P, 3, D])
        fcT = sb("fcT", [P, 2, D])
        W1 = sb("W1", [P, E0 * H0])
        Ws1 = sb("Ws1", [P, H0])
        gate0 = sb("gate0", [P, E0])
        W2 = sb("W2", [P, 4, D])
        Ws2 = sb("Ws2", [H0, D])
        b1 = sb("b1", [P, 4])
        bs1 = sb("bs1", [H0, 1])
        b2 = sb("b2", [3 * E0, D])
        b2s = sb("b2s", [3 * E0, 3, D], BF16)
        b2r = sb("b2r", [3 * E0, D])
        route_scale = sb("route_scale", [P, 1])
        gate1 = sb("gate1", [P, E1])
        mask_i = sb("mask_i", [P, NB, NI * KEYS], I32)
        maskb = mask_i[:, :, :].bitcast(F32)
        keyA = sb("keyA", [P, NB * KEYS])
        keyc = sb("keyc", [1, NB * KEYS])
        Vo = sb("Vo", [KEYS, NB, D + 1])
        iota8 = sb("iota8", [P, NI, E0])
        sel = sb("sel", [3 * HEADS, 2, NC * P], BF16)
        selG = sb("selG", [3 * E0, 4, P], BF16)
        r_s = sb("r_s", [P, 2, NI, E0])
        r_a = sb("r_a", [P, 2, NI, E0])
        r_b = sb("r_b", [P, 2, NI, E0])
        r_o1 = sb("r_o1", [P, 2, NI, E0])
        r_o2 = sb("r_o2", [P, 2, NI, E0])
        r_m = sb("r_m", [P, 2, 6, NI])

        l0 = ExitStack()
        ctx_tok = sb("ctx_tok", [KEYS, NB, D], at=l0)
        ctxT = sb("ctxT", [P, NB * KEYS], at=l0)
        wnat = sb("wnat", [P, 4, D], at=l0)
        wT = sb("wT", [P, 3, D], at=l0)
        bqkv = sb("bqkv", [P, 3], at=l0)
        KT = sb("KT", [P, NB * KEYS], at=l0)
        VT = sb("VT", [P, NB * KEYS], at=l0)
        fcn = sb("fcn", [P, 2, D], at=l0)
        gate1n = sb("gate1n", [E1, D], at=l0)
        fm = sb("fm", [HD, HD + 1], at=l0)
        fmT = sb("fmT", [P, HD + 1], at=l0)
        mask16 = sb("mask16", [P, 2, HEADS], at=l0)
        maskK = sb("maskK", [P, HH], at=l0)
        ind = sb("ind", [P, NC, HH], at=l0)
        indw = sb("indw", [P, 2, NC, 3, HEADS], BF16, at=l0)
        Wz = sb("Wz", [P, 2, HH, 2, HD], at=l0)
        kbhi = sb("kbhi", [P, NB, 2, HK], F32R, at=l0)
        kblo = sb("kblo", [P, NB, 2, HK], F32R, at=l0)
        Vx = sb("Vx", [P, NB * 2, NC, HH, FD + 1], at=l0)
        qf = sb("qf", [P, 2, SEQ], at=l0)
        qhi = sb("qhi", [P, NB, 2, SEQ], F32R, at=l0)
        qlo = sb("qlo", [P, NB, 2, SEQ], F32R, at=l0)
        mx = sb("mx", [P, 2, NI, HEADS], at=l0)
        nm = sb("nm", [P, 2, NI, 3, HEADS], BF16, at=l0)
        nmr = sb("nmr", [P, 2, NI, HEADS], at=l0)
        nmT = sb("nmT", [3 * HEADS, 2, SEQ], BF16, at=l0)
        selGt = sb("selGt", [3 * E0, 3, 4 * P], BF16, at=l0)
        early = ExitStack()
        kf = sb("kf", [P, 2, NB * KEYS], at=early)
        kfhi = sb("kfhi", [P, 2, NB * KEYS], F32R, at=early)
        kflo = sb("kflo", [P, 2, NB * KEYS], F32R, at=early)
        isgn = sb("isgn", [HD, HH, 2, HD], at=early)
        fmrep = sb("fmrep", [HD, HEADS, HD], at=early)
        early.close()
        ex = sb("ex", [P, 2 * NC, SEQ], at=l0)
        rec = sb("rec", [P, 2, HEADS], at=l0)
        on = sb("on", [P, NI, HEADS * FD], at=l0)
        onT = sb("onT", [P, NI, 2, P], at=l0)
        l0.close()

        sc = sb("sc", [P, 2, NI, KEYS])
        scm = sb("scm", [P, 2, NI])
        pr = sb("pr", [P, NB, NI, KEYS])
        prT = sb("prT", [KEYS, 2, SEQ])
        srec = sb("srec", [P, 2, NI])
        upn = sb("upn", [P, WR, 8, D])
        dnn = sb("dnn", [P, WR, F1])
        uphi = sb("uphi", [P, E1 * 2 * F1], F32R)
        uplo = sb("uplo", [P, E1 * 2 * F1], F32R)
        dnT = sb("dnT", [P, E1 * F1])
        onehot = sb("onehot", [P, CH, NT, E1])
        wgt = sb("wgt", [P, CH, NT])
        cnt = sb("cnt", [P, NT + 1, E1], BF16)
        lower = sb("lower", [P, P], BF16)
        onesb = sb("onesb", [P, P], BF16)
        before = sb("before", [P, E1, E1])
        iota_n = sb("iota_n", [P, E1, NT])
        iota_k = sb("iota_k", [P, NBLK])
        iota_r = sb("iota_r", [P, P], BF16)
        tile_q = sb("tile_q", [P, CH * NT], BF16)
        p_one = sb("p_one", [P, 1])
        pad_row = sb("pad_row", [P, NBLK])
        m_n = sb("m_n", [P, E1])
        m_cmp = sb("m_cmp", [P, E1, NT])
        m_nb = sb("m_nb", [P, E1])
        m_bb = sb("m_bb", [P, E1])
        m_ce = sb("m_ce", [P, E1])
        m_lt = sb("m_lt", [P, E1, E1])
        m_at = sb("m_at", [P, NT, E1])
        m_pos = sb("m_pos", [P, CH * NT])
        m_posi = sb("m_posi", [P, 3, CH * NT], I32)
        m_posf = sb("m_posf", [P, 2, CH * NT])
        m_pe = sb("m_pe", [P, CH, NT, E1])
        m_k = sb("m_k", [1, NBLK, E1])
        m_kf = sb("m_kf", [1, NBLK])
        blk_e = sb("blk_e", [1, NBLK], I32)
        m_pack = sb("m_pack", [1, NBLK])
        blk_es = sb("blk_es", [1, NBLK], I32)
        inv = sb("inv", [P, 2, NBLK])
        row_f = sb("row_f", [P, 3, NBLK])
        src_row = sb("src_row", [P, NBLK], I32)
        dst_row = sb("dst_row", [P, NBLK], I32)
        mlp = ExitStack()
        hraw = sb("hraw", [P, 2, SEQ], at=mlp)
        hg = sb("hg", [P, 2, 4, SEQ], at=mlp)
        hs = sb("hs", [H0, 2, SEQ], at=mlp)
        g3 = sb("g3", [P, NB, NI, 3, E0], BF16, at=mlp)
        g3r = sb("g3r", [P, NB, NI, E0], at=mlp)
        gT3 = sb("gT3", [3 * E0, NB, SEQ], BF16, at=mlp)
        mlp.close()
        slots = ExitStack()
        r_hot = sb("r_hot", [P, CH * NT, P], BF16, at=slots)
        b_hot = sb("b_hot", [P, CH * NT, NBLK], BF16, at=slots)
        b_val = sb("b_val", [P, CH * NT, 2, NBLK], BF16, at=slots)
        slots.close()
        yc = sb("yc", [P, 2, CH, NI, D])
        gl = sb("gl", [P, 2, F1])
        hh = sb("hh", [P, 2, F1])
        hhT = sb("hhT", [P, 2, 4, P])
        xg = sb("xg", [P, 2, D])
        xghi = sb("xghi", [P, 2, P], F32R)
        xglo = sb("xglo", [P, 2, P], F32R)
        yb = sb("yb", [P, 2, D])
        xn_dram = nc.dram_tensor("xn_dram", (ROWS, D), F32, kind="Internal").ap()
        y_dram = nc.dram_tensor("y_dram", (CH * ROWS + NBLK * P, D), F32, kind="Internal").ap()

        n_ld = [0]

        def load_sem(name):
            return sem("ld_" + name)

        ld_x = [load_sem(f"x{b}") for b in range(NB)]
        ld_ctx, ld_fm, ld_w, ld_small, ld_mask = (load_sem(n) for n in ("ctx", "fm", "w", "small", "mask"))
        ld_up = [load_sem(f"up{e}") for e in range(E1)]
        ld_dn = [load_sem(f"dn{e}") for e in range(E1)]
        stored = sem("stored")
        pool_ident, pool_const, pool_mask, pool_ind, pool_kb = (sem("pool_" + n) for n in ("ident", "const", "mask", "ind", "kb"))
        pool_xb, pool_var, pool_rstd, pool_q = (sem("pool_" + n) for n in ("xb", "var", "rstd", "q"))
        dve_c, dve_link = sem("dve_c"), sem("dve_link")
        pe_ctxT, pe_fm, pe_kz, pe_wT, pe_kv, pe_ak, pe_vt = (sem("pe_" + n) for n in ("ctxT", "fm", "kz", "wT", "kv", "ak", "vt"))
        dve_ctxT, dve_fmT, dve_Wz, dve_kf, dve_kb, dve_wT, dve_kv, dve_ak = (
            sem("dve_" + n) for n in ("ctxT", "fmT", "Wz", "kf", "kb", "wT", "kv", "ak"))
        act_kf, act_vx = sem("act_kf"), sem("act_vx")
        dve_mv, dve_xn, pe_xT, xT_ready = sem("dve_mv"), sem("dve_xn"), sem("pe_xT"), sem("act_xT")
        pe_z, act_q, dve_q = sem("pe_z"), sem("act_q"), sem("dve_q")
        pe_max, dve_max, dve_nm, pe_nmT, act_nmT = (sem(n) for n in ("pe_max", "dve_max", "dve_nm", "pe_nmT", "act_nmT"))
        pe_sc, act_ex, pe_av, dve_on, pe_onT, act_onT, pe_fc = (
            sem(n) for n in ("pe_sc", "act_ex", "pe_av", "dve_on", "pe_onT", "act_onT", "pe_fc"))
        dve_x = sem("dve_x")
        pe_lg, act_lg, dve_g, pe_gT, dve_gT, pe_G, pe_h, act_h, dve_hg, pe_y = (
            sem(n) for n in ("pe_lg", "act_lg", "dve_g", "pe_gT", "dve_gT", "pe_G", "pe_h", "act_h", "dve_hg", "pe_y"))
        pe_s1, dve_s1, act_s1, pe_pT, act_pT, pe_o1 = (sem(n) for n in ("pe_s1", "dve_s1", "act_s1", "pe_pT", "act_pT", "pe_o1"))
        pe_upT, act_upT, dve_upT = sem("pe_upT"), sem("act_upT"), sem("dve_upT")
        dve_cnt, pe_rank, dve_hot, pe_inv, dve_idx = (sem(n) for n in ("dve_cnt", "pe_rank", "dve_hot", "pe_inv", "dve_idx"))
        pe_xg, dve_xg, pe_up, act_gl, dve_h, pe_hT, act_hT, pe_y1, dve_y1 = (
            sem(n) for n in ("pe_xg", "dve_xg", "pe_up", "act_gl", "dve_h", "pe_hT", "act_hT", "pe_y1", "dve_y1"))
        xn_stored = sem("xn_stored")
        gathered = [sem("gathered0"), sem("gathered1")]
        scattered = [sem("scattered0"), sem("scattered1")]
        y_loaded = [sem(f"y_loaded{b}") for b in range(NB)]
        dve_out = sem("dve_out")

        x_dram = A["x"].rearrange("b (i p) d -> b p i d", p=P)
        out_dram = out.rearrange("b (i p) d -> b p i d", p=P)
        mask_dram = A["mask_BxSxS2_ik0"].rearrange("b (i p) k -> b p i k", p=P)

        def row(name):
            return A[name].rearrange("(a n) -> a n", a=1)

        def col(name):
            return A[name].rearrange("(n a) -> n a", a=1)

        def everywhere(name, n=P):
            return A[name].partition_broadcast(n)

        block = ctx.enter_context(nc.Block())

        N_SMALL = 14
        N_FM = 2
        N_W = 9

        @block.sync
        def _(sp):
            sp.dma_start(ctx_tok[:, :, :], A["ctx_1024"].rearrange("b k d -> k b d")).then_inc(ld_ctx, 16)
            sp.dma_start(fm[:, 0:HD], A["L0_xattn_fm_w"]).then_inc(ld_fm, 16)
            sp.dma_start(fm[:, HD:HD + 1], col("L0_xattn_fm_b")).then_inc(ld_fm, 16)
            for b in range(NB):
                sp.dma_start(x[:, b, :, :], x_dram[b]).then_inc(ld_x[b], 16)
            for n, name in enumerate(("Wq", "Wk", "Wv", "Wo")):
                sp.dma_start(wnat[:, n, :], A["L1_xattn_" + name]).then_inc(ld_w, 16)
            for n, name in enumerate(("bq", "bk", "bv")):
                sp.dma_start(bqkv[:, n:n + 1], col("L1_xattn_" + name)).then_inc(ld_w, 16)
            sp.dma_start(fcn[:, :, :], A["L0_xattn_fc_w"].rearrange("n (a f) -> n a f", a=2)).then_inc(ld_w, 16)
            sp.dma_start(gate1n[:, :], A["L1_ffn_gate_w"]).then_inc(ld_w, 16)
            for n, name in enumerate(("L0_xattn_fc_b", "L0_ffn_bs2", "L1_xattn_bo")):
                sp.dma_start(biases[:, n, :], everywhere(name)).then_inc(ld_small, 16)
            sp.dma_start(W1[:, :].rearrange("d (e h) -> d e h", e=E0), A["L0_ffn_W1"].rearrange("e d h -> d e h")).then_inc(ld_small, 16)
            sp.dma_start(Ws1[:, :], A["L0_ffn_Ws1"]).then_inc(ld_small, 16)
            sp.dma_start(gate0[:, :], A["L0_ffn_gate_W"]).then_inc(ld_small, 16)
            sp.dma_start(W2[:, :, :], A["L0_ffn_W2"].rearrange("(c a) h d -> (a h) c d", a=2)).then_inc(ld_small, 16)
            sp.dma_start(Ws2[:, :], A["L0_ffn_Ws2"]).then_inc(ld_small, 16)
            sp.dma_start(b1[:, :], A["L0_ffn_b1"].rearrange("(c a) h -> (a h) c", a=2),
                         allow_slow_non_contiguous=True).then_inc(ld_small, 16)
            sp.dma_start(bs1[:, :], col("L0_ffn_bs1")).then_inc(ld_small, 16)
            for t in range(3):
                sp.dma_start(b2[E0 * t:E0 * t + E0, :], A["L0_ffn_b2"]).then_inc(ld_small, 16)
            sp.dma_start(route_scale[:, :], A["L0_ffn_route_scale"].partition_broadcast(P)).then_inc(ld_small, 16)
            for b in range(NB):
                sp.dma_start(mask_i[:, b, :].rearrange("p (i k) -> p i k", i=NI), mask_dram[b]).then_inc(ld_mask, 16)
            sp.wait_ge(pe_fc, NB)
            sp.wait_ge(dve_on, NB * NI)
            sp.wait_ge(act_onT, NB * NI)
            sp.wait_ge(pool_mask, 3)
            for e in range(E1):
                if e >= WR:
                    sp.wait_ge(pe_upT, 3 * (e - WR + 1))
                sp.dma_start(upn[:, e % WR, :, :], A["L1_ffn_gate_up_w"][e].rearrange("(c f) h -> f c h", f=P)).then_inc(ld_up[e], 16)
                sp.dma_start(dnn[:, e % WR, :], A["L1_ffn_down_w"][e]).then_inc(ld_dn[e], 16)
            for b in range(NB):
                sp.wait_ge(dve_xn, (3 * NB + b + 1) * NI)
                sp.dma_start(xn_dram[b * SEQ:(b + 1) * SEQ, :].rearrange("(i p) d -> p i d", p=P), xn[:, b, :, :]).then_inc(xn_stored, 16)
            for s in range(2):
                sp.wait_ge(scattered[s], 16 * ((NBLK - s + 1) // 2))
            for b in range(NB):
                if b >= 2:
                    sp.wait_ge(dve_out, b - 1)
                for c in range(CH):
                    sp.dma_start(yc[:, b % 2, c, :, :],
                                 y_dram[c * ROWS + b * SEQ:c * ROWS + (b + 1) * SEQ, :].rearrange("(i p) d -> p i d", p=P))\
                        .then_inc(y_loaded[b], 16)
            for b in range(NB):
                sp.wait_ge(dve_out, b + 1)
                sp.dma_start(out_dram[b], x[:, b, :, :]).then_inc(stored, 16)
            sp.wait_ge(stored, 16 * NB)


        def wide(ap, *shape):
            return ap.to_broadcast(list(shape))

        @block.gpsimd
        def _(g):
            link = [0]

            def ordered(ins):
                link[0] += 1
                ins.then_inc(pool_const, 1)
                g.wait_ge(pool_const, link[0])

            def band(t, pattern, mult, width, base=0):
                ordered(g.affine_select(out=t, in_=t, compare_op=ALU.is_ge, fill=0.0, base=base,
                                        pattern=pattern, channel_multiplier=mult))
                ordered(g.affine_select(out=t, in_=t, compare_op=ALU.is_ge, fill=0.0, base=width - 1 - base,
                                        pattern=[[-s, n] for s, n in pattern], channel_multiplier=-mult))

            def layernorm_rstd(k):
                for b in range(NB):
                    g.wait_ge(dve_mv, k * NB + b + 1)
                    ordered(g.tensor_scalar(rstd[:, b, :], mv[:, b, :, 1], EPS, None, ALU.add))
                    g.tensor_tensor(rstd[:, b, :], rstd[:, b, :], neghalf[:, :], ALU.pow).then_inc(pool_rstd, 1)

            def add_bias(k):
                for b in range(NB):
                    if k == 0:
                        g.wait_ge(ld_x[b], 16)
                        g.wait_ge(ld_small, 16 * N_SMALL)
                    else:
                        g.wait_ge(dve_x, (k - 1) * NB + b + 1)
                    g.tensor_tensor(xb[:, b, :, :], x[:, b, :, :], wide(biases[:, k:k + 1, :], P, NI, D), ALU.add)\
                        .then_inc(pool_xb, 1)

            ordered(g.memset(ident[:, :], 1.0))
            band(ident[:, :], [[-1, P]], 1, 1)
            g.tensor_copy(identb[:, :], ident[:, :]).then_inc(pool_ident, 1)
            g.tensor_copy(identr[:, :], ident[:, :]).then_inc(pool_ident, 1)
            ordered(g.memset(mask16[:, 0, :], 1.0))
            band(mask16[:, 0, :], [[-HD, HEADS]], 1, HD)
            ordered(g.memset(maskK[:, :], 1.0))
            band(maskK[:, :], [[-FD, HH]], 1, FD)
            ordered(g.memset(isgn[:, :, 0, :], 1.0))
            band(isgn[:, :, 0, :], [[0, HH], [-1, HD]], 1, 1)
            g.tensor_scalar(isgn[:, :, 1, :], isgn[:, :, 0, :], -1.0, None, ALU.mult).then_inc(pool_mask, 1)
            g.tensor_scalar(mask16[:, 1, :], mask16[:, 0, :], -1.0, None, ALU.mult).then_inc(pool_mask, 1)
            ordered(g.memset(neghalf[:, :], -0.5))
            layernorm_rstd(0)
            ordered(g.memset(ind[:, :, :], 1.0))
            band(ind[:, :, :], [[P, NC], [-KEYS, HH]], 1, KEYS)
            ordered(g.memset(indw[:, :, :, :, :], 0.0))
            for half in range(2):
                for part in range(3):
                    g.tensor_copy(indw[:, half, :, part, half * HH:half * HH + HH], ind[:, :, :]).then_inc(pool_ind, 1)
            g.tensor_copy(Vx[:, :, :, :, FD],
                          wide(ind[:, :, :].unsqueeze(1), P, NB * 2, NC, HH)).then_inc(pool_ind, 1)
            for b in range(NB):
                for half in range(2):
                    if b == half == 0:
                        g.wait_ge(dve_kf, 4)
                    g.tensor_tensor(kblo[:, b, half, :].bitcast(F32R).rearrange("p (h k) -> p h k", h=HH),
                                    wide(kflo[:, half, b * KEYS:(b + 1) * KEYS].bitcast(F32).unsqueeze(1), P, HH, KEYS),
                                    wide(maskK[:, :].unsqueeze(2), P, HH, KEYS), ALU.mult).then_inc(pool_kb, 1)
            add_bias(0)
            ordered(g.memset(ones_row[:, :], 1.0))
            ordered(g.iota(iota8[:, :, :], pattern=[[0, NI], [-1, E0]], base=E0, channel_multiplier=0,
                           allow_small_or_imprecise_dtypes=True))
            for part in range(3):
                ordered(g.memset(selGt[:, part, :], 1.0))
                band(selGt[:, part, :], [[1, 4 * P]], -H0, H0, base=H0 * E0 * part)
            ordered(g.tensor_tensor(selGt[:, 0, :], selGt[:, 0, :], selGt[:, 1, :], ALU.add))
            ordered(g.tensor_tensor(selGt[:, 0, :], selGt[:, 0, :], selGt[:, 2, :], ALU.add))
            ordered(g.tensor_copy(selG[:, :, :].rearrange("q c r -> q (c r)"), selGt[:, 0, :]))
            g.wait_ge(ld_small, 16 * N_SMALL)
            ordered(g.tensor_copy(b2s[:, 0, :], b2[:, :]))
            ordered(g.tensor_tensor(b2r[:, :], b2[:, :], b2s[:, 0, :], ALU.subtract))
            ordered(g.tensor_copy(b2s[:, 1, :], b2r[:, :]))
            ordered(g.tensor_tensor(b2r[:, :], b2r[:, :], b2s[:, 1, :], ALU.subtract))
            ordered(g.tensor_copy(b2s[:, 2, :], b2r[:, :]))
            g.wait_ge(ld_mask, 16 * NB)
            ordered(g.tensor_scalar(maskb[:, :, :], mask_i[:, :, :], 0.0, -BIG, ALU.is_equal, ALU.mult))
            g.memset(Vo[:, :, D:D + 1], 1.0).then_inc(pool_mask, 1)
            layernorm_rstd(1)
            add_bias(1)
            layernorm_rstd(2)
            add_bias(2)
            layernorm_rstd(3)
            def const(t, value=None, **iota):
                if value is not None:
                    ordered(g.memset(t, value))
                else:
                    ordered(g.iota(t, allow_small_or_imprecise_dtypes=True, **iota))

            const(lower[:, :], 1.0)
            ordered(g.affine_select(out=lower[:, :], in_=lower[:, :], compare_op=ALU.is_gt, fill=0.0, base=0,
                                    pattern=[[1, P]], channel_multiplier=-1))
            const(onesb[:, :], 1.0)
            const(cnt[:, NT, :], 0.0)
            const(before[:, :, :], 1.0)
            ordered(g.affine_select(out=before[:, :, :], in_=before[:, :, :], compare_op=ALU.is_gt, fill=0.0, base=0,
                                    pattern=[[1, E1], [-1, E1]], channel_multiplier=0))
            const(iota_n[:, :, :], pattern=[[0, E1], [P, NT]], base=0, channel_multiplier=0)
            const(iota_k[:, :], pattern=[[1, NBLK]], base=0, channel_multiplier=0)
            const(iota_r[:, :], pattern=[[1, P]], base=0, channel_multiplier=0)
            const(tile_q[:, :], pattern=[[1, CH * NT]], base=0, channel_multiplier=0)
            const(p_one[:, :], pattern=[[0, 1]], base=1, channel_multiplier=1)
            g.iota(pad_row[:, :], pattern=[[P, NBLK]], base=CH * ROWS + 1, channel_multiplier=1,
                   allow_small_or_imprecise_dtypes=True).then_inc(pool_mask, 1)

            def gather(k):
                if k >= 2:
                    g.wait_ge(pe_xg, k - 1)
                g.indirect_dma_start(xg[:, k % 2, :], None, xn_dram,
                                     bass.IndirectOffsetOnAxis(ap=src_row[:, k:k + 1], axis=0)).then_inc(gathered[k % 2], 16)

            def scatter(k):
                g.wait_ge(dve_y1, k + 1)
                g.indirect_dma_start(y_dram, bass.IndirectOffsetOnAxis(ap=dst_row[:, k:k + 1], axis=0),
                                     yb[:, k % 2, :], None).then_inc(scattered[k % 2], 16)

            g.wait_ge(dve_idx, 1)
            g.wait_ge(xn_stored, 16 * NB)
            for k in range(NBLK):
                gather(k)
                if k >= 4:
                    scatter(k - 4)
            for k in range(NBLK - 4, NBLK):
                scatter(k)

        @block.vector
        def _(v):
            link = [0]

            def step(ins):
                link[0] += 1
                ins.then_inc(dve_link, 1)

            def settle():
                v.wait_ge(dve_link, link[0])

            def layernorm_stats(b):
                for i in range(NI):
                    step(v.bn_stats(stats[:, b, i, :], x[:, b, i, :]))
                settle()
                for i in range(NI):
                    ins = v.bn_aggr(mv[:, b, i, :], stats[:, b, i, :])
                    if i < NI - 1:
                        step(ins)
                settle()
                ins.then_inc(dve_mv, 1)

            def layernorm_apply(k, b):
                v.wait_ge(pool_rstd, k * NB + b + 1)
                for i in range(NI):
                    v.tensor_scalar(xn[:, b, i, :], x[:, b, i, :], mv[:, b, i, 0:1], rstd[:, b, i:i + 1],
                                    ALU.subtract, ALU.mult).then_inc(dve_xn, 1)

            def route(b, scores, sem_done):
                s, a, t = r_s[:, b % 2], r_a[:, b % 2], r_b[:, b % 2]
                o1, o2, m = r_o1[:, b % 2], r_o2[:, b % 2], r_m[:, b % 2]

                def w(i):
                    return wide(m[:, i, :].unsqueeze(2), P, NI, E0)

                def first_best(src, best, onehot, i):
                    step(v.tensor_reduce(m[:, i, :], src, AX.X, ALU.max))
                    settle()
                    step(v.tensor_tensor(t, src, w(i), ALU.is_equal))
                    settle()
                    step(v.tensor_tensor(t, t, iota8[:, :, :], ALU.mult))
                    settle()
                    step(v.tensor_reduce(m[:, i + 1, :], t, AX.X, ALU.max))
                    settle()
                    step(v.tensor_tensor(onehot, t, w(i + 1), ALU.is_equal))
                    settle()

                first_best(s, None, o1, 0)
                step(v.scalar_tensor_tensor(out=a, in0=o1, scalar=-BIG, in1=s, op0=ALU.mult, op1=ALU.add))
                settle()
                first_best(a, None, o2, 2)
                step(v.tensor_tensor(m[:, 4, :], m[:, 0, :], m[:, 2, :], ALU.add))
                settle()
                step(v.reciprocal(m[:, 5, :], m[:, 4, :]))
                settle()
                step(v.tensor_tensor(m[:, 0, :], m[:, 0, :], m[:, 5, :], ALU.mult))
                step(v.tensor_tensor(m[:, 2, :], m[:, 2, :], m[:, 5, :], ALU.mult))
                settle()

            v.wait_ge(ld_fm, 16 * N_FM)
            v.tensor_copy(fmrep[:, :, :], wide(fm[:, 0:HD].unsqueeze(1), HD, HEADS, HD)).then_inc(dve_c, 1)
            v.wait_ge(pe_ctxT, 1)
            v.tensor_copy(ctxT[:, :], bank[0][:, 0:NB * KEYS]).then_inc(dve_ctxT, 1)
            v.wait_ge(pe_fm, 1)
            v.tensor_copy(fmT[:, :], bank[1][:, 0:HD + 1]).then_inc(dve_fmT, 1)
            v.wait_ge(dve_fmT, 1)
            v.wait_ge(pool_mask, 2)
            for half in range(2):
                for s in range(2):
                    v.tensor_tensor(Wz[:, half, :, s, :], wide(fmT[:, 0:HD].unsqueeze(1), P, HH, HD),
                                    wide(mask16[:, s, half * HH:half * HH + HH].unsqueeze(2), P, HH, HD),
                                    ALU.mult).then_inc(dve_Wz, 1)
            for b in range(NB):
                v.wait_ge(ld_x[b], 16)
                layernorm_stats(b)
            for b in range(NB):
                layernorm_apply(0, b)
            v.wait_ge(act_kf, 2)
            for half in range(2):
                v.tensor_copy(kfhi[:, half, :], kf[:, half, :]).then_inc(dve_kf, 1)
            v.wait_ge(dve_kf, 2)
            for half in range(2):
                v.tensor_tensor(kflo[:, half, :], kf[:, half, :], kfhi[:, half, :].bitcast(F32), ALU.subtract)\
                    .then_inc(dve_kf, 1)
            for b in range(NB):
                for half in range(2):
                    v.tensor_tensor(kbhi[:, b, half, :].rearrange("p (h k) -> p h k", h=HH),
                                    wide(kfhi[:, half, b * KEYS:(b + 1) * KEYS].bitcast(F32).unsqueeze(1), P, HH, KEYS),
                                    wide(maskK[:, :].unsqueeze(2), P, HH, KEYS), ALU.mult).then_inc(dve_kb, 1)
                for half in range(2):
                    n = 2 * b + half
                    v.wait_ge(act_q, n + 1)
                    v.tensor_copy(qhi[:, b, half, :], qf[:, half, :]).then_inc(dve_q, 1)
                    v.wait_ge(dve_q, 2 * n + 1)
                    v.tensor_tensor(qlo[:, b, half, :], qf[:, half, :], qhi[:, b, half, :].bitcast(F32), ALU.subtract)\
                        .then_inc(dve_q, 1)
            for half in range(2):
                v.wait_ge(pe_kz, 3 + half)
                v.tensor_copy(sel[:, half, :], bank[6 + half].bitcast(BF16)[0:3 * HEADS, 0:NC * P]).then_inc(dve_Wz, 1)
            v.wait_ge(pe_wT, 2)
            v.tensor_copy(wT[:, :, :], bank[0][:, 0:3 * D].rearrange("p (n d) -> p n d", n=3)).then_inc(dve_wT, 1)
            v.tensor_copy(fcT[:, :, :], bank[1][:, 0:2 * D].rearrange("p (n d) -> p n d", n=2)).then_inc(dve_wT, 1)
            v.tensor_copy(gate1[:, :], bank[1][:, 2 * D:2 * D + E1]).then_inc(dve_wT, 1)
            v.wait_ge(pe_kv, 2)
            v.wait_ge(ld_w, 16 * N_W)
            v.tensor_scalar(KT[:, :], bank[2][:, 0:NB * KEYS], bqkv[:, 1:2], None, ALU.add).then_inc(dve_kv, 1)
            v.tensor_scalar(VT[:, :], bank[3][:, 0:NB * KEYS], bqkv[:, 2:3], None, ALU.add).then_inc(dve_kv, 1)
            v.wait_ge(pe_ak, 3)
            v.tensor_copy(keyA[:, :], bank[0][:, 0:NB * KEYS]).then_inc(dve_ak, 1)
            v.tensor_copy(keyc[:, :], bank[1][0:1, 0:NB * KEYS]).then_inc(dve_ak, 1)
            v.tensor_copy(Vo[:, :, 0:D], bank[2][0:KEYS, :].rearrange("k (b d) -> k b d", b=NB)).then_inc(dve_ak, 1)

            def maxima(b):
                for j in range(2 * NI):
                    i, half = divmod(j, 2)
                    n = b * 2 * NI + j
                    v.wait_ge(pe_max, n + 1)
                    pair = 4 + 2 * (n % 2)
                    v.tensor_reduce(mx[:, b % 2, i, half * HH:half * HH + HH].rearrange("p (a h) -> p a h", a=2),
                                    ps[:, pair:pair + 2, 0:HK // 2].rearrange("p a (h k) -> p a h k", h=HH // 2),
                                    AX.X, ALU.max).then_inc(dve_max, 1)
                v.wait_ge(dve_max, (b + 1) * 2 * NI)
                if b >= 2:
                    v.wait_ge(pe_nmT, b - 1)
                m, r = mx[:, b % 2], nmr[:, b % 2]
                step(v.tensor_scalar(nm[:, b % 2, :, 0, :], m, -1.0, None, ALU.mult))
                settle()
                step(v.scalar_tensor_tensor(out=r, in0=m, scalar=-1.0, in1=nm[:, b % 2, :, 0, :], op0=ALU.mult, op1=ALU.subtract))
                settle()
                step(v.tensor_copy(nm[:, b % 2, :, 1, :], r))
                settle()
                v.tensor_tensor(nm[:, b % 2, :, 2, :], r, nm[:, b % 2, :, 1, :], ALU.subtract).then_inc(dve_nm, 1)

            maxima(0)
            for b in range(NB + 1):
                if b >= 1:
                    for i in range(NI):
                        n = (b - 1) * NI + i
                        v.wait_ge(pe_av, n + 1)
                        if n >= NI:
                            v.wait_ge(pe_onT, n - NI + 1)
                        av = bank[4 + i][:, 0:HEADS * (FD + 1)].rearrange("p (h f) -> p h f", h=HEADS)
                        step(v.reciprocal(rec[:, n % 2, :], av[:, :, FD]))
                        settle()
                        v.tensor_tensor(on[:, i, :].rearrange("p (h f) -> p h f", h=HEADS), av[:, :, 0:FD],
                                        wide(rec[:, n % 2, :].unsqueeze(2), P, HEADS, FD), ALU.mult).then_inc(dve_on, 1)
                if b + 1 < NB:
                    maxima(b + 1)
                if b >= 1:
                    v.wait_ge(pe_fc, b)
                    v.wait_ge(pool_xb, b)
                    v.tensor_tensor(x[:, b - 1, :, :].rearrange("p i d -> p (i d)"), bank[3],
                                    xb[:, b - 1, :, :].rearrange("p i d -> p (i d)"), ALU.add).then_inc(dve_x, 1)
                    v.wait_ge(dve_x, b)
                    layernorm_stats(b - 1)
                if b >= 2:
                    layernorm_apply(1, b - 2)
            layernorm_apply(1, NB - 1)

            for b in range(NB):
                v.wait_ge(act_lg, b + 1)
                s = r_s[:, b % 2]
                step(v.tensor_scalar(s, s, 1.0, None, ALU.add))
                settle()
                step(v.reciprocal(s, s))
                settle()
                step(v.tensor_scalar(s, s, route_scale[:, 0:1], None, ALU.mult))
                settle()
                route(b, s, None)
                o1, o2, r, m = r_o1[:, b % 2], r_o2[:, b % 2], g3r[:, b], r_m[:, b % 2]
                step(v.tensor_tensor(o1, o1, wide(m[:, 0, :].unsqueeze(2), P, NI, E0), ALU.mult))
                step(v.tensor_tensor(o2, o2, wide(m[:, 2, :].unsqueeze(2), P, NI, E0), ALU.mult))
                settle()
                step(v.tensor_tensor(r, o1, o2, ALU.add))
                settle()
                step(v.tensor_copy(g3[:, b, :, 0, :], r))
                settle()
                step(v.tensor_tensor(r, r, g3[:, b, :, 0, :], ALU.subtract))
                settle()
                step(v.tensor_copy(g3[:, b, :, 1, :], r))
                settle()
                v.tensor_tensor(g3[:, b, :, 2, :], r, g3[:, b, :, 1, :], ALU.subtract).then_inc(dve_g, 1)
            for b in range(NB + 1):
                if b < NB:
                    v.wait_ge(pe_gT, b + 1)
                    v.tensor_copy(gT3[:, b, :], bank[0].bitcast(BF16)[0:3 * E0, 0:SEQ]).then_inc(dve_gT, 1)
                    if b >= 2:
                        v.wait_ge(pe_y, b - 1)
                    for c in range(4):
                        n = 4 * b + c
                        v.wait_ge(act_h, 5 * b + c + 1)
                        v.wait_ge(pe_G, n + 1)
                        v.tensor_tensor(hg[:, b % 2, c, :], hraw[:, n % 2, :], bank[3 + n % 2], ALU.mult).then_inc(dve_hg, 1)
                if b >= 1:
                    v.wait_ge(pe_y, b)
                    v.wait_ge(pool_xb, NB + b)
                    v.tensor_tensor(x[:, b - 1, :, :].rearrange("p i d -> p (i d)"), bank[5 + (b - 1) % 2],
                                    xb[:, b - 1, :, :].rearrange("p i d -> p (i d)"), ALU.add).then_inc(dve_x, 1)
                    v.wait_ge(dve_x, NB + b)
                    layernorm_stats(b - 1)
                if b >= 2:
                    layernorm_apply(2, b - 2)
            layernorm_apply(2, NB - 1)

            for b in range(NB):
                for e in (2 * b, 2 * b + 1):
                    for c in range(2):
                        n = 2 * e + c
                        cols = slice(n * SEQ, (n + 1) * SEQ)
                        v.wait_ge(act_upT, 3 * e + c + 1)
                        v.tensor_tensor(uplo[:, cols], bank[2 + c], uphi[:, cols].bitcast(F32), ALU.subtract).then_inc(dve_upT, 1)
                v.wait_ge(pe_s1, b + 1)
                if b >= 2:
                    v.wait_ge(act_s1, b - 1)
                s = sc[:, b % 2]
                step(v.tensor_tensor(s, bank[4 + b % 2][:, 0:NI * KEYS].rearrange("p (i k) -> p i k", i=NI),
                                     maskb[:, b, :].rearrange("p (i k) -> p i k", i=NI), ALU.add))
                settle()
                step(v.tensor_reduce(scm[:, b % 2, :], s, AX.X, ALU.max))
                settle()
                v.scalar_tensor_tensor(out=s, in0=wide(scm[:, b % 2, :].unsqueeze(2), P, NI, KEYS), scalar=-BIG / 2,
                                       in1=s, op0=ALU.max, op1=ALU.subtract).then_inc(dve_s1, 1)
            for b in range(NB):
                for pair in range(2):
                    v.wait_ge(pe_o1, 2 * b + pair + 1)
                    o = bank[6 + pair][:, 0:2 * (D + 1)].rearrange("p (i d) -> p i d", i=2)
                    step(v.reciprocal(srec[:, b % 2, 2 * pair:2 * pair + 2], o[:, :, D]))
                    settle()
                    v.wait_ge(pool_xb, 2 * NB + b + 1)
                    for i in range(2):
                        t = 2 * pair + i
                        ins = v.scalar_tensor_tensor(out=x[:, b, t, :], in0=o[:, i, 0:D], scalar=srec[:, b % 2, t:t + 1],
                                                     in1=xb[:, b, t, :], op0=ALU.mult, op1=ALU.add)
                        if t < NI - 1:
                            step(ins)
                ins.then_inc(dve_x, 1)
                settle()
                v.wait_ge(dve_x, 2 * NB + b + 1)
                layernorm_stats(b)
            for b in range(NB):
                layernorm_apply(3, b)

            for b in range(NB):
                v.wait_ge(pe_lg, NB + b + 1)
                s, t, m = r_s[:, b % 2], r_a[:, b % 2], r_m[:, b % 2]
                lg = bank[4 + b][:, 0:NI * E1].rearrange("p (i e) -> p i e", i=NI)
                step(v.tensor_reduce(m[:, 0, :], lg, AX.X, ALU.max))
                settle()
                v.tensor_tensor(t, lg, wide(m[:, 0, :].unsqueeze(2), P, NI, E1), ALU.subtract).then_inc(dve_g, 1)
                v.wait_ge(act_lg, NB + b + 1)
                route(b, s, None)
                o1, o2, tiles = r_o1[:, b % 2], r_o2[:, b % 2], slice(b * NI, (b + 1) * NI)
                step(v.tensor_copy(onehot[:, 0, tiles, :], o1))
                step(v.tensor_copy(onehot[:, 1, tiles, :], o2))
                step(v.tensor_copy(wgt[:, 0, tiles], m[:, 0, :]))
                step(v.tensor_copy(wgt[:, 1, tiles], m[:, 2, :]))
                v.tensor_tensor(cnt[:, tiles, :], o1, o2, ALU.add).then_inc(dve_cnt, 1)
            rank = bank[6][:, 0:(NT + 1) * E1].rearrange("p (t e) -> p t e", e=E1)
            v.wait_ge(pool_mask, 4)
            v.wait_ge(pe_rank, 1)
            step(v.tensor_copy(m_n[:, :], rank[:, NT, :]))
            settle()
            step(v.tensor_tensor(m_cmp[:, :, :], wide(m_n[:, :].unsqueeze(2), P, E1, NT), iota_n[:, :, :], ALU.is_gt))
            settle()
            step(v.tensor_reduce(m_nb[:, :], m_cmp[:, :, :], AX.X, ALU.add))
            settle()
            step(v.tensor_tensor(m_lt[:, :, :], wide(m_nb[:, :].unsqueeze(1), P, E1, E1), before[:, :, :], ALU.mult))
            settle()
            step(v.tensor_reduce(m_bb[:, :], m_lt[:, :, :], AX.X, ALU.add))
            settle()
            step(v.tensor_tensor(m_ce[:, :], m_bb[:, :], m_nb[:, :], ALU.add))
            step(v.scalar_tensor_tensor(out=m_at[:, :, :], in0=wide(m_bb[:, :].unsqueeze(1), P, NT, E1), scalar=float(P),
                                        in1=rank[:, 0:NT, :], op0=ALU.mult, op1=ALU.add))
            settle()
            step(v.tensor_tensor(m_pe[:, :, :, :], onehot[:, :, :, :], wide(m_at[:, :, :].unsqueeze(1), P, CH, NT, E1), ALU.mult))
            settle()
            step(v.tensor_reduce(m_pos[:, :].rearrange("p (c t) -> p c t", c=CH), m_pe[:, :, :, :], AX.X, ALU.add))
            settle()
            step(v.tensor_copy(m_posi[:, 0, :], m_pos[:, :]))
            settle()
            step(v.tensor_scalar(m_posi[:, 1, :], m_posi[:, 0, :], P - 1, None, ALU.bitwise_and))
            step(v.tensor_scalar(m_posi[:, 2, :], m_posi[:, 0, :], 7, None, ALU.logical_shift_right))
            settle()
            step(v.tensor_copy(m_posf[:, :, :], m_posi[:, 1:3, :]))
            settle()
            step(v.tensor_tensor(b_hot[:, :, :], wide(m_posf[:, 1, :].unsqueeze(2), P, CH * NT, NBLK),
                                 wide(iota_k[:, :].unsqueeze(1), P, CH * NT, NBLK), ALU.is_equal))
            for n in range(CH * NT):
                step(v.tensor_scalar(r_hot[:, n, :], iota_r[:, :], m_posf[:, 0, n:n + 1], None, ALU.is_equal))
            settle()
            step(v.tensor_tensor(b_val[:, :, 0, :], b_hot[:, :, :], wide(tile_q[:, :].unsqueeze(2), P, CH * NT, NBLK), ALU.mult))
            step(v.tensor_scalar(b_val[:, :, 1, :], b_hot[:, :, :], p_one[:, 0:1], None, ALU.mult))
            settle()
            step(v.tensor_tensor(m_k[:, :, :], wide(m_ce[0:1, :].unsqueeze(1), 1, NBLK, E1),
                                 wide(iota_k[0:1, :].unsqueeze(2), 1, NBLK, E1), ALU.is_le))
            settle()
            step(v.tensor_reduce(m_kf[:, :], m_k[:, :, :], AX.X, ALU.add))
            settle()
            step(v.tensor_scalar(m_kf[:, :], m_kf[:, :], float(E1 - 1), None, ALU.min))
            settle()
            step(v.tensor_copy(blk_e[:, :], m_kf[:, :]))
            body = slice(LOOP0, LOOP1)
            step(v.tensor_copy(m_pack[:, body], m_kf[:, LOOP0 - 2:LOOP1 - 2]))
            for j in range(1, UNROLL + 2):
                settle()
                step(v.scalar_tensor_tensor(out=m_pack[:, body], in0=m_kf[:, LOOP0 - 2 + j:LOOP1 - 2 + j],
                                            scalar=float(E1 ** j), in1=m_pack[:, body], op0=ALU.mult, op1=ALU.add))
            settle()
            v.tensor_copy(blk_es[:, body], m_pack[:, body]).then_inc(dve_hot, 1)
            v.wait_ge(pe_inv, 1)
            step(v.tensor_copy(inv[:, :, :], bank[7][:, 0:2 * NBLK].rearrange("p (a k) -> p a k", a=2)))
            settle()
            q, u, row, t0, t1 = inv[:, 0, :], inv[:, 1, :], row_f[:, 0, :], row_f[:, 1, :], row_f[:, 2, :]
            step(v.scalar_tensor_tensor(out=row, in0=q, scalar=float(P), in1=u, op0=ALU.mult, op1=ALU.add))
            step(v.tensor_scalar(t0, q, float(NT), -float(ROWS), ALU.is_ge, ALU.mult))
            step(v.scalar_tensor_tensor(out=t1, in0=u, scalar=0.0, in1=pad_row[:, :], op0=ALU.is_equal, op1=ALU.mult))
            settle()
            step(v.scalar_tensor_tensor(out=t0, in0=row, scalar=-1.0, in1=t0, op0=ALU.add, op1=ALU.add))
            step(v.scalar_tensor_tensor(out=t1, in0=row, scalar=-1.0, in1=t1, op0=ALU.add, op1=ALU.add))
            settle()
            step(v.tensor_scalar(src_row[:, :], t0, 0.0, None, ALU.max))
            settle()
            v.tensor_copy(dst_row[:, :], t1).then_inc(dve_idx, 1)

            def split_xg(k, s):
                v.wait_ge(pe_xg, k + 1)
                v.tensor_copy(xghi[:, s, :], bank[7][:, 0:P]).then_inc(dve_xg, 1)
                v.wait_ge(dve_xg, 2 * k + 1)
                v.tensor_tensor(xglo[:, s, :], bank[7][:, 0:P], xghi[:, s, :].bitcast(F32), ALU.subtract).then_inc(dve_xg, 1)

            def gate_up(k, s, first=False):
                v.wait_ge(act_gl, k + 1)
                if not first:
                    v.wait_ge(pe_hT, k - 1)
                v.tensor_tensor(hh[:, s, :], gl[:, s, :], bank[2 + s], ALU.mult).then_inc(dve_h, 1)

            def copy_y(k, s, first=False):
                v.wait_ge(pe_y1, k + 1)
                if not first:
                    v.wait_ge(scattered[s], 8 * k - 8 * s)
                v.tensor_copy(yb[:, s, :], bank[6][:, 0:D]).then_inc(dve_y1, 1)

            def block_step(k, s, first=False):
                split_xg(k + 1, 1 - s)
                copy_y(k - 2, s, first)
                gate_up(k, s)

            split_xg(0, 0)
            for k in range(2):
                split_xg(k + 1, 1 - k)
                gate_up(k, k, first=True)
            for k in range(2, LOOP0):
                block_step(k, k % 2, first=True)
            with v.Fori(LOOP0, LOOP1, UNROLL) as k0:
                for j in range(UNROLL):
                    block_step(k0 + j, j % 2)
            for k in range(LOOP1, NBLK - 1):
                block_step(k, k % 2)
            gate_up(NBLK - 1, (NBLK - 1) % 2)
            for k in range(NBLK - 3, NBLK):
                copy_y(k, k % 2)
            for b in range(NB):
                v.wait_ge(y_loaded[b], 32)
                for c in range(CH):
                    for i in range(NI):
                        at = yc[:, b % 2, c, i, :]
                        ins = v.scalar_tensor_tensor(out=x[:, b, i, :], in0=at, scalar=wgt[:, c, b * NI + i:b * NI + i + 1],
                                                     in1=x[:, b, i, :], op0=ALU.mult, op1=ALU.add)
                        if c < CH - 1 or i < NI - 1:
                            step(ins)
                    if c < CH - 1:
                        settle()
                ins.then_inc(dve_out, 1)

        @block.scalar
        def _(s):
            def copy_xT(k, b, src):
                s.wait_ge(pe_xT, k * NB + b + 1)
                s.activation(xnT[:, b, :], src, ACT.Copy).then_inc(xT_ready, 1)

            for half in range(2):
                s.wait_ge(pe_kz, half + 1)
                s.wait_ge(dve_fmT, 1)
                s.activation(kf[:, half, :], bank[2 + half][:, 0:NB * KEYS], ACT.Exp, bias=fmT[:, HD:HD + 1]).then_inc(act_kf, 1)
            for b in range(NB):
                copy_xT(0, b, bank[4 + b % 2])
                for half in range(2):
                    n = 2 * b + half
                    s.wait_ge(pe_z, n + 1)
                    if b >= 1:
                        s.wait_ge(dve_q, 2 * n - 2)
                    s.activation(qf[:, half, :], bank[half], ACT.Exp, bias=fmT[:, HD:HD + 1]).then_inc(act_q, 1)
            for n in range(2 * NB):
                s.wait_ge(pe_vt, n + 1)
                if n == 0:
                    s.wait_ge(pool_ind, 7)
                for c0, c1, bk in ((0, 4, 2), (4, NC, 3)):
                    rows = chunk_rows(c1 - 1)
                    s.activation(Vx[0:rows, n, c0:c1, :, 0:FD],
                                 bank[bk][0:rows, 0:(c1 - c0) * P].rearrange("r (c h f) -> r c h f", h=HH, f=FD),
                                 ACT.Copy).then_inc(act_vx, 1)
            for b in range(NB + 1):
                if b < NB:
                    s.wait_ge(pe_nmT, b + 1)
                    s.activation(nmT[:, b % 2, :], bank[0].bitcast(BF16)[0:3 * HEADS, 0:SEQ], ACT.Copy).then_inc(act_nmT, 1)
                    for j in range(2 * NC):
                        n = 2 * NC * b + j
                        rows = chunk_rows(j % NC)
                        s.wait_ge(pe_sc, n + 1)
                        if b >= 1 and j == 0:
                            s.wait_ge(pe_av, NI * b)
                        s.activation(ex[0:rows, j, :], bank[1 + n % 3][0:rows, :], ACT.Exp, scale=SCALE).then_inc(act_ex, 1)
                if b >= 1:
                    for pair in range(2):
                        s.wait_ge(pe_onT, (b - 1) * NI + 2 * pair + 2)
                        s.activation(onT[:, 2 * pair:2 * pair + 2, :, :].rearrange("p i a t -> p (i a t)"),
                                     bank[1 + pair], ACT.Copy).then_inc(act_onT, 2)
            for b in range(NB):
                copy_xT(1, b, bank[b])
            for b in range(NB):
                s.wait_ge(pe_lg, b + 1)
                if b >= 2:
                    s.wait_ge(dve_g, b - 1)
                s.activation(r_s[:, b % 2], bank[4 + b][:, 0:NI * E0].rearrange("p (i e) -> p i e", i=NI),
                             ACT.Exp, scale=-1.0).then_inc(act_lg, 1)
            s.wait_ge(ld_small, 16 * N_SMALL)
            for b in range(NB):
                for c in range(5):
                    n = 5 * b + c
                    s.wait_ge(pe_h, n + 1)
                    if c < 4:
                        m = 4 * b + c
                        if m >= 2:
                            s.wait_ge(dve_hg, m - 1)
                        s.activation(hraw[:, m % 2, :], bank[1 + n % 2], ACT.Gelu, bias=b1[:, c:c + 1]).then_inc(act_h, 1)
                    else:
                        if b >= 2:
                            s.wait_ge(pe_y, b - 1)
                        s.activation(hs[:, b % 2, :], bank[1 + n % 2][0:H0, :], ACT.Gelu, bias=bs1[:, 0:1]).then_inc(act_h, 1)
            for b in range(NB):
                copy_xT(2, b, bank[b])

            def copy_weights(e):
                for c in range(3):
                    s.wait_ge(pe_upT, 3 * e + c + 1)
                    cols = slice((2 * e + c) * SEQ, (2 * e + c + 1) * SEQ)
                    dst = uphi[:, cols] if c < 2 else dnT[:, e * F1:(e + 1) * F1]
                    s.activation(dst, bank[2 + c] if c < 2 else bank[0], ACT.Copy).then_inc(act_upT, 1)

            for b in range(NB):
                copy_weights(2 * b)
                copy_weights(2 * b + 1)
                s.wait_ge(dve_s1, b + 1)
                s.activation(pr[:, b], sc[:, b % 2], ACT.Exp, scale=-SCALE).then_inc(act_s1, 1)
            for b in range(NB):
                s.wait_ge(pe_pT, b + 1)
                if b >= 2:
                    s.wait_ge(pe_o1, 2 * (b - 1))
                s.activation(prT[:, b % 2, :], bank[b % 2][0:KEYS, :], ACT.Copy).then_inc(act_pT, 1)
            for b in range(NB):
                copy_xT(3, b, bank[b])
            for b in range(NB):
                s.wait_ge(dve_g, NB + b + 1)
                s.activation(r_s[:, b % 2], r_a[:, b % 2], ACT.Exp).then_inc(act_lg, 1)

            def gelu(k, s_, first=False):
                s.wait_ge(pe_up, k + 1)
                if not first:
                    s.wait_ge(dve_h, k - 1)
                s.activation(gl[:, s_, :], bank[s_], ACT.Gelu).then_inc(act_gl, 1)

            def copy_hT(k, s_, first=False):
                s.wait_ge(pe_hT, k + 1)
                if not first:
                    s.wait_ge(pe_y1, k - 1)
                s.activation(hhT[:, s_, :, :].rearrange("p c t -> p (c t)"), bank[4], ACT.Copy).then_inc(act_hT, 1)

            gelu(0, 0, first=True)
            for k in range(1, LOOP0):
                gelu(k, k % 2, first=k < 2)
                copy_hT(k - 1, (k - 1) % 2, first=k < 3)
            with s.Fori(LOOP0, LOOP1, UNROLL) as k0:
                for j in range(UNROLL):
                    gelu(k0 + j, j % 2)
                    copy_hT(k0 + j - 1, 1 - j % 2)
            for k in range(LOOP1, NBLK):
                gelu(k, k % 2)
                copy_hT(k - 1, (k - 1) % 2)
            copy_hT(NBLK - 1, (NBLK - 1) % 2)

        @block.tensor
        def _(pe):
            def mm(out_, lhsT, rhs, start=True, stop=True):
                return pe.matmul(out_, lhsT, rhs, start=start, stop=stop, skip_group_check=True)

            def transpose_xn(k, b, dst):
                for i in range(NI):
                    pe.wait_ge(dve_xn, (k * NB + b) * NI + i + 1)
                    ins = pe.transpose(dst[:, i * P:(i + 1) * P], xn[:, b, i, :], ident[:, :])
                ins.then_inc(pe_xT, 1)

            pe.wait_ge(pool_ident, 2)
            pe.wait_ge(ld_ctx, 16)
            for b in range(NB):
                ins = pe.transpose(bank[0][:, b * KEYS:(b + 1) * KEYS], ctx_tok[:, b, :], ident[0:KEYS, 0:KEYS])
            ins.then_inc(pe_ctxT, 1)
            pe.wait_ge(ld_fm, 16 * N_FM)
            pe.wait_ge(pool_mask, 2)
            pe.wait_ge(dve_c, 1)
            mm(bank[1][:, 0:HD], fmrep[:, :, :].rearrange("e h d -> e (h d)"), ident[0:HD, 0:HD])
            mm(bank[1][:, HD:HD + 1], isgn[:, :, :, :].rearrange("e h s d -> e (h s d)"), fm[:, HD:HD + 1]).then_inc(pe_fm, 1)
            pe.wait_ge(dve_ctxT, 1)
            pe.wait_ge(dve_Wz, 4)
            for half in range(2):
                mm(bank[2 + half][:, 0:NB * KEYS], Wz[:, half].rearrange("p h s d -> p (h s d)"), ctxT[:, :]).then_inc(pe_kz, 1)
            for b in range(NB):
                if b >= 2:
                    pe.wait_ge(xT_ready, b - 1)
                transpose_xn(0, b, bank[4 + b % 2])
                pe.wait_ge(xT_ready, b + 1)
                for half in range(2):
                    n = 2 * b + half
                    if b >= 1:
                        pe.wait_ge(act_q, n - 1)
                    mm(bank[half], Wz[:, half].rearrange("p h s d -> p (h s d)"), xnT[:, b, :]).then_inc(pe_z, 1)
            pe.wait_ge(pool_ind, 6)
            for half in range(2):
                for c in range(NC):
                    ins = pe.transpose(bank[6 + half].bitcast(BF16)[0:3 * HEADS, c * P:(c + 1) * P],
                                       indw[:, half, c, :, :].rearrange("p a h -> p (a h)"), identb[:, :])
                ins.then_inc(pe_kz, 1)
            pe.wait_ge(act_kf, 2)
            for n in range(2 * NB):
                b, half = divmod(n, 2)
                pe.wait_ge(dve_kb, n + 1)
                pe.wait_ge(pool_kb, n + 1)
                if n >= 1:
                    pe.wait_ge(act_vx, 2 * n)
                for c in range(NC):
                    rows = chunk_rows(c)
                    bk, at = (2, c * P) if c < 4 else (3, 0)
                    mm(bank[bk][0:rows, at:at + P], kbhi[:, b, half, c * P:c * P + rows], identr[:, :], True, False)
                    ins = mm(bank[bk][0:rows, at:at + P], kblo[:, b, half, c * P:c * P + rows], identr[:, :], False, True)
                ins.then_inc(pe_vt, 1)
            pe.wait_ge(ld_w, 16 * N_W)
            pe.wait_ge(act_q, 2 * NB)
            for n in range(3):
                ins = pe.transpose(bank[0][:, n * D:(n + 1) * D], wnat[:, n + 1, :], ident[:, :])
            ins.then_inc(pe_wT, 1)
            for n in range(2):
                pe.transpose(bank[1][:, n * D:(n + 1) * D], fcn[:, n, :], ident[:, :])
            pe.transpose(bank[1][:, 2 * D:2 * D + E1], gate1n[:, :], ident[0:E1, 0:E1]).then_inc(pe_wT, 1)
            pe.wait_ge(dve_wT, 3)
            pe.wait_ge(act_vx, 4 * NB)
            for n in range(2):
                mm(bank[2 + n][:, 0:NB * KEYS], wT[:, n, :], ctxT[:, :]).then_inc(pe_kv, 1)
            pe.wait_ge(dve_kv, 2)
            mm(bank[0][:, 0:NB * KEYS], wnat[:, 0, :], KT[:, :]).then_inc(pe_ak, 1)
            mm(bank[1][0:1, 0:NB * KEYS], bqkv[:, 0:1], KT[:, :]).then_inc(pe_ak, 1)
            for b in range(NB):
                ins = mm(bank[2][0:KEYS, b * D:(b + 1) * D], VT[:, b * KEYS:(b + 1) * KEYS], wT[:, 2, :])
            ins.then_inc(pe_ak, 1)
            pe.wait_ge(dve_ak, 3)

            def max_job(b, j):
                i, half = divmod(j, 2)
                n = b * 2 * NI + j
                if n >= 2:
                    pe.wait_ge(dve_max, n - 1)
                if b >= 2 and j < 2:
                    pe.wait_ge(dve_on, NI * (b - 1))
                pair = 4 + 2 * (n % 2)
                for a in range(2):
                    ins = mm(bank[pair + a][:, 0:HK // 2], qhi[:, b, half, i * P:(i + 1) * P],
                             kbhi[:, b, half, a * (HK // 2):(a + 1) * (HK // 2)])
                ins.then_inc(pe_max, 1)

            def score_job(b, j):
                half, c = divmod(j, NC)
                n = b * 2 * NC + j
                rows = chunk_rows(c)
                cols = slice(c * P, c * P + rows)
                o = bank[1 + n % 3][0:rows, :]
                if n >= 3:
                    pe.wait_ge(act_ex, n - 2)
                mm(o, sel[:, half, cols], nmT[:, b % 2, :], True, False)
                mm(o, kbhi[:, b, half, cols], qhi[:, b, half, :], False, False)
                mm(o, kblo[:, b, half, cols], qhi[:, b, half, :], False, False)
                mm(o, kbhi[:, b, half, cols], qlo[:, b, half, :], False, True).then_inc(pe_sc, 1)

            pe.wait_ge(dve_q, 4 * NB)
            pe.wait_ge(dve_Wz, 6)
            for j in range(2 * NI):
                max_job(0, j)
            for b in range(NB + 1):
                if b >= 1:
                    pe.wait_ge(act_ex, 2 * NC * b)
                    for i in range(NI):
                        o = bank[4 + i]
                        if b >= 2:
                            pe.wait_ge(dve_on, NI * (b - 2) + i + 1)
                        pe.wait_ge(dve_max, 2 * NI * min(b + 1, NB))
                        for half in range(2):
                            for c in range(NC):
                                rows = chunk_rows(c)
                                h0, h1 = chunk_heads(c)
                                at = (half * HH + h0) * (FD + 1)
                                ins = mm(o[:, at:at + (h1 - h0) * (FD + 1)],
                                         ex[0:rows, half * NC + c, i * P:(i + 1) * P],
                                         Vx[0:rows, 2 * (b - 1) + half, c, h0:h1, :].rearrange("r h f -> r (h f)"),
                                         start=(half == c == 0), stop=(half == 1 and c == NC - 1))
                        ins.then_inc(pe_av, 1)
                if b < NB:
                    pe.wait_ge(dve_nm, b + 1)
                    for i in range(NI):
                        ins = pe.transpose(bank[0].bitcast(BF16)[0:3 * HEADS, i * P:(i + 1) * P],
                                           nm[:, b % 2, i].rearrange("p a h -> p (a h)"), identb[:, :])
                    ins.then_inc(pe_nmT, 1)
                    pe.wait_ge(act_nmT, b + 1)
                    if b >= 2:
                        pe.wait_ge(dve_x, b - 1)
                        pe.wait_ge(act_onT, NI * (b - 1))
                    for j in range(2 * NC):
                        score_job(b, j)
                        if b + 1 < NB and j < 2 * NI:
                            max_job(b + 1, j)
                if b >= 1:
                    pe.wait_ge(act_ex, 2 * NC * min(b + 1, NB))
                    for i in range(NI):
                        n = (b - 1) * NI + i
                        pe.wait_ge(dve_on, n + 1)
                        if i == 0 and b >= 2:
                            pe.wait_ge(dve_x, b - 1)
                        for a in range(2):
                            at = 256 * (i % 2) + a * P
                            ins = pe.transpose(bank[1 + i // 2][:, at:at + P], on[:, i, a * P:(a + 1) * P], ident[:, :])
                        if i % 2:
                            ins.then_inc(pe_onT, 2)
                    for i in range(NI):
                        pe.wait_ge(act_onT, (b - 1) * NI + i + 1)
                        for a in range(2):
                            ins = mm(bank[3][:, i * D:(i + 1) * D], onT[:, i, a, :], fcT[:, a, :], a == 0, a == 1)
                    ins.then_inc(pe_fc, 1)

            for b in range(NB):
                if b == 3:
                    pe.wait_ge(dve_x, NB)
                transpose_xn(1, b, bank[b])
            pe.wait_ge(ld_small, 16 * N_SMALL)
            for b in range(NB):
                pe.wait_ge(xT_ready, NB + b + 1)
                pe.wait_ge(dve_on, NB * NI)
                for i in range(NI):
                    ins = mm(bank[4 + b][:, i * E0:(i + 1) * E0], xnT[:, b, i * P:(i + 1) * P], gate0[:, :])
                ins.then_inc(pe_lg, 1)
            pe.wait_ge(pool_mask, 3)
            for b in range(NB + 1):
                if b < NB:
                    pe.wait_ge(dve_g, b + 1)
                    if b >= 1:
                        pe.wait_ge(dve_gT, b)
                    for i in range(NI):
                        ins = pe.transpose(bank[0].bitcast(BF16)[0:3 * E0, i * P:(i + 1) * P],
                                           g3[:, b, i].rearrange("p a e -> p (a e)"), identb[:, :])
                    ins.then_inc(pe_gT, 1)
                    for c in range(5):
                        n = 5 * b + c
                        if n >= 2:
                            pe.wait_ge(act_h, n - 1)
                        if c < 4:
                            mm(bank[1 + n % 2], W1[:, c * P:(c + 1) * P], xnT[:, b, :]).then_inc(pe_h, 1)
                            m = 4 * b + c
                            if c == 0:
                                pe.wait_ge(dve_gT, b + 1)
                                pe.wait_ge(act_lg, NB)
                            if m >= 2:
                                pe.wait_ge(dve_hg, m - 1)
                            mm(bank[3 + m % 2], selG[:, c, :], gT3[:, b, :]).then_inc(pe_G, 1)
                        else:
                            mm(bank[1 + n % 2][0:H0, :], Ws1[:, :], xnT[:, b, :]).then_inc(pe_h, 1)
                if b >= 1:
                    p = b - 1
                    pe.wait_ge(dve_hg, 4 * b)
                    pe.wait_ge(act_h, 5 * b)
                    if p >= 2:
                        pe.wait_ge(dve_x, NB + p - 1)
                    for i in range(NI):
                        o = bank[5 + p % 2][:, i * D:(i + 1) * D]
                        tok = slice(i * P, (i + 1) * P)
                        for c in range(4):
                            mm(o, hg[:, p % 2, c, tok], W2[:, c, :], c == 0, False)
                        mm(o, hs[:, p % 2, tok], Ws2[:, :], False, False)
                        for t in range(3):
                            ins = mm(o, gT3[:, p, tok], b2s[:, t, :], False, t == 2)
                    ins.then_inc(pe_y, 1)

            pe.wait_ge(dve_x, 2 * NB)
            for b in range(NB):
                transpose_xn(2, b, bank[b])
            def turn_weights(e):
                pe.wait_ge(ld_up[e], 16)
                pe.wait_ge(ld_dn[e], 16)
                for c in range(3):
                    if c == 2:
                        pe.wait_ge(xT_ready, 2 * NB + NB)
                        if e >= 1:
                            pe.wait_ge(act_upT, 3 * e)
                    elif e >= 1:
                        pe.wait_ge(dve_upT, 2 * (e - 1) + c + 1)
                    else:
                        pe.wait_ge(xT_ready, 2 * NB + NB)
                    for j in range(4):
                        src = upn[:, e % WR, 4 * c + j, :] if c < 2 else dnn[:, e % WR, j * P:(j + 1) * P]
                        ins = pe.transpose((bank[2 + c] if c < 2 else bank[0])[:, j * P:(j + 1) * P], src, ident[:, :])
                    ins.then_inc(pe_upT, 1)

            for b in range(NB):
                turn_weights(2 * b)
                turn_weights(2 * b + 1)
                pe.wait_ge(xT_ready, 2 * NB + b + 1)
                if b >= 2:
                    pe.wait_ge(dve_s1, b - 1)
                for i in range(NI):
                    o = bank[4 + b % 2][:, i * KEYS:(i + 1) * KEYS]
                    mm(o, xnT[:, b, i * P:(i + 1) * P], keyA[:, b * KEYS:(b + 1) * KEYS], True, False)
                    ins = mm(o, ones_row[:, :], keyc[:, b * KEYS:(b + 1) * KEYS], False, True)
                ins.then_inc(pe_s1, 1)
            pe.wait_ge(act_upT, 3 * E1)
            for b in range(NB + 1):
                if b < NB:
                    pe.wait_ge(act_s1, b + 1)
                    if b >= 2:
                        pe.wait_ge(act_pT, b - 1)
                    for i in range(NI):
                        ins = pe.transpose(bank[b % 2][0:KEYS, i * P:(i + 1) * P], pr[:, b, i, :], ident[:, :])
                    ins.then_inc(pe_pT, 1)
                if b >= 1:
                    p = b - 1
                    pe.wait_ge(act_pT, b)
                    for pair in range(2):
                        if p >= 1:
                            pe.wait_ge(dve_x, 2 * NB + p)
                        for i in range(2):
                            t = 2 * pair + i
                            ins = mm(bank[6 + pair][:, i * (D + 1):(i + 1) * (D + 1)],
                                     prT[:, p % 2, t * P:(t + 1) * P], Vo[:, p, :])
                        ins.then_inc(pe_o1, 1)

            for b in range(NB):
                transpose_xn(3, b, bank[b])
            for b in range(NB):
                pe.wait_ge(xT_ready, 3 * NB + b + 1)
                if b == 0:
                    pe.wait_ge(dve_x, 3 * NB)
                for i in range(NI):
                    ins = mm(bank[4 + b][:, i * E1:(i + 1) * E1], xnT[:, b, i * P:(i + 1) * P], gate1[:, :])
                ins.then_inc(pe_lg, 1)
            pe.wait_ge(dve_x, 3 * NB)
            pe.wait_ge(pool_mask, 4)
            pe.wait_ge(dve_cnt, NB)
            rank = bank[6][:, 0:(NT + 1) * E1]
            mm(rank, lower[:, :], cnt[:, :, :].rearrange("p t e -> p (t e)"), True, False)
            for t in range(NT):
                left = NT - t
                ins = mm(rank[:, (t + 1) * E1:].rearrange("p (t e) -> p t e", e=E1), onesb[:, :],
                         wide(cnt[:, t:t + 1, :], P, left, E1), False, t == NT - 1)
            ins.then_inc(pe_rank, 1)
            pe.wait_ge(dve_hot, 1)
            pe.wait_ge(act_lg, 2 * NB)
            for n in range(CH * NT):
                ins = mm(bank[7][:, 0:2 * NBLK], r_hot[:, n, :], b_val[:, n, :, :].rearrange("p a k -> p (a k)"),
                         n == 0, n == CH * NT - 1)
            ins.then_inc(pe_inv, 1)

            def turn_xg(k, s, first=False):
                pe.wait_ge(gathered[s], 8 * k - 8 * s + 16)
                if not first:
                    pe.wait_ge(dve_xg, 2 * k)
                pe.transpose(bank[7][:, 0:P], xg[:, s, :], ident[:, :]).then_inc(pe_xg, 1)

            def expert(k):
                return pe.value_load(blk_e[0:1, bass.ds(k, 1)], min_val=0, max_val=E1 - 1)

            def up(k, s, e, first=False):
                pe.wait_ge(dve_xg, 2 * k + 2)
                if not first:
                    pe.wait_ge(dve_h, k - 1)
                for a in range(2):
                    o = bank[2 * a + s]
                    cols = bass.ds(e * (2 * F1) + a * F1, F1)
                    mm(o, xghi[:, s, :], uphi[:, cols], True, False)
                    mm(o, xghi[:, s, :], uplo[:, cols], False, False)
                    ins = mm(o, xglo[:, s, :], uphi[:, cols], False, True)
                ins.then_inc(pe_up, 1)

            def turn_h(k, s, first=False):
                pe.wait_ge(dve_h, k + 1)
                if not first:
                    pe.wait_ge(act_hT, k)
                for c in range(4):
                    ins = pe.transpose(bank[4][:, c * P:(c + 1) * P], hh[:, s, c * P:(c + 1) * P], ident[:, :])
                ins.then_inc(pe_hT, 1)

            def down(k, s, e, first=False):
                pe.wait_ge(act_hT, k + 1)
                if not first:
                    pe.wait_ge(dve_y1, k)
                for c in range(4):
                    ins = mm(bank[6][:, 0:D], hhT[:, s, c, :], dnT[:, bass.ds(e * F1 + c * P, P)], c == 0, c == 3)
                ins.then_inc(pe_y1, 1)

            def block_step(k, s, e, e2, first=False):
                up(k, s, e)
                turn_xg(k + 1, 1 - s)
                down(k - 2, s, e2, first)
                turn_h(k - 1, 1 - s)

            pe.wait_ge(dve_upT, 2 * E1)
            turn_xg(0, 0, first=True)
            e = [expert(k) for k in range(2)]
            up(0, 0, e[0], first=True)
            turn_xg(1, 1)
            up(1, 1, e[1], first=True)
            turn_xg(2, 0)
            turn_h(0, 0, first=True)
            for k in range(2, LOOP0):
                block_step(k, k % 2, expert(k), e[k - 2], first=k == 2)
            with pe.Fori(LOOP0, LOOP1, UNROLL) as k0:
                packed = pe.value_load(blk_es[0:1, bass.ds(k0, 1)], min_val=0, max_val=E1 ** (UNROLL + 2) - 1)
                e = [(packed // E1 ** j) % E1 for j in range(UNROLL + 2)]
                for j in range(UNROLL):
                    block_step(k0 + j, j % 2, e[j + 2], e[j])
            e = [expert(LOOP1 - 2), expert(LOOP1 - 1)]
            for k in range(LOOP1, NBLK - 1):
                e.append(expert(k))
                block_step(k, k % 2, e[-1], e[-3])
            last = NBLK - 1
            e.append(expert(last))
            up(last, last % 2, e[-1])
            down(last - 2, last % 2, e[-3])
            turn_h(last - 1, 1 - last % 2)
            down(last - 1, 1 - last % 2, e[-2])
            turn_h(last, last % 2)
            down(last, last % 2, e[-1])


_INS = ["x", "ctx_1024", "mask_BxSxS2_ik0", "L0_xattn_fm_w", "L0_xattn_fm_b", "L0_xattn_fc_w", "L0_xattn_fc_b",
        "L0_ffn_gate_W", "L0_ffn_W1", "L0_ffn_b1", "L0_ffn_W2", "L0_ffn_b2", "L0_ffn_Ws1", "L0_ffn_bs1", "L0_ffn_Ws2",
        "L0_ffn_bs2", "L0_ffn_route_scale", "L1_xattn_Wq", "L1_xattn_bq", "L1_xattn_Wk", "L1_xattn_bk", "L1_xattn_Wv",
        "L1_xattn_bv", "L1_xattn_Wo", "L1_xattn_bo", "L1_ffn_gate_w", "L1_ffn_gate_up_w", "L1_ffn_down_w"]


def kernel(**inputs):
    import numpy as _np
    import concourse.bacc as _bacc
    from concourse import mybir as _mybir
    from concourse.bass_utils import run_bass_kernel_spmd as _run

    nc = _bacc.Bacc("TRN2", target_bir_lowering=False, num_devices=1)
    arrays, aps = {}, {}
    for name in _INS:
        a = _np.ascontiguousarray(inputs[name])
        if a.ndim == 0:
            a = a.reshape(1)
        arrays[f"in_{name}_dram"] = a
        aps[name] = nc.dram_tensor(f"in_{name}_dram", a.shape, _mybir.dt.from_np(a.dtype), kind="ExternalInput").ap()
    out = nc.dram_tensor("out_0_dram", (NB, SEQ, D), F32, kind="ExternalOutput").ap()
    two_layer_kernel(nc, aps, out)
    r = _run(nc, [arrays], core_ids=[0])
    return r.results[0]["out_0_dram"]
```

```python
from contextlib import ExitStack

import concourse.bass as bass
from concourse import mybir

F32 = mybir.dt.float32
F32R = mybir.dt.float32r
BF16 = mybir.dt.bfloat16
I32 = mybir.dt.int32
ALU = mybir.AluOpType
ACT = mybir.ActivationFunctionType
AX = mybir.AxisListType

P = 128
NB, SEQ, D = 4, 512, 128
NI = SEQ // P
KEYS = 77
HEADS, HD, FD = 16, 8, 16
HH = HEADS // 2
HK = HH * KEYS
NC = -(-HK // P)
E0, H0 = 8, 64
E1, F1 = 8, 512
WR = 3
NT = NB * NI
CH = 2
ROWS = NT * P
NBLK = CH * NT + E1 - 1
EPS = 1e-5
BIG = 3.0e38
SCALE = float(D) ** -0.5

NJ = 2 * NC
LAG = 2
RING = 5
STEPS = NB * NJ + LAG
UNITS = 2 * NI
UNIT = HH * (FD + 1)
AV_BANKS = (3, 6, 7)
UNIT_GROUPS = ((0, 3), (3, 4), (4, 6), (6, 8))
EARLY = 2

HOT_DVE = 27
VAL_DVE = 8
XR = 4
UNROLL = 8
PACK = 6
LOOP0 = 4
LOOP1 = LOOP0 + (NBLK - 1 - LOOP0) // UNROLL * UNROLL


def max_banks(b, j):
    return 6 if b == 0 and j % 2 else 4


def chunks_of_step(m):
    c = m - LAG
    if not 0 < c < NB * NJ or c % NJ == 0:
        return []
    return [c - 1, c] if c % NJ == 1 else [c]


def chunk_rows(c):
    return min(P, HK - c * P)


def chunk_heads(c):
    first = c * P // KEYS
    last = (c * P + chunk_rows(c) - 1) // KEYS
    return first, last + 1


def two_layer_kernel(nc, A, out):
    with ExitStack() as ctx:
        def sem(name):
            return ctx.enter_context(nc.semaphore(name))

        def sb(name, shape, dt=F32, at=ctx):
            return at.enter_context(nc.sbuf_tensor(name, shape, dt))

        ps = ctx.enter_context(nc.psum_tensor("ps", [P, 8, 512], F32))
        bank = [ps[:, i, :] for i in range(8)]

        x = sb("x", [P, NB, NI, D])
        xb = sb("xb", [P, NB, NI, D])
        xn = sb("xn", [P, NB, NI, D])
        xnT = sb("xnT", [P, NB, SEQ])
        stats = sb("stats", [P, NB, NI, 6])
        mv = sb("mv", [P, NB, NI, 2])
        rstd = sb("rstd", [P, NB, NI])
        ident = sb("ident", [P, P])
        identb = sb("identb", [P, P], BF16)
        neghalf = sb("neghalf", [P, NI])
        biases = sb("biases", [P, 3, D])
        fcT = sb("fcT", [P, 2, D])
        W1 = sb("W1", [P, E0 * H0])
        Ws1 = sb("Ws1", [P, H0])
        gate0 = sb("gate0", [P, E0])
        W2 = sb("W2", [P, 4, D])
        Ws2 = sb("Ws2", [H0, D])
        b1 = sb("b1", [P, 4])
        bs1 = sb("bs1", [H0, 1])
        b2 = sb("b2", [3 * E0, D])
        b2s = sb("b2s", [3 * E0, 3, D], BF16)
        b2r = sb("b2r", [3 * E0, D])
        route_scale = sb("route_scale", [P, 1])
        gate1 = sb("gate1", [P, E1])
        mask_i = sb("mask_i", [P, NB, NI * KEYS], I32)
        maskb = mask_i[:, :, :].bitcast(F32)
        keyA = sb("keyA", [P, NB * KEYS])
        keyc = sb("keyc", [P, NB * KEYS])
        Vo = sb("Vo", [KEYS, NB, D + 1])
        iota8 = sb("iota8", [P, NT, E0])
        sel = sb("sel", [3 * HEADS, 2, NC * P], BF16)
        selG = sb("selG", [3 * E0, 4, P], BF16)
        r_s = sb("r_s", [P, NT, E0])
        r_a = sb("r_a", [P, NT, E0])
        r_b = sb("r_b", [P, NT, E0])
        r_o1 = sb("r_o1", [P, NT, E0])
        r_o2 = sb("r_o2", [P, NT, E0])
        r_m = sb("r_m", [P, 6, NT])

        g3 = sb("g3", [P, NT, 3, E0], BF16)
        g3r = sb("g3r", [P, NT, E0])

        l0 = ExitStack()
        ctx_tok = sb("ctx_tok", [KEYS, NB, D], at=l0)
        ctxT = sb("ctxT", [P, NB * KEYS], at=l0)
        wnat = sb("wnat", [P, 4, D], at=l0)
        wT = sb("wT", [P, 3, D], at=l0)
        bqkv = sb("bqkv", [P, 3], at=l0)
        KT = sb("KT", [P, NB * KEYS], at=l0)
        VT = sb("VT", [P, NB * KEYS], at=l0)
        fcn = sb("fcn", [P, 2, D], at=l0)
        gate1n = sb("gate1n", [E1, D], at=l0)
        fm = sb("fm", [HD, HD + 1], at=l0)
        fmT = sb("fmT", [P, HD + 1], at=l0)
        mask16 = sb("mask16", [P, 2, HEADS], at=l0)
        maskK = sb("maskK", [P, HH], at=l0)
        ind = sb("ind", [P, NC, HH], at=l0)
        indw = sb("indw", [P, 2, NC, 3, HEADS], BF16, at=l0)
        Wz = sb("Wz", [P, 2, HH, 2, HD], at=l0)
        kbhi = sb("kbhi", [P, NB, 2, HK], F32R, at=l0)
        kblo = sb("kblo", [P, NB, 2, HK], F32R, at=l0)
        Vx = sb("Vx", [P, NB * 2, NC, HH, FD + 1], at=l0)
        qf = sb("qf", [P, 2, SEQ], at=l0)
        qhi = sb("qhi", [P, NB, 2, SEQ], F32R, at=l0)
        qlo = sb("qlo", [P, NB, 2, SEQ], F32R, at=l0)
        mx = sb("mx", [P, 2, NI, HEADS], at=l0)
        nm = sb("nm", [P, 2, NI, 3, HEADS], BF16, at=l0)
        nmr = sb("nmr", [P, 2, NI, HEADS], at=l0)
        nmT = sb("nmT", [3 * HEADS, 2, SEQ], BF16, at=l0)
        selGt = sb("selGt", [3 * E0, 3, 4 * P], BF16, at=l0)
        early = ExitStack()
        kbf = sb("kbf", [P, NB, 2, HK], at=early)
        kf = sb("kf", [P, 2, NB * KEYS], at=early)
        kfhi = sb("kfhi", [P, 2, NB * KEYS], F32R, at=early)
        kflo = sb("kflo", [P, 2, NB * KEYS], F32R, at=early)
        isgn = sb("isgn", [HD, HH, 2, HD], at=early)
        fmrep = sb("fmrep", [HD, HEADS, HD], at=early)
        early.close()
        ex = sb("ex", [P, RING, SEQ], at=l0)
        rec = sb("rec", [P, UNITS, HH], at=l0)
        on = sb("on", [P, NI, HEADS * FD], at=l0)
        onT = sb("onT", [P, NI, 2, P], at=l0)
        l0.close()

        mlp = ExitStack()
        hraw = sb("hraw", [P, 2, SEQ], at=mlp)
        hg = sb("hg", [P, 2, 4, SEQ], at=mlp)
        hs = sb("hs", [H0, 2, SEQ], at=mlp)
        gT3 = sb("gT3", [3 * E0, NB, SEQ], BF16, at=mlp)
        mlp.close()
        r_hot = sb("r_hot", [P, CH * NT, P], BF16)
        b_val = sb("b_val", [P, CH * NT, 2, NBLK], BF16)
        slots = ExitStack()
        b_hot = sb("b_hot", [P, CH * NT, NBLK], BF16, at=slots)
        slots.close()
        gl = sb("gl", [P, 2, F1])
        hh = sb("hh", [P, 2, F1])
        hhT = sb("hhT", [P, 2, 4, P])
        xg = sb("xg", [P, XR, D])
        xghi = sb("xghi", [P, 2, P], F32R)
        xglo = sb("xglo", [P, 2, P], F32R)
        yb = sb("yb", [P, 2, D])
        sc = sb("sc", [P, 2, NI, KEYS])
        scm = sb("scm", [P, 2, NI])
        pr = sb("pr", [P, NB, NI, KEYS])
        prT = sb("prT", [KEYS, 2, SEQ])
        srec = sb("srec", [P, 2, NI])
        upn = sb("upn", [P, WR, 8, D])
        dnn = sb("dnn", [P, WR, F1])
        uphi = sb("uphi", [P, E1 * 2 * F1], F32R)
        uplo = sb("uplo", [P, E1 * 2 * F1], F32R)
        dnT = sb("dnT", [P, E1 * F1])
        onehot = sb("onehot", [P, CH, NT, E1])
        wgt = sb("wgt", [P, CH, NT])
        cnt = sb("cnt", [P, NT + 1, E1], BF16)
        lower = sb("lower", [P, P], BF16)
        onesb = sb("onesb", [P, P], BF16)
        before = sb("before", [P, E1, E1])
        iota_n = sb("iota_n", [P, E1, NT])
        iota_k = sb("iota_k", [P, NBLK])
        iota_r = sb("iota_r", [P, P], BF16)
        tile_q = sb("tile_q", [P, CH * NT], BF16)
        p_one = sb("p_one", [P, 1])
        pad_row = sb("pad_row", [P, NBLK])
        m_n = sb("m_n", [P, E1])
        m_cmp = sb("m_cmp", [P, E1, NT])
        m_nb = sb("m_nb", [P, E1])
        m_bb = sb("m_bb", [P, E1])
        m_ce = sb("m_ce", [P, E1])
        m_lt = sb("m_lt", [P, E1, E1])
        m_at = sb("m_at", [P, NT, E1])
        m_pos = sb("m_pos", [P, CH * NT])
        m_posi = sb("m_posi", [P, 3, CH * NT], I32)
        m_posf = sb("m_posf", [P, 2, CH * NT])
        m_pe = sb("m_pe", [P, CH, NT, E1])
        m_k = sc[0:1, :, :, :].rearrange("p s i k -> p (s i k)")[:, 0:NBLK * E1].rearrange("p (k e) -> p k e", e=E1)
        m_kf = sb("m_kf", [1, NBLK])
        blk_e = sb("blk_e", [1, NBLK], I32)
        m_pack = sb("m_pack", [1, NBLK])
        blk_es = sb("blk_es", [1, NBLK + PACK], I32)
        inv = sb("inv", [P, 2, NBLK])
        row_f = sb("row_f", [P, 3, NBLK])
        src_row = sb("src_row", [P, NBLK], I32)
        dst_row = sb("dst_row", [P, NBLK], I32)
        yc = dnT[:, :].rearrange("p (b c i d) -> p b c i d", b=NB, c=CH, i=NI)
        xn_dram = nc.dram_tensor("xn_dram", (ROWS, D), F32, kind="Internal").ap()
        y_dram = nc.dram_tensor("y_dram", (CH * ROWS + NBLK * P, D), F32, kind="Internal").ap()

        XT2 = (0, 1, 7, 1)
        XT3 = (5, 5, 5, 1)
        UPT = (2, 3, 0)

        def load_sem(name):
            return sem("ld_" + name)

        ld_x = [load_sem(f"x{b}") for b in range(NB)]
        ld_ctx, ld_fm, ld_w, ld_small, ld_mask = (load_sem(n) for n in ("ctx", "fm", "w", "small", "mask"))
        ld_up = [load_sem(f"up{e}") for e in range(E1)]
        ld_dn = [load_sem(f"dn{e}") for e in range(E1)]
        stored = sem("stored")
        pool_ident, pool_const, pool_mask, pool_ind, pool_kb = (sem("pool_" + n) for n in ("ident", "const", "mask", "ind", "kb"))
        pool_kbf = sem("pool_kbf")
        pool_xb, pool_rstd = sem("pool_xb"), sem("pool_rstd")
        dve_c, dve_link = sem("dve_c"), sem("dve_link")
        pe_ctxT, pe_fm, pe_kz, pe_wT, pe_kv, pe_ak, pe_vt = (sem("pe_" + n) for n in ("ctxT", "fm", "kz", "wT", "kv", "ak", "vt"))
        dve_ctxT, dve_fmT, dve_Wz, dve_kf, dve_kb = (sem("dve_" + n) for n in ("ctxT", "fmT", "Wz", "kf", "kb"))
        act_wT, act_kv, act_ak = (sem("act_" + n) for n in ("wT", "kv", "ak"))
        act_kf, act_vx = sem("act_kf"), sem("act_vx")
        dve_mv, dve_xn, pe_xT, xT_ready = sem("dve_mv"), sem("dve_xn"), sem("pe_xT"), sem("act_xT")
        pe_z, act_qhi, act_q, dve_q = sem("pe_z"), sem("act_qhi"), sem("act_q"), sem("dve_q")
        pe_max, dve_max, dve_nm, pe_nmT, act_nmT = (sem(n) for n in ("pe_max", "dve_max", "dve_nm", "pe_nmT", "act_nmT"))
        pe_sc, act_ex, pe_av, dve_on, pe_onT, act_onT, pe_fc = (
            sem(n) for n in ("pe_sc", "act_ex", "pe_av", "dve_on", "pe_onT", "act_onT", "pe_fc"))
        dve_x = sem("dve_x")
        pe_lg, act_lg, dve_g, pe_gT, dve_gT, pe_G, pe_h, act_h, dve_hg, pe_y = (
            sem(n) for n in ("pe_lg", "act_lg", "dve_g", "pe_gT", "dve_gT", "pe_G", "pe_h", "act_h", "dve_hg", "pe_y"))
        pe_s1, dve_s1, act_s1, pe_pT, act_pT, pe_o1 = (sem(n) for n in ("pe_s1", "dve_s1", "act_s1", "pe_pT", "act_pT", "pe_o1"))
        pe_upT, act_upT, dve_upT = sem("pe_upT"), sem("act_upT"), sem("dve_upT")
        dve_cnt, pe_rank, dve_hot, pe_inv, dve_idx = (sem(n) for n in ("dve_cnt", "pe_rank", "dve_hot", "pe_inv", "dve_idx"))
        pe_xg, dve_xg, pe_up, act_gl, dve_h, pe_hT, act_hT, pe_y1, dve_y1 = (
            sem(n) for n in ("pe_xg", "dve_xg", "pe_up", "act_gl", "dve_h", "pe_hT", "act_hT", "pe_y1", "dve_y1"))
        dve_posf, dve_bhot, dve_rhot, pool_rhot = (sem(n) for n in ("dve_posf", "dve_bhot", "dve_rhot", "pool_rhot"))
        dve_bval, act_bval, pool_bval = (sem(n) for n in ("dve_bval", "act_bval", "pool_bval"))
        xn_stored = sem("xn_stored")
        gathered = [sem(f"gathered{r}") for r in range(XR)]
        scattered = [sem("scattered0"), sem("scattered1")]
        y_loaded = [sem(f"y_loaded{b}") for b in range(NB)]
        act_y, dve_y, dve_out, pool_out = sem("act_y"), sem("dve_y"), sem("dve_out"), sem("pool_out")

        x_dram = A["x"].rearrange("b (i p) d -> b p i d", p=P)
        out_dram = out.rearrange("b (i p) d -> b p i d", p=P)
        mask_dram = A["mask_BxSxS2_ik0"].rearrange("b (i p) k -> b p i k", p=P)

        def row(name):
            return A[name].rearrange("(a n) -> a n", a=1)

        def col(name):
            return A[name].rearrange("(n a) -> n a", a=1)

        def everywhere(name, n=P):
            return A[name].partition_broadcast(n)

        block = ctx.enter_context(nc.Block())

        N_SMALL = 14
        N_FM = 2
        N_W = 9

        @block.sync
        def _(sp):
            sp.dma_start(ctx_tok[:, :, :], A["ctx_1024"].rearrange("b k d -> k b d")).then_inc(ld_ctx, 16)
            sp.dma_start(fm[:, 0:HD], A["L0_xattn_fm_w"]).then_inc(ld_fm, 16)
            sp.dma_start(fm[:, HD:HD + 1], col("L0_xattn_fm_b")).then_inc(ld_fm, 16)
            for b in range(NB):
                sp.dma_start(x[:, b, :, :], x_dram[b]).then_inc(ld_x[b], 16)
            for n, name in enumerate(("Wq", "Wk", "Wv", "Wo")):
                sp.dma_start(wnat[:, n, :], A["L1_xattn_" + name]).then_inc(ld_w, 16)
            for n, name in enumerate(("bq", "bk", "bv")):
                sp.dma_start(bqkv[:, n:n + 1], col("L1_xattn_" + name)).then_inc(ld_w, 16)
            sp.dma_start(fcn[:, :, :], A["L0_xattn_fc_w"].rearrange("n (a f) -> n a f", a=2)).then_inc(ld_w, 16)
            sp.dma_start(gate1n[:, :], A["L1_ffn_gate_w"]).then_inc(ld_w, 16)
            for n, name in enumerate(("L0_xattn_fc_b", "L0_ffn_bs2", "L1_xattn_bo")):
                sp.dma_start(biases[:, n, :], everywhere(name)).then_inc(ld_small, 16)
            sp.dma_start(W1[:, :].rearrange("d (e h) -> d e h", e=E0), A["L0_ffn_W1"].rearrange("e d h -> d e h")).then_inc(ld_small, 16)
            sp.dma_start(Ws1[:, :], A["L0_ffn_Ws1"]).then_inc(ld_small, 16)
            sp.dma_start(gate0[:, :], A["L0_ffn_gate_W"]).then_inc(ld_small, 16)
            sp.dma_start(W2[:, :, :], A["L0_ffn_W2"].rearrange("(c a) h d -> (a h) c d", a=2)).then_inc(ld_small, 16)
            sp.dma_start(Ws2[:, :], A["L0_ffn_Ws2"]).then_inc(ld_small, 16)
            sp.dma_start(b1[:, :], A["L0_ffn_b1"].rearrange("(c a) h -> (a h) c", a=2),
                         allow_slow_non_contiguous=True).then_inc(ld_small, 16)
            sp.dma_start(bs1[:, :], col("L0_ffn_bs1")).then_inc(ld_small, 16)
            for t in range(3):
                sp.dma_start(b2[E0 * t:E0 * t + E0, :], A["L0_ffn_b2"]).then_inc(ld_small, 16)
            sp.dma_start(route_scale[:, :], A["L0_ffn_route_scale"].partition_broadcast(P)).then_inc(ld_small, 16)
            for b in range(NB):
                sp.dma_start(mask_i[:, b, :].rearrange("p (i k) -> p i k", i=NI), mask_dram[b]).then_inc(ld_mask, 16)
            sp.wait_ge(pe_fc, NB)
            sp.wait_ge(dve_on, len(UNIT_GROUPS) * NB)
            sp.wait_ge(act_onT, NB * NI)
            sp.wait_ge(pool_mask, 3)
            for e in range(E1):
                if e >= WR:
                    sp.wait_ge(pe_upT, 3 * (e - WR + 1))
                sp.dma_start(upn[:, e % WR, :, :], A["L1_ffn_gate_up_w"][e].rearrange("(c f) h -> f c h", f=P)).then_inc(ld_up[e], 16)
                sp.dma_start(dnn[:, e % WR, :], A["L1_ffn_down_w"][e]).then_inc(ld_dn[e], 16)
            for b in range(NB):
                sp.wait_ge(dve_xn, (3 * NB + b + 1) * NI)
                sp.dma_start(xn_dram[b * SEQ:(b + 1) * SEQ, :].rearrange("(i p) d -> p i d", p=P), xn[:, b, :, :]).then_inc(xn_stored, 16)
            for s in range(2):
                sp.wait_ge(scattered[s], 16 * ((NBLK - s + 1) // 2))
            for b in range(NB):
                for c in range(CH):
                    sp.dma_start(yc[:, b, c, :, :],
                                 y_dram[c * ROWS + b * SEQ:c * ROWS + (b + 1) * SEQ, :].rearrange("(i p) d -> p i d", p=P))\
                        .then_inc(y_loaded[b], 16)
            for b in range(NB):
                if b < NB - 1:
                    sp.wait_ge(pool_out, b + 1)
                else:
                    sp.wait_ge(dve_out, 1)
                sp.dma_start(out_dram[b], x[:, b, :, :]).then_inc(stored, 16)
            sp.wait_ge(stored, 16 * NB)


        def wide(ap, *shape):
            return ap.to_broadcast(list(shape))

        @block.gpsimd
        def _(g):
            link = [0]

            def ordered(ins):
                link[0] += 1
                ins.then_inc(pool_const, 1)
                g.wait_ge(pool_const, link[0])

            def band(t, pattern, mult, width, base=0):
                ordered(g.affine_select(out=t, in_=t, compare_op=ALU.is_ge, fill=0.0, base=base,
                                        pattern=pattern, channel_multiplier=mult))
                ordered(g.affine_select(out=t, in_=t, compare_op=ALU.is_ge, fill=0.0, base=width - 1 - base,
                                        pattern=[[-s, n] for s, n in pattern], channel_multiplier=-mult))

            def layernorm_rstd(k):
                for b in range(NB):
                    g.wait_ge(dve_mv, k * NB + b + 1)
                    ordered(g.tensor_scalar(rstd[:, b, :], mv[:, b, :, 1], EPS, None, ALU.add))
                    g.tensor_tensor(rstd[:, b, :], rstd[:, b, :], neghalf[:, :], ALU.pow).then_inc(pool_rstd, 1)

            def add_bias(k):
                for b in range(NB):
                    if k == 0:
                        g.wait_ge(ld_x[b], 16)
                        g.wait_ge(ld_small, 16 * N_SMALL)
                    else:
                        g.wait_ge(dve_x, (k - 1) * NB + b + 1)
                    g.tensor_tensor(xb[:, b, :, :], x[:, b, :, :], wide(biases[:, k:k + 1, :], P, NI, D), ALU.add)\
                        .then_inc(pool_xb, 1)

            ordered(g.memset(ident[:, :], 1.0))
            band(ident[:, :], [[-1, P]], 1, 1)
            g.tensor_copy(identb[:, :], ident[:, :]).then_inc(pool_ident, 1)
            ordered(g.memset(mask16[:, 0, :], 1.0))
            band(mask16[:, 0, :], [[-HD, HEADS]], 1, HD)
            ordered(g.memset(maskK[:, :], 1.0))
            band(maskK[:, :], [[-FD, HH]], 1, FD)
            ordered(g.memset(isgn[:, :, 0, :], 1.0))
            band(isgn[:, :, 0, :], [[0, HH], [-1, HD]], 1, 1)
            g.tensor_scalar(isgn[:, :, 1, :], isgn[:, :, 0, :], -1.0, None, ALU.mult).then_inc(pool_mask, 1)
            g.tensor_scalar(mask16[:, 1, :], mask16[:, 0, :], -1.0, None, ALU.mult).then_inc(pool_mask, 1)
            ordered(g.memset(neghalf[:, :], -0.5))
            layernorm_rstd(0)
            ordered(g.memset(ind[:, :, :], 1.0))
            band(ind[:, :, :], [[P, NC], [-KEYS, HH]], 1, KEYS)
            ordered(g.memset(indw[:, :, :, :, :], 0.0))
            for half in range(2):
                for part in range(3):
                    g.tensor_copy(indw[:, half, :, part, half * HH:half * HH + HH], ind[:, :, :]).then_inc(pool_ind, 1)
            g.tensor_copy(Vx[:, :, :, :, FD],
                          wide(ind[:, :, :].unsqueeze(1), P, NB * 2, NC, HH)).then_inc(pool_ind, 1)
            g.wait_ge(act_kf, 2)
            for b in range(NB):
                for half in range(2):
                    g.tensor_tensor(kbf[:, b, half, :].rearrange("p (h k) -> p h k", h=HH),
                                    wide(kf[:, half, b * KEYS:(b + 1) * KEYS].unsqueeze(1), P, HH, KEYS),
                                    wide(maskK[:, :].unsqueeze(2), P, HH, KEYS), ALU.mult).then_inc(pool_kbf, 1)
            g.wait_ge(dve_kf, 4)
            for b in range(NB):
                for half in range(2):
                    g.tensor_tensor(kblo[:, b, half, :].bitcast(F32R).rearrange("p (h k) -> p h k", h=HH),
                                    wide(kflo[:, half, b * KEYS:(b + 1) * KEYS].bitcast(F32).unsqueeze(1), P, HH, KEYS),
                                    wide(maskK[:, :].unsqueeze(2), P, HH, KEYS), ALU.mult).then_inc(pool_kb, 1)
            add_bias(0)
            ordered(g.iota(iota8[:, :, :], pattern=[[0, NT], [-1, E0]], base=E0, channel_multiplier=0,
                           allow_small_or_imprecise_dtypes=True))
            for part in range(3):
                ordered(g.memset(selGt[:, part, :], 1.0))
                band(selGt[:, part, :], [[1, 4 * P]], -H0, H0, base=H0 * E0 * part)
            ordered(g.tensor_tensor(selGt[:, 0, :], selGt[:, 0, :], selGt[:, 1, :], ALU.add))
            ordered(g.tensor_tensor(selGt[:, 0, :], selGt[:, 0, :], selGt[:, 2, :], ALU.add))
            ordered(g.tensor_copy(selG[:, :, :].rearrange("q c r -> q (c r)"), selGt[:, 0, :]))
            g.wait_ge(ld_small, 16 * N_SMALL)
            ordered(g.tensor_copy(b2s[:, 0, :], b2[:, :]))
            ordered(g.tensor_tensor(b2r[:, :], b2[:, :], b2s[:, 0, :], ALU.subtract))
            ordered(g.tensor_copy(b2s[:, 1, :], b2r[:, :]))
            ordered(g.tensor_tensor(b2r[:, :], b2r[:, :], b2s[:, 1, :], ALU.subtract))
            ordered(g.tensor_copy(b2s[:, 2, :], b2r[:, :]))
            g.wait_ge(ld_mask, 16 * NB)
            ordered(g.tensor_scalar(maskb[:, :, :], mask_i[:, :, :], 0.0, -BIG, ALU.is_equal, ALU.mult))
            g.wait_ge(act_ak, 2)
            ordered(g.tensor_tensor(maskb[:, :, :].rearrange("p b (i k) -> p b i k", i=NI),
                                    maskb[:, :, :].rearrange("p b (i k) -> p b i k", i=NI),
                                    wide(keyc[:, :].rearrange("p (b i k) -> p b i k", b=NB, i=1), P, NB, NI, KEYS), ALU.add))
            g.memset(Vo[:, :, D:D + 1], 1.0).then_inc(pool_mask, 1)
            layernorm_rstd(1)
            add_bias(1)
            layernorm_rstd(2)
            add_bias(2)
            layernorm_rstd(3)
            def const(t, value=None, **iota):
                if value is not None:
                    ordered(g.memset(t, value))
                else:
                    ordered(g.iota(t, allow_small_or_imprecise_dtypes=True, **iota))

            const(lower[:, :], 1.0)
            ordered(g.affine_select(out=lower[:, :], in_=lower[:, :], compare_op=ALU.is_gt, fill=0.0, base=0,
                                    pattern=[[1, P]], channel_multiplier=-1))
            const(onesb[:, :], 1.0)
            const(cnt[:, NT, :], 0.0)
            const(before[:, :, :], 1.0)
            ordered(g.affine_select(out=before[:, :, :], in_=before[:, :, :], compare_op=ALU.is_gt, fill=0.0, base=0,
                                    pattern=[[1, E1], [-1, E1]], channel_multiplier=0))
            const(iota_n[:, :, :], pattern=[[0, E1], [P, NT]], base=0, channel_multiplier=0)
            const(iota_k[:, :], pattern=[[1, NBLK]], base=0, channel_multiplier=0)
            const(iota_r[:, :], pattern=[[1, P]], base=0, channel_multiplier=0)
            const(tile_q[:, :], pattern=[[1, CH * NT]], base=0, channel_multiplier=0)
            const(p_one[:, :], pattern=[[0, 1]], base=1, channel_multiplier=1)
            g.iota(pad_row[:, :], pattern=[[P, NBLK]], base=CH * ROWS + 1, channel_multiplier=1,
                   allow_small_or_imprecise_dtypes=True).then_inc(pool_mask, 1)

            def gather(k):
                if k >= XR:
                    g.wait_ge(pe_xg, k - XR + 1)
                g.indirect_dma_start(xg[:, k % XR, :], None, xn_dram,
                                     bass.IndirectOffsetOnAxis(ap=src_row[:, k:k + 1], axis=0)).then_inc(gathered[k % XR], 16)

            def scatter(k):
                g.wait_ge(dve_y1, k + 1)
                g.indirect_dma_start(y_dram, bass.IndirectOffsetOnAxis(ap=dst_row[:, k:k + 1], axis=0),
                                     yb[:, k % 2, :], None).then_inc(scattered[k % 2], 16)

            g.wait_ge(dve_posf, 1)
            for n in range(HOT_DVE, CH * NT):
                if n == HOT_DVE + 2:
                    g.wait_ge(dve_bhot, 1)
                    g.tensor_tensor(b_val[:, VAL_DVE:, 0, :], b_hot[:, VAL_DVE:, :],
                                    wide(tile_q[:, VAL_DVE:].unsqueeze(2), P, CH * NT - VAL_DVE, NBLK), ALU.mult).then_inc(pool_bval, 1)
                g.tensor_scalar(r_hot[:, n, :], iota_r[:, :], m_posf[:, 0, n:n + 1], None, ALU.is_equal).then_inc(pool_rhot, 1)
            g.wait_ge(dve_idx, 1)
            g.wait_ge(xn_stored, 16 * NB)
            for k in range(NBLK):
                gather(k)
                if k >= XR + 2:
                    scatter(k - XR - 2)
            for k in range(NBLK - XR - 2, NBLK):
                scatter(k)
            for b in range(NB - 1):
                g.wait_ge(dve_y, (b + 1) * NI)
                g.wait_ge(act_y, (b + 1) * NI)
                g.tensor_tensor(x[:, b, :, :], x[:, b, :, :], yc[:, b, 1, :, :], ALU.add).then_inc(pool_out, 1)

        @block.vector
        def _(v):
            link = [0]

            def step(ins):
                link[0] += 1
                ins.then_inc(dve_link, 1)

            def settle():
                v.wait_ge(dve_link, link[0])

            def layernorm_stats(b):
                for i in range(NI):
                    step(v.bn_stats(stats[:, b, i, :], x[:, b, i, :]))
                settle()
                for i in range(NI):
                    ins = v.bn_aggr(mv[:, b, i, :], stats[:, b, i, :])
                    if i < NI - 1:
                        step(ins)
                settle()
                ins.then_inc(dve_mv, 1)

            def layernorm_apply(k, b):
                v.wait_ge(pool_rstd, k * NB + b + 1)
                for i in range(NI):
                    v.tensor_scalar(xn[:, b, i, :], x[:, b, i, :], mv[:, b, i, 0:1], rstd[:, b, i:i + 1],
                                    ALU.subtract, ALU.mult).then_inc(dve_xn, 1)

            def first_best(t0, t1, src, best, onehot_):
                t, n = slice(t0, t1), t1 - t0

                def w(i):
                    return wide(r_m[:, i, t].unsqueeze(2), P, n, E0)

                step(v.tensor_reduce(r_m[:, best, t], src[:, t, :], AX.X, ALU.max))
                settle()
                step(v.tensor_tensor(r_b[:, t, :], src[:, t, :], w(best), ALU.is_equal))
                settle()
                step(v.tensor_tensor(r_b[:, t, :], r_b[:, t, :], iota8[:, t, :], ALU.mult))
                settle()
                step(v.tensor_reduce(r_m[:, best + 1, t], r_b[:, t, :], AX.X, ALU.max))
                settle()
                step(v.tensor_tensor(onehot_[:, t, :], r_b[:, t, :], w(best + 1), ALU.is_equal))
                settle()

            def second_best(t0, t1):
                t = slice(t0, t1)
                step(v.scalar_tensor_tensor(out=r_a[:, t, :], in0=r_o1[:, t, :], scalar=-BIG, in1=r_s[:, t, :],
                                            op0=ALU.mult, op1=ALU.add))
                settle()
                first_best(t0, t1, r_a, 2, r_o2)

            def best_weights(t0, t1):
                m, t = r_m, slice(t0, t1)
                step(v.tensor_tensor(m[:, 4, t], m[:, 0, t], m[:, 2, t], ALU.add))
                settle()
                step(v.reciprocal(m[:, 5, t], m[:, 4, t]))
                settle()
                step(v.tensor_tensor(m[:, 0, t], m[:, 0, t], m[:, 5, t], ALU.mult))
                step(v.tensor_tensor(m[:, 2, t], m[:, 2, t], m[:, 5, t], ALU.mult))
                settle()

            v.wait_ge(ld_fm, 16 * N_FM)
            v.tensor_copy(fmrep[:, :, :], wide(fm[:, 0:HD].unsqueeze(1), HD, HEADS, HD)).then_inc(dve_c, 1)
            v.wait_ge(pe_ctxT, 1)
            v.tensor_copy(ctxT[:, :], bank[0][:, 0:NB * KEYS]).then_inc(dve_ctxT, 1)
            v.wait_ge(pe_fm, 1)
            v.tensor_copy(fmT[:, :], bank[1][:, 0:HD + 1]).then_inc(dve_fmT, 1)
            v.wait_ge(dve_fmT, 1)
            v.wait_ge(pool_mask, 2)
            for half in range(2):
                for s in range(2):
                    v.tensor_tensor(Wz[:, half, :, s, :], wide(fmT[:, 0:HD].unsqueeze(1), P, HH, HD),
                                    wide(mask16[:, s, half * HH:half * HH + HH].unsqueeze(2), P, HH, HD),
                                    ALU.mult).then_inc(dve_Wz, 1)
            for b in range(NB):
                v.wait_ge(ld_x[b], 16)
                layernorm_stats(b)
            for b in range(NB):
                layernorm_apply(0, b)
            v.wait_ge(act_kf, 2)
            for half in range(2):
                v.tensor_copy(kfhi[:, half, :], kf[:, half, :]).then_inc(dve_kf, 1)
            v.wait_ge(dve_kf, 2)
            for half in range(2):
                v.tensor_tensor(kflo[:, half, :], kf[:, half, :], kfhi[:, half, :].bitcast(F32), ALU.subtract)\
                    .then_inc(dve_kf, 1)
            for b in range(NB):
                for half in range(2):
                    v.tensor_tensor(kbhi[:, b, half, :].rearrange("p (h k) -> p h k", h=HH),
                                    wide(kfhi[:, half, b * KEYS:(b + 1) * KEYS].bitcast(F32).unsqueeze(1), P, HH, KEYS),
                                    wide(maskK[:, :].unsqueeze(2), P, HH, KEYS), ALU.mult).then_inc(dve_kb, 1)
                for half in range(2):
                    n = 2 * b + half
                    v.wait_ge(act_q, n + 1)
                    v.tensor_tensor(qlo[:, b, half, :], qf[:, half, :], qhi[:, b, half, :].bitcast(F32), ALU.subtract)\
                        .then_inc(dve_q, 1)
            for half in range(2):
                v.wait_ge(pe_kz, 3 + half)
                v.tensor_copy(sel[:, half, :], bank[6 + half].bitcast(BF16)[0:3 * HEADS, 0:NC * P]).then_inc(dve_Wz, 1)
            def max_of(b, j):
                i, half = divmod(j, 2)
                pair = max_banks(b, j)
                v.wait_ge(pe_max, b * 2 * NI + j + 1)
                v.tensor_reduce(mx[:, b % 2, i, half * HH:half * HH + HH].rearrange("p (a h) -> p a h", a=2),
                                ps[:, pair:pair + 2, 0:HK // 2].rearrange("p a (h k) -> p a h k", h=HH // 2),
                                AX.X, ALU.max).then_inc(dve_max, 1)

            def negate_max(b):
                v.wait_ge(dve_max, (b + 1) * 2 * NI)
                if b >= 2:
                    v.wait_ge(pe_nmT, b - 1)
                m, r = mx[:, b % 2], nmr[:, b % 2]
                step(v.tensor_scalar(nm[:, b % 2, :, 0, :], m, -1.0, None, ALU.mult))
                settle()
                step(v.scalar_tensor_tensor(out=r, in0=m, scalar=-1.0, in1=nm[:, b % 2, :, 0, :], op0=ALU.mult, op1=ALU.subtract))
                settle()
                step(v.tensor_copy(nm[:, b % 2, :, 1, :], r))
                settle()
                v.tensor_tensor(nm[:, b % 2, :, 2, :], r, nm[:, b % 2, :, 1, :], ALU.subtract).then_inc(dve_nm, 1)

            def normalise(b, groups):
                v.wait_ge(pe_av, NJ * (b + 1))
                if b >= 1:
                    v.wait_ge(pe_onT, NI * b)
                for u0, u1 in groups:
                    av = bank[AV_BANKS[u0 // 3]][:, (u0 % 3) * UNIT:(u0 % 3 + u1 - u0) * UNIT]\
                        .rearrange("p (u h f) -> p u h f", u=u1 - u0, h=HH)
                    step(v.reciprocal(rec[:, u0:u1, :], av[:, :, :, FD]))
                    settle()
                    half, i = divmod(u0, NI)
                    v.tensor_tensor(on[:, i:i + u1 - u0, half * HH * FD:(half + 1) * HH * FD].rearrange("p u (h f) -> p u h f", h=HH),
                                    av[:, :, :, 0:FD], wide(rec[:, u0:u1, :].unsqueeze(3), P, u1 - u0, HH, FD),
                                    ALU.mult).then_inc(dve_on, 1)

            def gate_scores(part, t0, t1):
                t = slice(t0, t1)
                v.wait_ge(act_lg, part + 1)
                step(v.tensor_scalar(r_s[:, t, :], r_s[:, t, :], 1.0, None, ALU.add))
                settle()
                step(v.reciprocal(r_s[:, t, :], r_s[:, t, :]))
                settle()
                step(v.tensor_scalar(r_s[:, t, :], r_s[:, t, :], route_scale[:, 0:1], None, ALU.mult))
                settle()

            def gate_parts(t0, t1):
                t, n = slice(t0, t1), t1 - t0
                step(v.tensor_tensor(r_o1[:, t, :], r_o1[:, t, :], wide(r_m[:, 0, t].unsqueeze(2), P, n, E0), ALU.mult))
                step(v.tensor_tensor(r_o2[:, t, :], r_o2[:, t, :], wide(r_m[:, 2, t].unsqueeze(2), P, n, E0), ALU.mult))
                settle()
                step(v.tensor_tensor(g3r[:, t, :], r_o1[:, t, :], r_o2[:, t, :], ALU.add))
                settle()
                step(v.tensor_copy(g3[:, t, 0, :], g3r[:, t, :]))
                settle()
                step(v.tensor_tensor(g3r[:, t, :], g3r[:, t, :], g3[:, t, 0, :], ALU.subtract))
                settle()
                step(v.tensor_copy(g3[:, t, 1, :], g3r[:, t, :]))
                settle()
                v.tensor_tensor(g3[:, t, 2, :], g3r[:, t, :], g3[:, t, 1, :], ALU.subtract).then_inc(dve_g, 1)

            def attention_out(b):
                v.wait_ge(pe_fc, b + 1)
                v.wait_ge(pool_xb, b + 1)
                v.tensor_tensor(x[:, b, :, :].rearrange("p i d -> p (i d)"), bank[0],
                                xb[:, b, :, :].rearrange("p i d -> p (i d)"), ALU.add).then_inc(dve_x, 1)
                v.wait_ge(dve_x, b + 1)
                layernorm_stats(b)

            for j in range(2 * NI):
                max_of(0, j)
            negate_max(0)
            for m in range(STEPS):
                b, j = divmod(m, NJ)
                if b >= 1 and j in (1, 2):
                    normalise(b - 1, UNIT_GROUPS[2 * j - 2:2 * j])
                if b + 1 < NB and j < 2 * NI:
                    max_of(b + 1, j)
                if b + 1 < NB and j == 2 * NI - 1:
                    negate_max(b + 1)
                if b >= 2:
                    tiles = ((b - 2) * NI, (b - 1) * NI)
                    if j == 3 and b < NB:
                        gate_scores(b - 2, *tiles)
                    if j == 4 and b < NB:
                        first_best(*tiles, r_s, 0, r_o1)
                    if j == 5 and b < NB:
                        second_best(*tiles)
                    if j == 8 and b < NB:
                        best_weights(*tiles)
                    if j == 9 and b < NB:
                        gate_parts(*tiles)
                if b >= 1 and j == 6:
                    attention_out(b - 1)
                if b >= 1 and j == 8:
                    layernorm_apply(1, b - 1)
            normalise(NB - 1, UNIT_GROUPS[2:])

            def copy_gates(b):
                v.wait_ge(pe_gT, b + 1)
                v.tensor_copy(gT3[:, b, :], bank[7].bitcast(BF16)[0:3 * E0, 0:SEQ]).then_inc(dve_gT, 1)

            for b in range(NB + 1):
                if b == 1:
                    layernorm_apply(1, NB - 1)
                if b < NB:
                    if b != EARLY:
                        copy_gates(b)
                    if b >= 2:
                        v.wait_ge(pe_y, b - 1)
                    for c in range(4):
                        n = 4 * b + c
                        v.wait_ge(act_h, 5 * b + c + 1)
                        v.wait_ge(pe_G, n + 1)
                        v.tensor_tensor(hg[:, b % 2, c, :], hraw[:, n % 2, :], bank[3 + n % 2], ALU.mult).then_inc(dve_hg, 1)
                        if b == 0 and c == 2:
                            attention_out(NB - 1)
                    if b == 1:
                        tiles = (EARLY * NI, NT)
                        gate_scores(EARLY, *tiles)
                        first_best(*tiles, r_s, 0, r_o1)
                        second_best(*tiles)
                        best_weights(*tiles)
                        gate_parts(*tiles)
                        copy_gates(EARLY)
                if b >= 1:
                    v.wait_ge(pe_y, b)
                    v.wait_ge(pool_xb, NB + b)
                    v.tensor_tensor(x[:, b - 1, :, :].rearrange("p i d -> p (i d)"), bank[5 + (b - 1) % 2],
                                    xb[:, b - 1, :, :].rearrange("p i d -> p (i d)"), ALU.add).then_inc(dve_x, 1)
                    v.wait_ge(dve_x, NB + b)
                    layernorm_stats(b - 1)
                if b >= 2:
                    layernorm_apply(2, b - 2)

            def softmax_shift(b):
                v.wait_ge(pe_s1, b + 1)
                if b >= 2:
                    v.wait_ge(act_s1, b - 1)
                s = sc[:, b % 2]
                step(v.tensor_tensor(s, bank[4 + b % 2][:, 0:NI * KEYS].rearrange("p (i k) -> p i k", i=NI),
                                     maskb[:, b, :].rearrange("p (i k) -> p i k", i=NI), ALU.add))
                settle()
                step(v.tensor_reduce(scm[:, b % 2, :], s, AX.X, ALU.max))
                settle()
                v.scalar_tensor_tensor(out=s, in0=wide(scm[:, b % 2, :].unsqueeze(2), P, NI, KEYS), scalar=-BIG / 2,
                                       in1=s, op0=ALU.max, op1=ALU.subtract).then_inc(dve_s1, 1)

            def low_weights(e):
                for c in range(2):
                    n = 2 * e + c
                    cols = slice(n * SEQ, (n + 1) * SEQ)
                    v.wait_ge(act_upT, 3 * e + c + 1)
                    v.tensor_tensor(uplo[:, cols], bank[UPT[c]], uphi[:, cols].bitcast(F32), ALU.subtract).then_inc(dve_upT, 1)

            def attention1_out(b):
                v.wait_ge(pe_o1, b + 1)
                o = ps[:, 6:8, 0:2 * (D + 1)].rearrange("p a (i d) -> p a i d", i=2)
                step(v.reciprocal(srec[:, b % 2, :].rearrange("p (a i) -> p a i", a=2), o[:, :, :, D]))
                settle()
                v.wait_ge(pool_xb, 2 * NB + b + 1)
                for t in range(NI):
                    ins = v.scalar_tensor_tensor(out=x[:, b, t, :], in0=o[:, t // 2, t % 2, 0:D], scalar=srec[:, b % 2, t:t + 1],
                                                 in1=xb[:, b, t, :], op0=ALU.mult, op1=ALU.add)
                    if t < NI - 1:
                        step(ins)
                ins.then_inc(dve_x, 1)
                settle()
                v.wait_ge(dve_x, 2 * NB + b + 1)
                layernorm_stats(b)

            low_weights(0)
            layernorm_apply(2, NB - 1)
            softmax_shift(0)
            low_weights(1)
            for b in range(1, NB):
                softmax_shift(b)
            for b in range(NB):
                if 1 <= b < NB - 1:
                    layernorm_apply(3, b - 1)
                if b < NB - 1:
                    low_weights(2 * b + 2)
                attention1_out(b)
                if b < NB - 1:
                    low_weights(2 * b + 3)
            for b in range(NB - 2, NB):
                layernorm_apply(3, b)

            v.wait_ge(pe_lg, EARLY + 2)
            lg = bank[4][:, 0:NT * E1].rearrange("p (i e) -> p i e", i=NT)
            step(v.tensor_reduce(r_m[:, 0, :], lg, AX.X, ALU.max))
            settle()
            v.tensor_tensor(r_a[:, :, :], lg, wide(r_m[:, 0, :].unsqueeze(2), P, NT, E1), ALU.subtract).then_inc(dve_g, 1)
            v.wait_ge(act_lg, EARLY + 2)
            first_best(0, NT, r_s, 0, r_o1)
            second_best(0, NT)
            best_weights(0, NT)
            v.tensor_tensor(cnt[:, 0:NT, :], r_o1[:, :, :], r_o2[:, :, :], ALU.add).then_inc(dve_cnt, 1)
            step(v.tensor_copy(onehot[:, 0, :, :], r_o1[:, :, :]))
            step(v.tensor_copy(onehot[:, 1, :, :], r_o2[:, :, :]))
            step(v.tensor_copy(wgt[:, 0, :], r_m[:, 0, :]))
            step(v.tensor_copy(wgt[:, 1, :], r_m[:, 2, :]))
            rank = bank[6][:, 0:(NT + 1) * E1].rearrange("p (t e) -> p t e", e=E1)
            v.wait_ge(pool_mask, 4)
            v.wait_ge(pe_rank, 1)
            step(v.tensor_copy(m_n[:, :], rank[:, NT, :]))
            settle()
            step(v.tensor_tensor(m_cmp[:, :, :], wide(m_n[:, :].unsqueeze(2), P, E1, NT), iota_n[:, :, :], ALU.is_gt))
            settle()
            step(v.tensor_reduce(m_nb[:, :], m_cmp[:, :, :], AX.X, ALU.add))
            settle()
            step(v.tensor_tensor(m_lt[:, :, :], wide(m_nb[:, :].unsqueeze(1), P, E1, E1), before[:, :, :], ALU.mult))
            settle()
            step(v.tensor_reduce(m_bb[:, :], m_lt[:, :, :], AX.X, ALU.add))
            settle()
            step(v.tensor_tensor(m_ce[:, :], m_bb[:, :], m_nb[:, :], ALU.add))
            step(v.scalar_tensor_tensor(out=m_at[:, :, :], in0=wide(m_bb[:, :].unsqueeze(1), P, NT, E1), scalar=float(P),
                                        in1=rank[:, 0:NT, :], op0=ALU.mult, op1=ALU.add))
            settle()
            step(v.tensor_tensor(m_pe[:, :, :, :], onehot[:, :, :, :], wide(m_at[:, :, :].unsqueeze(1), P, CH, NT, E1), ALU.mult))
            settle()
            step(v.tensor_reduce(m_pos[:, :].rearrange("p (c t) -> p c t", c=CH), m_pe[:, :, :, :], AX.X, ALU.add))
            settle()
            step(v.tensor_copy(m_posi[:, 0, :], m_pos[:, :]))
            settle()
            step(v.tensor_scalar(m_posi[:, 1, :], m_posi[:, 0, :], P - 1, None, ALU.bitwise_and))
            step(v.tensor_scalar(m_posi[:, 2, :], m_posi[:, 0, :], 7, None, ALU.logical_shift_right))
            settle()
            v.tensor_copy(m_posf[:, :, :], m_posi[:, 1:3, :]).then_inc(dve_posf, 1)
            v.wait_ge(dve_posf, 1)
            v.tensor_tensor(b_hot[:, :, :], wide(m_posf[:, 1, :].unsqueeze(2), P, CH * NT, NBLK),
                            wide(iota_k[:, :].unsqueeze(1), P, CH * NT, NBLK), ALU.is_equal).then_inc(dve_bhot, 1)
            v.wait_ge(dve_bhot, 1)
            v.tensor_tensor(b_val[:, 0:VAL_DVE, 0, :], b_hot[:, 0:VAL_DVE, :],
                            wide(tile_q[:, 0:VAL_DVE].unsqueeze(2), P, VAL_DVE, NBLK), ALU.mult).then_inc(dve_bval, 1)
            for n in range(HOT_DVE):
                v.tensor_scalar(r_hot[:, n, :], iota_r[:, :], m_posf[:, 0, n:n + 1], None, ALU.is_equal).then_inc(dve_rhot, 1)
            v.wait_ge(pe_inv, 1)
            step(v.tensor_copy(inv[:, :, :], bank[7][:, 0:2 * NBLK].rearrange("p (a k) -> p a k", a=2)))
            settle()
            q, u, row, t0, t1 = inv[:, 0, :], inv[:, 1, :], row_f[:, 0, :], row_f[:, 1, :], row_f[:, 2, :]
            step(v.scalar_tensor_tensor(out=row, in0=q, scalar=float(P), in1=u, op0=ALU.mult, op1=ALU.add))
            step(v.tensor_scalar(t0, q, float(NT), -float(ROWS), ALU.is_ge, ALU.mult))
            step(v.scalar_tensor_tensor(out=t1, in0=u, scalar=0.0, in1=pad_row[:, :], op0=ALU.is_equal, op1=ALU.mult))
            settle()
            step(v.scalar_tensor_tensor(out=t0, in0=row, scalar=-1.0, in1=t0, op0=ALU.add, op1=ALU.add))
            step(v.scalar_tensor_tensor(out=t1, in0=row, scalar=-1.0, in1=t1, op0=ALU.add, op1=ALU.add))
            settle()
            step(v.tensor_scalar(src_row[:, :], t0, 0.0, None, ALU.max))
            settle()
            v.tensor_copy(dst_row[:, :], t1).then_inc(dve_idx, 1)
            step(v.tensor_tensor(m_k[:, :, :], wide(m_ce[0:1, :].unsqueeze(1), 1, NBLK, E1),
                                 wide(iota_k[0:1, :].unsqueeze(2), 1, NBLK, E1), ALU.is_le))
            settle()
            step(v.tensor_reduce(m_kf[:, :], m_k[:, :, :], AX.X, ALU.add))
            settle()
            step(v.tensor_scalar(m_kf[:, :], m_kf[:, :], float(E1 - 1), None, ALU.min))
            settle()
            step(v.tensor_copy(blk_e[:, :], m_kf[:, :]))
            end = NBLK - PACK + 3
            body = slice(LOOP0, end)
            step(v.tensor_copy(m_pack[:, body], m_kf[:, LOOP0 - 2:end - 2]))
            for j in range(1, PACK):
                settle()
                step(v.scalar_tensor_tensor(out=m_pack[:, body], in0=m_kf[:, LOOP0 - 2 + j:end - 2 + j],
                                            scalar=float(E1 ** j), in1=m_pack[:, body], op0=ALU.mult, op1=ALU.add))
            settle()
            v.tensor_copy(blk_es[:, body], m_pack[:, body]).then_inc(dve_hot, 1)

            def split_xg(k, s):
                v.wait_ge(pe_xg, k + 1)
                v.tensor_copy(xghi[:, s, :], bank[7][:, 0:P]).then_inc(dve_xg, 1)
                v.wait_ge(dve_xg, 2 * k + 1)
                v.tensor_tensor(xglo[:, s, :], bank[7][:, 0:P], xghi[:, s, :].bitcast(F32), ALU.subtract).then_inc(dve_xg, 1)

            def gate_up(k, s, first=False):
                v.wait_ge(act_gl, k + 1)
                if not first:
                    v.wait_ge(pe_hT, k - 1)
                v.tensor_tensor(hh[:, s, :], gl[:, s, :], bank[2 + s], ALU.mult).then_inc(dve_h, 1)

            def copy_y(k, s, first=False):
                v.wait_ge(pe_y1, k + 1)
                if not first:
                    v.wait_ge(scattered[s], 8 * k - 8 * s)
                v.tensor_copy(yb[:, s, :], bank[6][:, 0:D]).then_inc(dve_y1, 1)

            def block_step(k, s, first=False):
                split_xg(k + 1, 1 - s)
                copy_y(k - 2, s, first)
                gate_up(k, s)

            split_xg(0, 0)
            for k in range(2):
                split_xg(k + 1, 1 - k)
                gate_up(k, k, first=True)
            for k in range(2, LOOP0):
                block_step(k, k % 2, first=True)
            with v.Fori(LOOP0, LOOP1, UNROLL) as k0:
                for j in range(UNROLL):
                    block_step(k0 + j, j % 2)
            for k in range(LOOP1, NBLK - 1):
                block_step(k, k % 2)
            gate_up(NBLK - 1, (NBLK - 1) % 2)
            for k in range(NBLK - 3, NBLK):
                copy_y(k, k % 2)
            for b in range(NB):
                v.wait_ge(y_loaded[b], 32)
                for i in range(NI):
                    v.scalar_tensor_tensor(out=x[:, b, i, :], in0=yc[:, b, 0, i, :], scalar=wgt[:, 0, b * NI + i:b * NI + i + 1],
                                           in1=x[:, b, i, :], op0=ALU.mult, op1=ALU.add).then_inc(dve_y, 1)
            b = NB - 1
            v.wait_ge(dve_y, NB * NI)
            v.wait_ge(act_y, NB * NI)
            v.tensor_tensor(x[:, b, :, :], x[:, b, :, :], yc[:, b, 1, :, :], ALU.add).then_inc(dve_out, 1)

        @block.scalar
        def _(s):
            def copy_xT(k, b, src):
                s.wait_ge(pe_xT, k * NB + b + 1)
                s.activation(xnT[:, b, :], src, ACT.Copy).then_inc(xT_ready, 1)

            for half in range(2):
                s.wait_ge(pe_kz, half + 1)
                s.wait_ge(dve_fmT, 1)
                s.activation(kf[:, half, :], bank[2 + half][:, 0:NB * KEYS], ACT.Exp, bias=fmT[:, HD:HD + 1]).then_inc(act_kf, 1)
            copy_xT(0, 0, bank[4])
            for b in range(NB):
                if b + 1 < NB:
                    copy_xT(0, b + 1, bank[4 + (b + 1) % 2])
                for half in range(2):
                    n = 2 * b + half
                    s.wait_ge(pe_z, n + 1)
                    if b >= 1:
                        s.wait_ge(dve_q, n - 1)
                    s.activation(qhi[:, b, half, :], bank[half], ACT.Exp, bias=fmT[:, HD:HD + 1]).then_inc(act_qhi, 1)
                    s.activation(qf[:, half, :], bank[half], ACT.Exp, bias=fmT[:, HD:HD + 1]).then_inc(act_q, 1)
                if b == 0:
                    s.wait_ge(pe_wT, 2)
                    s.activation(wT[:, :, :].rearrange("p n d -> p (n d)"), bank[2][:, 0:3 * D], ACT.Copy).then_inc(act_wT, 1)
                    s.activation(fcT[:, :, :].rearrange("p n d -> p (n d)"), bank[3][:, 0:2 * D], ACT.Copy).then_inc(act_wT, 1)
                    s.activation(gate1[:, :], bank[3][:, 2 * D:2 * D + E1], ACT.Copy).then_inc(act_wT, 1)
                elif b == 1:
                    s.wait_ge(pe_kv, 2)
                    s.wait_ge(ld_w, 16 * N_W)
                    s.activation(KT[:, :], bank[2][:, 0:NB * KEYS], ACT.Identity, bias=bqkv[:, 1:2]).then_inc(act_kv, 1)
                    s.activation(VT[:, :], bank[3][:, 0:NB * KEYS], ACT.Identity, bias=bqkv[:, 2:3]).then_inc(act_kv, 1)
                elif b == 2:
                    s.wait_ge(pe_ak, 2)
                    s.activation(keyA[:, :], bank[2][:, 0:NB * KEYS], ACT.Copy).then_inc(act_ak, 1)
                    s.activation(keyc[:, :], bank[3][:, 0:NB * KEYS], ACT.Copy).then_inc(act_ak, 1)
                else:
                    s.wait_ge(pe_ak, 3)
                    s.activation(Vo[:, :, 0:D], bank[2][0:KEYS, :].rearrange("k (b d) -> k b d", b=NB), ACT.Copy).then_inc(act_ak, 1)
            for n in range(2 * NB):
                s.wait_ge(pe_vt, n + 1)
                if n == 0:
                    s.wait_ge(pool_ind, 7)
                for c0, c1, bk in ((0, 4, 2 - 2 * (n % 2)), (4, NC, 3 - 2 * (n % 2))):
                    rows = chunk_rows(c1 - 1)
                    s.activation(Vx[0:rows, n, c0:c1, :, 0:FD],
                                 bank[bk][0:rows, 0:(c1 - c0) * P].rearrange("r (c h f) -> r c h f", h=HH, f=FD),
                                 ACT.Copy).then_inc(act_vx, 1)
            def copy_nmT(b):
                s.wait_ge(pe_nmT, b + 1)
                s.activation(nmT[:, b % 2, :], bank[0].bitcast(BF16)[0:3 * HEADS, 0:SEQ], ACT.Copy).then_inc(act_nmT, 1)

            def copy_onT(b, pair):
                s.wait_ge(pe_onT, b * NI + 2 * pair + 2)
                s.activation(onT[:, 2 * pair:2 * pair + 2, :, :].rearrange("p i a t -> p (i a t)"),
                             bank[0], ACT.Copy).then_inc(act_onT, 2)

            def gate_exp(part, t0, t1):
                s.wait_ge(pe_lg, part + 1)
                s.activation(r_s[:, t0:t1, :], bank[0][:, t0 * E0:t1 * E0].rearrange("p (i e) -> p i e", i=t1 - t0),
                             ACT.Exp, scale=-1.0).then_inc(act_lg, 1)

            copy_nmT(0)
            for m in range(STEPS):
                b, j = divmod(m, NJ)
                if b < NB:
                    rows = chunk_rows(j % NC)
                    s.wait_ge(pe_sc, m + 1)
                    if m >= RING:
                        s.wait_ge(pe_av, m - RING + 1)
                    s.activation(ex[0:rows, m % RING, :], bank[1 + m % 2][0:rows, :], ACT.Exp, scale=SCALE).then_inc(act_ex, 1)
                if b >= 2 and j == 0:
                    copy_xT(1, b - 2, bank[0])
                if 2 <= b < NB and j == 2:
                    gate_exp(b - 2, (b - 2) * NI, (b - 1) * NI)
                if 1 <= b < NB and j in (3, 4):
                    copy_onT(b - 1, j - 3)
                if b + 1 < NB and j == NJ - 1:
                    copy_nmT(b + 1)
            s.wait_ge(ld_small, 16 * N_SMALL)
            for b in range(NB):
                for c in range(5):
                    n = 5 * b + c
                    s.wait_ge(pe_h, n + 1)
                    if c < 4:
                        m = 4 * b + c
                        if m >= 2:
                            s.wait_ge(dve_hg, m - 1)
                        s.activation(hraw[:, m % 2, :], bank[1 + n % 2], ACT.Gelu, bias=b1[:, c:c + 1]).then_inc(act_h, 1)
                    else:
                        if b >= 2:
                            s.wait_ge(pe_y, b - 1)
                        s.activation(hs[:, b % 2, :], bank[1 + n % 2][0:H0, :], ACT.Gelu, bias=bs1[:, 0:1]).then_inc(act_h, 1)
                    if b == 0 and c in (1, 2):
                        copy_onT(NB - 1, c - 1)
                    if b == 1 and c == 1:
                        copy_xT(1, NB - 1, bank[0])
                    if b == 1 and c == 2:
                        gate_exp(EARLY, EARLY * NI, NT)
            def copy_weights(e):
                for c in range(3):
                    s.wait_ge(pe_upT, 3 * e + c + 1)
                    cols = slice((2 * e + c) * SEQ, (2 * e + c + 1) * SEQ)
                    dst = uphi[:, cols] if c < 2 else dnT[:, e * F1:(e + 1) * F1]
                    s.activation(dst, bank[UPT[c]], ACT.Copy).then_inc(act_upT, 1)

            def softmax_exp(b):
                s.wait_ge(dve_s1, b + 1)
                s.activation(pr[:, b], sc[:, b % 2], ACT.Exp, scale=-SCALE).then_inc(act_s1, 1)

            copy_xT(2, 0, bank[XT2[0]])
            copy_xT(2, 1, bank[XT2[1]])
            copy_weights(0)
            copy_xT(2, 2, bank[XT2[2]])
            copy_weights(1)
            copy_xT(2, 3, bank[XT2[3]])
            for b in range(NB):
                softmax_exp(b)
            def copy_probs(b):
                s.wait_ge(pe_pT, b + 1)
                if b >= 2:
                    s.wait_ge(pe_o1, b - 1)
                s.activation(prT[:, b % 2, :], bank[1][0:KEYS, :], ACT.Copy).then_inc(act_pT, 1)

            copy_probs(0)
            for b in range(NB):
                if b < NB - 1:
                    copy_weights(2 * b + 2)
                    copy_probs(b + 1)
                if b >= 1:
                    copy_xT(3, b - 1, bank[XT3[b - 1]])
                if b < NB - 1:
                    copy_weights(2 * b + 3)
            copy_xT(3, NB - 1, bank[XT3[NB - 1]])
            s.wait_ge(dve_g, EARLY + 2)
            s.activation(r_s[:, :, :], r_a[:, :, :], ACT.Exp).then_inc(act_lg, 1)

            s.wait_ge(dve_bhot, 1)
            s.activation(b_val[:, :, 1, :], b_hot[:, :, :], ACT.Copy, scale=p_one[:, 0:1]).then_inc(act_bval, 1)

            def gelu(k, s_, first=False):
                s.wait_ge(pe_up, k + 1)
                if not first:
                    s.wait_ge(dve_h, k - 1)
                s.activation(gl[:, s_, :], bank[s_], ACT.Gelu).then_inc(act_gl, 1)

            def copy_hT(k, s_, first=False):
                s.wait_ge(pe_hT, k + 1)
                if not first:
                    s.wait_ge(pe_y1, k - 1)
                s.activation(hhT[:, s_, :, :].rearrange("p c t -> p (c t)"), bank[4], ACT.Copy).then_inc(act_hT, 1)

            gelu(0, 0, first=True)
            for k in range(1, LOOP0):
                gelu(k, k % 2, first=k < 2)
                copy_hT(k - 1, (k - 1) % 2, first=k < 3)
            with s.Fori(LOOP0, LOOP1, UNROLL) as k0:
                for j in range(UNROLL):
                    gelu(k0 + j, j % 2)
                    copy_hT(k0 + j - 1, 1 - j % 2)
            for k in range(LOOP1, NBLK):
                gelu(k, k % 2)
                copy_hT(k - 1, (k - 1) % 2)
            copy_hT(NBLK - 1, (NBLK - 1) % 2)
            s.wait_ge(dve_idx, 1)
            for b in range(NB):
                s.wait_ge(y_loaded[b], 32)
                for i in range(NI):
                    s.activation(yc[:, b, 1, i, :], yc[:, b, 1, i, :], ACT.Copy,
                                 scale=wgt[:, 1, b * NI + i:b * NI + i + 1]).then_inc(act_y, 1)

        @block.tensor
        def _(pe):
            def mm(out_, lhsT, rhs, start=True, stop=True):
                return pe.matmul(out_, lhsT, rhs, start=start, stop=stop, skip_group_check=True)

            def transpose_xn(k, b, dst):
                for i in range(NI):
                    pe.wait_ge(dve_xn, (k * NB + b) * NI + i + 1)
                    ins = pe.transpose(dst[:, i * P:(i + 1) * P], xn[:, b, i, :], ident[:, :])
                ins.then_inc(pe_xT, 1)

            pe.wait_ge(pool_ident, 1)
            pe.wait_ge(ld_ctx, 16)
            for b in range(NB):
                ins = pe.transpose(bank[0][:, b * KEYS:(b + 1) * KEYS], ctx_tok[:, b, :], ident[0:KEYS, 0:KEYS])
            ins.then_inc(pe_ctxT, 1)
            pe.wait_ge(ld_fm, 16 * N_FM)
            pe.wait_ge(pool_mask, 2)
            pe.wait_ge(dve_c, 1)
            mm(bank[1][:, 0:HD], fmrep[:, :, :].rearrange("e h d -> e (h d)"), ident[0:HD, 0:HD])
            mm(bank[1][:, HD:HD + 1], isgn[:, :, :, :].rearrange("e h s d -> e (h s d)"), fm[:, HD:HD + 1]).then_inc(pe_fm, 1)
            pe.wait_ge(dve_ctxT, 1)
            pe.wait_ge(dve_Wz, 4)
            for half in range(2):
                mm(bank[2 + half][:, 0:NB * KEYS], Wz[:, half].rearrange("p h s d -> p (h s d)"), ctxT[:, :]).then_inc(pe_kz, 1)
            def fold(b):
                if b == 0:
                    pe.wait_ge(ld_w, 16 * N_W)
                    pe.wait_ge(act_kf, 2)
                    for n in range(3):
                        ins = pe.transpose(bank[2][:, n * D:(n + 1) * D], wnat[:, n + 1, :], ident[:, :])
                    ins.then_inc(pe_wT, 1)
                    for n in range(2):
                        pe.transpose(bank[3][:, n * D:(n + 1) * D], fcn[:, n, :], ident[:, :])
                    pe.transpose(bank[3][:, 2 * D:2 * D + E1], gate1n[:, :], ident[0:E1, 0:E1]).then_inc(pe_wT, 1)
                elif b == 1:
                    pe.wait_ge(act_wT, 3)
                    for n in range(2):
                        mm(bank[2 + n][:, 0:NB * KEYS], wT[:, n, :], ctxT[:, :]).then_inc(pe_kv, 1)
                elif b == 2:
                    pe.wait_ge(act_kv, 2)
                    mm(bank[2][:, 0:NB * KEYS], wnat[:, 0, :], KT[:, :]).then_inc(pe_ak, 1)
                    mm(bank[3][:, 0:NB * KEYS], wide(bqkv[:, 0:1], P, P), KT[:, :]).then_inc(pe_ak, 1)
                else:
                    pe.wait_ge(act_ak, 2)
                    for i in range(NB):
                        ins = mm(bank[2][0:KEYS, i * D:(i + 1) * D], VT[:, i * KEYS:(i + 1) * KEYS], wT[:, 2, :])
                    ins.then_inc(pe_ak, 1)

            transpose_xn(0, 0, bank[4])
            for b in range(NB):
                pe.wait_ge(xT_ready, b + 1)
                if b + 1 < NB:
                    transpose_xn(0, b + 1, bank[4 + (b + 1) % 2])
                for half in range(2):
                    n = 2 * b + half
                    if b >= 1:
                        pe.wait_ge(act_q, n - 1)
                    mm(bank[half], Wz[:, half].rearrange("p h s d -> p (h s d)"), xnT[:, b, :]).then_inc(pe_z, 1)
                fold(b)
            pe.wait_ge(pool_ind, 6)
            for half in range(2):
                for c in range(NC):
                    ins = pe.transpose(bank[6 + half].bitcast(BF16)[0:3 * HEADS, c * P:(c + 1) * P],
                                       indw[:, half, c, :, :].rearrange("p a h -> p (a h)"), identb[:, :])
                ins.then_inc(pe_kz, 1)
            def max_job(b, j):
                i, half = divmod(j, 2)
                n = b * 2 * NI + j
                pair = max_banks(b, j)
                if b == 0 and n >= 2:
                    pe.wait_ge(dve_max, n - 1)
                elif b >= 1:
                    pe.wait_ge(dve_max, n)
                for a in range(2):
                    ins = mm(bank[pair + a][:, 0:HK // 2], qhi[:, b, half, i * P:(i + 1) * P],
                             kbhi[:, b, half, a * (HK // 2):(a + 1) * (HK // 2)])
                ins.then_inc(pe_max, 1)

            def turn_nm(b):
                pe.wait_ge(dve_nm, b + 1)
                if b >= 2:
                    pe.wait_ge(dve_x, b - 1)
                for i in range(NI):
                    ins = pe.transpose(bank[0].bitcast(BF16)[0:3 * HEADS, i * P:(i + 1) * P],
                                       nm[:, b % 2, i].rearrange("p a h -> p (a h)"), identb[:, :])
                ins.then_inc(pe_nmT, 1)

            def score_job(m):
                b, j = divmod(m, NJ)
                half, c = divmod(j, NC)
                rows = chunk_rows(c)
                cols = slice(c * P, c * P + rows)
                o = bank[1 + m % 2][0:rows, :]
                if j == 0:
                    pe.wait_ge(act_nmT, b + 1)
                if m >= 2:
                    pe.wait_ge(act_ex, m - 1)
                mm(o, sel[:, half, cols], nmT[:, b % 2, :], True, False)
                mm(o, kbhi[:, b, half, cols], qhi[:, b, half, :], False, False)
                mm(o, kblo[:, b, half, cols], qhi[:, b, half, :], False, False)
                mm(o, kbhi[:, b, half, cols], qlo[:, b, half, :], False, True).then_inc(pe_sc, 1)

            def gate_logits(b, last):
                pe.wait_ge(ld_small, 16 * N_SMALL)
                pe.wait_ge(xT_ready, NB + b + 1)
                for i in range(NI):
                    at = (b * NI + i) * E0
                    ins = mm(bank[0][:, at:at + E0], xnT[:, b, i * P:(i + 1) * P], gate0[:, :])
                if last:
                    ins.then_inc(pe_lg, 1)

            def turn_on(b, pair):
                pe.wait_ge(dve_on, len(UNIT_GROUPS) * (b + 1))
                if pair == 1:
                    pe.wait_ge(act_onT, b * NI + 2)
                elif 1 <= b < NB - 1:
                    pe.wait_ge(act_lg, b)
                elif b == 0:
                    pe.wait_ge(act_nmT, 2)
                else:
                    pe.wait_ge(xT_ready, 2 * NB - 1)
                for i in range(2):
                    for a in range(2):
                        at = (2 * i + a) * P
                        ins = pe.transpose(bank[0][:, at:at + P], on[:, 2 * pair + i, a * P:(a + 1) * P], ident[:, :])
                ins.then_inc(pe_onT, 2)

            def project(b):
                pe.wait_ge(act_onT, (b + 1) * NI)
                for i in range(NI):
                    for a in range(2):
                        ins = mm(bank[0][:, i * D:(i + 1) * D], onT[:, i, a, :], fcT[:, a, :], a == 0, a == 1)
                ins.then_inc(pe_fc, 1)

            def value_job(n):
                b, j = divmod(n, NJ)
                half, c = divmod(j, NC)
                rows = chunk_rows(c)
                h0, h1 = chunk_heads(c)
                pe.wait_ge(act_ex, n + 1)
                for i in range(NI):
                    u = half * NI + i
                    if c == 0 and u in (0, 3, 6) and b >= 1:
                        pe.wait_ge(dve_on, len(UNIT_GROUPS) * (b - 1) + {0: 1, 3: 3, 6: 4}[u])
                    at = (u % 3) * UNIT + h0 * (FD + 1)
                    ins = mm(bank[AV_BANKS[u // 3]][:, at:at + (h1 - h0) * (FD + 1)],
                             ex[0:rows, n % RING, i * P:(i + 1) * P],
                             Vx[0:rows, 2 * b + half, c, h0:h1, :].rearrange("r h f -> r (h f)"),
                             start=c == 0 and u in (0, 3, 6), stop=False)
                ins.then_inc(pe_av, 1)

            pe.wait_ge(act_ak, 3)
            pe.wait_ge(act_q, 2 * NB)
            pe.wait_ge(dve_q, 2 * NB)
            pe.wait_ge(dve_Wz, 6)
            for n in range(2 * NB):
                b, half = divmod(n, 2)
                pe.wait_ge(dve_kb, n + 1)
                pe.wait_ge(pool_kbf, n + 1)
                if n >= 2:
                    pe.wait_ge(act_vx, 2 * (n - 1))
                for c in range(NC):
                    rows = chunk_rows(c)
                    bk, at = (2 - 2 * (n % 2), c * P) if c < 4 else (3 - 2 * (n % 2), 0)
                    ins = pe.transpose(bank[bk][0:rows, at:at + P], kbf[:, b, half, c * P:c * P + rows], ident[:, :])
                ins.then_inc(pe_vt, 1)
                max_job(0, n)
            pe.wait_ge(act_vx, 4 * NB)
            pe.wait_ge(pool_kb, 2 * NB)
            turn_nm(0)
            for m in range(STEPS):
                b, j = divmod(m, NJ)
                for n in chunks_of_step(m):
                    value_job(n)
                if b < NB:
                    score_job(m)
                if b + 1 < NB and j < 2 * NI:
                    max_job(b + 1, j)
                if b >= 2 and j == 0:
                    pe.wait_ge(act_nmT, min(b + 1, NB))
                    pe.wait_ge(dve_x, b - 1)
                    transpose_xn(1, b - 2, bank[0])
                if 2 <= b < NB and j == 2:
                    gate_logits(b - 2, True)
                if 1 <= b < NB and j in (3, 4):
                    turn_on(b - 1, j - 3)
                if 1 <= b < NB and j == 5:
                    project(b - 1)
                if b + 1 < NB and j == NJ - 1:
                    turn_nm(b + 1)

            def turn_gates(b):
                pe.wait_ge(dve_g, min(b, EARLY) + 1)
                if b == 0:
                    pe.wait_ge(dve_on, len(UNIT_GROUPS) * NB)
                else:
                    pe.wait_ge(dve_gT, b)
                for i in range(NI):
                    ins = pe.transpose(bank[7].bitcast(BF16)[0:3 * E0, i * P:(i + 1) * P],
                                       g3[:, b * NI + i].rearrange("p a e -> p (a e)"), identb[:, :])
                ins.then_inc(pe_gT, 1)

            def hidden(b, c):
                n = 5 * b + c
                if n >= 2:
                    pe.wait_ge(act_h, n - 1)
                if c < 4:
                    mm(bank[1 + n % 2], W1[:, c * P:(c + 1) * P], xnT[:, b, :]).then_inc(pe_h, 1)
                else:
                    mm(bank[1 + n % 2][0:H0, :], Ws1[:, :], xnT[:, b, :]).then_inc(pe_h, 1)

            def spread_gates(b, c):
                m = 4 * b + c
                if c == 0:
                    pe.wait_ge(dve_gT, b + 1)
                if m >= 2:
                    pe.wait_ge(dve_hg, m - 1)
                mm(bank[3 + m % 2], selG[:, c, :], gT3[:, b, :]).then_inc(pe_G, 1)

            pe.wait_ge(pool_mask, 3)
            pe.wait_ge(act_ex, NB * NJ)
            for b in range(NB + 1):
                if b < NB:
                    for c in range(5):
                        hidden(b, c)
                        if c == 1:
                            turn_gates(b)
                        if c == 2:
                            spread_gates(b, 0)
                        if c >= 2:
                            spread_gates(b, c - 1)
                        if b == 0 and c in (1, 2):
                            turn_on(NB - 1, c - 1)
                        if b == 0 and c == 3:
                            project(NB - 1)
                        if b == 1 and c == 1:
                            pe.wait_ge(dve_x, NB)
                            transpose_xn(1, NB - 1, bank[0])
                        if b == 1 and c == 2:
                            pe.wait_ge(xT_ready, 2 * NB)
                            for e in range(EARLY, NB):
                                gate_logits(e, e == NB - 1)
                if b == NB:
                    pe.wait_ge(act_lg, EARLY + 1)
                    transpose_xn(2, 0, bank[XT2[0]])
                if b >= 1:
                    p = b - 1
                    pe.wait_ge(dve_hg, 4 * b)
                    pe.wait_ge(act_h, 5 * b)
                    if p >= 2:
                        pe.wait_ge(dve_x, NB + p - 1)
                    for i in range(NI):
                        o = bank[5 + p % 2][:, i * D:(i + 1) * D]
                        tok = slice(i * P, (i + 1) * P)
                        for c in range(4):
                            mm(o, hg[:, p % 2, c, tok], W2[:, c, :], c == 0, False)
                        mm(o, hs[:, p % 2, tok], Ws2[:, :], False, False)
                        for t in range(3):
                            ins = mm(o, gT3[:, p, tok], b2s[:, t, :], False, t == 2)
                    ins.then_inc(pe_y, 1)

            def scores1(b):
                pe.wait_ge(xT_ready, 2 * NB + b + 1)
                if b >= 2:
                    pe.wait_ge(dve_s1, b - 1)
                for i in range(NI):
                    o = bank[4 + b % 2][:, i * KEYS:(i + 1) * KEYS]
                    ins = mm(o, xnT[:, b, i * P:(i + 1) * P], keyA[:, b * KEYS:(b + 1) * KEYS])
                ins.then_inc(pe_s1, 1)

            def turn_weights(e):
                pe.wait_ge(ld_up[e], 16)
                pe.wait_ge(ld_dn[e], 16)
                if e == 0:
                    pe.wait_ge(xT_ready, 2 * NB + 1)
                    pe.wait_ge(act_h, 5 * NB)
                    pe.wait_ge(dve_hg, 4 * NB)
                for c in range(3):
                    if e >= 1:
                        if c == 2:
                            pe.wait_ge(act_upT, 3 * e)
                        else:
                            pe.wait_ge(dve_upT, 2 * (e - 1) + c + 1)
                    for j in range(4):
                        src = upn[:, e % WR, 4 * c + j, :] if c < 2 else dnn[:, e % WR, j * P:(j + 1) * P]
                        ins = pe.transpose(bank[UPT[c]][:, j * P:(j + 1) * P], src, ident[:, :])
                    ins.then_inc(pe_upT, 1)

            def turn_probs(b):
                pe.wait_ge(act_s1, b + 1)
                if b >= 1:
                    pe.wait_ge(act_pT, b)
                else:
                    pe.wait_ge(xT_ready, 3 * NB)
                for i in range(NI):
                    ins = pe.transpose(bank[1][0:KEYS, i * P:(i + 1) * P], pr[:, b, i, :], ident[:, :])
                ins.then_inc(pe_pT, 1)

            def values1(b):
                pe.wait_ge(act_pT, b + 1)
                pe.wait_ge(dve_x, 2 * NB + b)
                for t in range(NI):
                    pair, i = divmod(t, 2)
                    ins = mm(bank[6 + pair][:, i * (D + 1):(i + 1) * (D + 1)],
                             prT[:, b % 2, t * P:(t + 1) * P], Vo[:, b, :])
                ins.then_inc(pe_o1, 1)

            def turn_xn3(b):
                if b == 0:
                    pe.wait_ge(dve_s1, NB)
                elif b < NB - 1:
                    pe.wait_ge(xT_ready, 3 * NB + b)
                else:
                    pe.wait_ge(act_pT, NB)
                transpose_xn(3, b, bank[XT3[b]])

            def expert_logits(b):
                pe.wait_ge(xT_ready, 3 * NB + b + 1)
                for i in range(NI):
                    at = (b * NI + i) * E1
                    ins = mm(bank[4][:, at:at + E1], xnT[:, b, i * P:(i + 1) * P], gate1[:, :])
                if b == NB - 1:
                    ins.then_inc(pe_lg, 1)

            transpose_xn(2, 1, bank[XT2[1]])
            turn_weights(0)
            scores1(0)
            transpose_xn(2, 2, bank[XT2[2]])
            turn_weights(1)
            scores1(1)
            transpose_xn(2, 3, bank[XT2[3]])
            scores1(2)
            scores1(3)
            turn_probs(0)
            for b in range(NB):
                if b == 0:
                    turn_weights(2)
                values1(b)
                if 1 <= b < NB - 1:
                    turn_weights(2 * b + 2)
                if b < NB - 1:
                    turn_probs(b + 1)
                if b >= 1:
                    turn_xn3(b - 1)
                if b < NB - 1:
                    turn_weights(2 * b + 3)
                else:
                    turn_xn3(NB - 1)
                if b >= 1:
                    expert_logits(b - 1)
            expert_logits(NB - 1)

            pe.wait_ge(dve_x, 3 * NB)
            pe.wait_ge(pool_mask, 4)
            pe.wait_ge(dve_cnt, 1)
            rank = bank[6][:, 0:(NT + 1) * E1]
            mm(rank, lower[:, :], cnt[:, :, :].rearrange("p t e -> p (t e)"), True, False)
            for t in range(NT):
                left = NT - t
                ins = mm(rank[:, (t + 1) * E1:].rearrange("p (t e) -> p t e", e=E1), onesb[:, :],
                         wide(cnt[:, t:t + 1, :], P, left, E1), False, t == NT - 1)
            ins.then_inc(pe_rank, 1)
            pe.wait_ge(dve_bval, 1)
            pe.wait_ge(pool_bval, 1)
            pe.wait_ge(act_bval, 1)
            for n in range(CH * NT):
                if n < HOT_DVE:
                    pe.wait_ge(dve_rhot, n + 1)
                else:
                    pe.wait_ge(pool_rhot, n - HOT_DVE + 1)
                ins = mm(bank[7][:, 0:2 * NBLK], r_hot[:, n, :], b_val[:, n, :, :].rearrange("p a k -> p (a k)"),
                         n == 0, n == CH * NT - 1)
            ins.then_inc(pe_inv, 1)

            def turn_xg(k, r, first=False):
                pe.wait_ge(gathered[r], (k - r) * (16 // XR) + 16)
                if not first:
                    pe.wait_ge(dve_xg, 2 * k)
                pe.transpose(bank[7][:, 0:P], xg[:, r, :], ident[:, :]).then_inc(pe_xg, 1)

            def experts(k):
                packed = pe.value_load(blk_es[0:1, bass.ds(k, 1)], min_val=0, max_val=E1 ** PACK - 1)
                return [((packed // E1 ** j) % E1) * F1 for j in range(PACK)]

            def up(k, s, e, first=False):
                pe.wait_ge(dve_xg, 2 * k + 2)
                if not first:
                    pe.wait_ge(dve_h, k - 1)
                for a in range(2):
                    o = bank[2 * a + s]
                    cols = bass.ds(e * 2 + a * F1, F1)
                    mm(o, xghi[:, s, :], uphi[:, cols], True, False)
                    mm(o, xghi[:, s, :], uplo[:, cols], False, False)
                    ins = mm(o, xglo[:, s, :], uphi[:, cols], False, True)
                ins.then_inc(pe_up, 1)

            def turn_h(k, s, first=False):
                pe.wait_ge(dve_h, k + 1)
                if not first:
                    pe.wait_ge(act_hT, k)
                for c in range(4):
                    ins = pe.transpose(bank[4][:, c * P:(c + 1) * P], hh[:, s, c * P:(c + 1) * P], ident[:, :])
                ins.then_inc(pe_hT, 1)

            def down(k, s, e, first=False):
                pe.wait_ge(act_hT, k + 1)
                if not first:
                    pe.wait_ge(dve_y1, k)
                for c in range(4):
                    ins = mm(bank[6][:, 0:D], hhT[:, s, c, :], dnT[:, bass.ds(e + c * P, P)], c == 0, c == 3)
                ins.then_inc(pe_y1, 1)

            def block_step(k, j, e, e2, first=False):
                s = j % 2
                up(k, s, e)
                turn_xg(k + 1, (j + 1) % XR)
                down(k - 2, s, e2, first)
                turn_h(k - 1, 1 - s)

            pe.wait_ge(dve_upT, 2 * E1)
            turn_xg(0, 0, first=True)
            turn_xg(1, 1)
            pe.wait_ge(dve_hot, 1)
            e = [pe.value_load(blk_e[0:1, 0:1], min_val=0, max_val=E1 - 1) * F1]
            up(0, 0, e[0], first=True)
            turn_xg(2, 2)
            e.append(pe.value_load(blk_e[0:1, 1:2], min_val=0, max_val=E1 - 1) * F1)
            up(1, 1, e[1], first=True)
            turn_h(0, 0, first=True)
            e += experts(LOOP0)
            for k in range(2, LOOP0):
                block_step(k, k, e[k], e[k - 2], first=k == 2)
            with pe.Fori(LOOP0, LOOP1, UNROLL) as k0:
                e = []
                for j in range(UNROLL + 2):
                    if j % PACK == 0:
                        columns = experts(k0 + j)
                    e.append(pe.snap(columns[j % PACK]))
                    if j >= 2:
                        block_step(k0 + j - 2, LOOP0 + j - 2, e[j], e[j - 2])
            last = NBLK - 1
            e = experts(last - PACK + 3)
            for k in range(LOOP1, last):
                block_step(k, k, e[k - last - 1], e[k - last - 3])
            up(last, last % 2, e[-1])
            turn_h(last - 1, 1 - last % 2)
            down(last - 2, last % 2, e[-3])
            turn_h(last, last % 2)
            down(last - 1, 1 - last % 2, e[-2])
            down(last, last % 2, e[-1])


_INS = ["x", "ctx_1024", "mask_BxSxS2_ik0", "L0_xattn_fm_w", "L0_xattn_fm_b", "L0_xattn_fc_w", "L0_xattn_fc_b",
        "L0_ffn_gate_W", "L0_ffn_W1", "L0_ffn_b1", "L0_ffn_W2", "L0_ffn_b2", "L0_ffn_Ws1", "L0_ffn_bs1", "L0_ffn_Ws2",
        "L0_ffn_bs2", "L0_ffn_route_scale", "L1_xattn_Wq", "L1_xattn_bq", "L1_xattn_Wk", "L1_xattn_bk", "L1_xattn_Wv",
        "L1_xattn_bv", "L1_xattn_Wo", "L1_xattn_bo", "L1_ffn_gate_w", "L1_ffn_gate_up_w", "L1_ffn_down_w"]


def kernel(**inputs):
    import numpy as _np
    import concourse.bacc as _bacc
    from concourse import mybir as _mybir
    from concourse.bass_utils import run_bass_kernel_spmd as _run

    nc = _bacc.Bacc("TRN2", target_bir_lowering=False, num_devices=1)
    arrays, aps = {}, {}
    for name in _INS:
        a = _np.ascontiguousarray(inputs[name])
        if a.ndim == 0:
            a = a.reshape(1)
        arrays[f"in_{name}_dram"] = a
        aps[name] = nc.dram_tensor(f"in_{name}_dram", a.shape, _mybir.dt.from_np(a.dtype), kind="ExternalInput").ap()
    out = nc.dram_tensor("out_0_dram", (NB, SEQ, D), F32, kind="ExternalOutput").ap()
    two_layer_kernel(nc, aps, out)
    r = _run(nc, [arrays], core_ids=[0])
    return r.results[0]["out_0_dram"]
```
